# Optimizing a Trainium2 kernel written in Bass

```python
import numpy as np
import jax
import jax.numpy as jnp

def _softmax(x, axis=-1):
    return jax.nn.softmax(x, axis=axis)

def _gelu(x):
    return jax.nn.gelu(x, approximate=True)

def _silu(x):
    return jax.nn.silu(x)

def _sigmoid(x):
    return jax.nn.sigmoid(x)

def _layernorm(x, axis=-1, eps=1e-05):
    m = jnp.mean(x, axis=axis, keepdims=True)
    v = jnp.var(x, axis=axis, keepdims=True)
    return (x - m) / jnp.sqrt(v + eps)

def _scatter_add(tgt, idx, src, axis=0):
    return tgt.at[idx].add(src)

def _segment_sum(src, seg, n):
    return jax.ops.segment_sum(src, seg, n)
kernel_name = 'mk_gps_d2_gnn_r8_5429af'

def setup_inputs(seed: int=0):
    np.random.seed(seed)
    _w = jnp.asarray

    def _rec_inputs():
        import jax
        import jax.numpy as jnp
        _gk = jax.random.key(seed)
        x = -0.0003713 + 1 * jax.random.normal(jax.random.fold_in(_gk, 1), (6250, 256), jnp.float32)
        src = jax.random.randint(jax.random.fold_in(_gk, 2), (200000,), 0, 6250, jnp.int32)
        dst = jax.random.randint(jax.random.fold_in(_gk, 3), (200000,), 0, 6250, jnp.int32)
        _o = jnp.argsort(dst, stable=True)
        src = src[_o]
        dst = dst[_o]
        edge_weight = jax.random.uniform(jax.random.fold_in(_gk, 12), (200000,), jnp.float32, 0.0, 0.999998)
        return (x, src, dst, edge_weight)
    x, src, dst, edge_weight = _rec_inputs()

    def _L0_gnn_setup():
        import jax, jax.numpy as jnp
        import numpy as np
        N_NODES = 6250
        key = jax.random.key(seed)
        k1, k2, k3 = jax.random.split(key, 3)
        x = jax.random.normal(k1, (N_NODES, 256), dtype=jnp.float32)
        W = jax.random.normal(k2, (256, 256), dtype=jnp.float32) * (1.0 / np.sqrt(256))
        edge_index = jax.random.randint(k3, (2, 200000), 0, N_NODES, dtype=jnp.int64)
        return {'x': x, 'W': W, 'edge_index': edge_index}
    _L0_gnn_all = _L0_gnn_setup()
    _L0_gnn_in = {k: v for k, v in _L0_gnn_all.items() if k in ('W',)}
    del _L0_gnn_all

    def _L0_mix_setup():
        import jax, jax.numpy as jnp
        import numpy as np
        NUM_HEADS = 8
        key = jax.random.key(seed)
        ks = jax.random.split(key, 5)
        B, N, C = (8, 2048, 256)
        x = jax.random.normal(ks[0], (B, N, C), dtype=jnp.float32)
        Wq = jax.random.normal(ks[1], (C, C), dtype=jnp.float32) * 0.02
        Wkv = jax.random.normal(ks[2], (2 * C, C), dtype=jnp.float32) * 0.02
        Wproj = jax.random.normal(ks[3], (C, C), dtype=jnp.float32) * 0.02
        bproj = jnp.zeros((C,), dtype=jnp.float32)
        return {'x': x, 'Wq': Wq, 'Wkv': Wkv, 'Wproj': Wproj, 'bproj': bproj}
    _L0_mix_all = _L0_mix_setup()
    _L0_mix_in = {k: v for k, v in _L0_mix_all.items() if k in ('Wq', 'Wkv', 'Wproj', 'bproj')}
    del _L0_mix_all

    def _L0_ffn_setup():
        import jax, jax.numpy as jnp
        import numpy as np
        DIM = 256
        H = 8
        D = 64
        G = 64
        INNER = H * D
        SCALE = D ** (-0.5)
        key = jax.random.key(seed)
        ks = jax.random.split(key, 12)
        B, N = (4, 2048)
        x = jax.random.normal(ks[0], (B, N, DIM), dtype=jnp.float32)
        s = lambda fan_in: 1.0 / np.sqrt(fan_in)
        W_fx = jax.random.normal(ks[1], (DIM, INNER), dtype=jnp.float32) * s(DIM)
        b_fx = jnp.zeros((INNER,), dtype=jnp.float32)
        W_x = jax.random.normal(ks[2], (DIM, INNER), dtype=jnp.float32) * s(DIM)
        b_x = jnp.zeros((INNER,), dtype=jnp.float32)
        A = jax.random.normal(ks[3], (G, D), dtype=jnp.float32)
        Q, _ = jnp.linalg.qr(A.T)
        W_slice = Q[:, :G].astype(jnp.float32)
        b_slice = jnp.zeros((G,), dtype=jnp.float32)
        W_q = jax.random.normal(ks[4], (D, D), dtype=jnp.float32) * s(D)
        W_k = jax.random.normal(ks[5], (D, D), dtype=jnp.float32) * s(D)
        W_v = jax.random.normal(ks[6], (D, D), dtype=jnp.float32) * s(D)
        W_out = jax.random.normal(ks[7], (INNER, DIM), dtype=jnp.float32) * s(INNER)
        b_out = jnp.zeros((DIM,), dtype=jnp.float32)
        temperature = jnp.ones((1, H, 1, 1), dtype=jnp.float32) * 0.5
        return {'x': x, 'W_fx': W_fx, 'b_fx': b_fx, 'W_x': W_x, 'b_x': b_x, 'W_slice': W_slice, 'b_slice': b_slice, 'W_q': W_q, 'W_k': W_k, 'W_v': W_v, 'W_out': W_out, 'b_out': b_out, 'temperature': temperature}
    _L0_ffn_all = _L0_ffn_setup()
    _L0_ffn_in = {k: v for k, v in _L0_ffn_all.items() if k in ('W_fx', 'b_fx', 'W_x', 'b_x', 'W_slice', 'b_slice', 'W_q', 'W_k', 'W_v', 'W_out', 'b_out', 'temperature')}
    del _L0_ffn_all

    def _L1_gnn_setup():
        import jax, jax.numpy as jnp
        import numpy as np
        EPS = 1e-05

        def _bn(x, gamma, beta):
            m = jnp.mean(x, axis=0)
            v = jnp.mean((x - m) ** 2, axis=0)
            return gamma * (x - m) * jax.lax.rsqrt(v + EPS) + beta

        def _hconv(x, src, dst, ew, w1, b1, w2, b2, g, b):
            h = jax.nn.relu(x @ w1 + b1)
            msg = ew[:, None] * h[src]
            agg = jax.ops.segment_sum(msg, dst, num_segments=x.shape[0])
            h = agg @ w2 + b2
            return jax.nn.relu(_bn(h, g, b))
        N, C, E = (6250, 256, 37500)
        key = jax.random.key(seed)
        ks = jax.random.split(key, 16)
        s = 1.0 / np.sqrt(C)
        inp = {'x': jax.random.normal(ks[0], (N, C), dtype=jnp.float32), 'hyperedge_index': jax.random.randint(ks[1], (2, E), 0, N, dtype=jnp.int32), 'hyperedge_weight': jax.random.uniform(ks[2], (E,), dtype=jnp.float32), 'c1_w1': jax.random.normal(ks[3], (C, C), dtype=jnp.float32) * s, 'c1_b1': jnp.zeros((C,), jnp.float32), 'c1_w2': jax.random.normal(ks[4], (C, C), dtype=jnp.float32) * s, 'c1_b2': jnp.zeros((C,), jnp.float32), 'c1_g': jnp.ones((C,), jnp.float32), 'c1_b': jnp.zeros((C,), jnp.float32), 'bn1_g': jnp.ones((C,), jnp.float32), 'bn1_b': jnp.zeros((C,), jnp.float32), 'c2_w1': jax.random.normal(ks[5], (C, C), dtype=jnp.float32) * s, 'c2_b1': jnp.zeros((C,), jnp.float32), 'c2_w2': jax.random.normal(ks[6], (C, C), dtype=jnp.float32) * s, 'c2_b2': jnp.zeros((C,), jnp.float32), 'c2_g': jnp.ones((C,), jnp.float32), 'c2_b': jnp.zeros((C,), jnp.float32), 'bn2_g': jnp.ones((C,), jnp.float32), 'bn2_b': jnp.zeros((C,), jnp.float32)}
        return inp
    _L1_gnn_all = _L1_gnn_setup()
    _L1_gnn_in = {k: v for k, v in _L1_gnn_all.items() if k in ('c1_w1', 'c1_b1', 'c1_w2', 'c1_b2', 'c1_g', 'c1_b', 'bn1_g', 'bn1_b', 'c2_w1', 'c2_b1', 'c2_w2', 'c2_b2', 'c2_g', 'c2_b', 'bn2_g', 'bn2_b')}
    del _L1_gnn_all

    def _L1_mix_setup():
        import jax, jax.numpy as jnp
        import numpy as np
        import math
        EMBED = 256
        HEADS = 4
        HEAD_DIM = EMBED // HEADS
        OUT_DIM = 256
        LN_EPS = 1e-05

        def _qkv_init(key):
            spread = math.sqrt(3.0 / EMBED)
            gain, delta = (0.01, 0.01)
            w = jax.random.uniform(key, (EMBED, EMBED), minval=-spread, maxval=spread) * gain
            return w + delta * jnp.eye(EMBED, dtype=w.dtype)

        def _layer_norm(x, g, b):
            mu = jnp.mean(x, axis=-1, keepdims=True)
            var = jnp.mean(jnp.square(x - mu), axis=-1, keepdims=True)
            return (x - mu) * jax.lax.rsqrt(var + LN_EPS) * g + b

        def _split_heads(x, B, S):
            return x.reshape(B, S, HEADS, HEAD_DIM).transpose(0, 2, 1, 3)
        key = jax.random.key(seed)
        ks = jax.random.split(key, 6)
        seq = jax.random.normal(ks[0], (4, 1024, EMBED), dtype=jnp.float32)
        wq = _qkv_init(ks[1])
        wk = _qkv_init(ks[2])
        wv = _qkv_init(ks[3])
        bound = 1.0 / math.sqrt(EMBED)
        wo = jax.random.uniform(ks[4], (OUT_DIM, EMBED), minval=-bound, maxval=bound)
        bo = jax.random.uniform(ks[5], (OUT_DIM,), minval=-bound, maxval=bound)
        ln_k_g = jnp.ones((HEAD_DIM,), jnp.float32)
        ln_k_b = jnp.zeros((HEAD_DIM,), jnp.float32)
        ln_v_g = jnp.ones((HEAD_DIM,), jnp.float32)
        ln_v_b = jnp.zeros((HEAD_DIM,), jnp.float32)
        return {'seq': seq, 'wq': wq, 'wk': wk, 'wv': wv, 'wo': wo, 'bo': bo, 'ln_k_g': ln_k_g, 'ln_k_b': ln_k_b, 'ln_v_g': ln_v_g, 'ln_v_b': ln_v_b}
    _L1_mix_all = _L1_mix_setup()
    _L1_mix_in = {k: v for k, v in _L1_mix_all.items() if k in ('wq', 'wk', 'wv', 'wo', 'bo', 'ln_k_g', 'ln_k_b', 'ln_v_g', 'ln_v_b')}
    del _L1_mix_all

    def _L1_ffn_setup():
        import jax, jax.numpy as jnp
        import numpy as np
        E = 8
        K = 2
        D = 256
        H = 512
        DOUT = 256
        EPS = 1e-05
        key = jax.random.key(seed)
        ks = jax.random.split(key, 9)
        s = 0.02
        return {'x': jax.random.normal(ks[0], (4, 1024, D), jnp.float32), 'gamma': 1.0 + 0.05 * jax.random.normal(ks[1], (D,), jnp.float32), 'beta': 0.05 * jax.random.normal(ks[2], (D,), jnp.float32), 'Wr': 0.01 * jax.random.normal(ks[3], (D, E), jnp.float32), 'br': jnp.zeros((E,), jnp.float32), 'W1': s * jax.random.normal(ks[4], (E, D, H), jnp.float32), 'b1': s * jax.random.normal(ks[5], (E, H), jnp.float32), 'W2': s * jax.random.normal(ks[6], (E, H, DOUT), jnp.float32), 'b2': s * jax.random.normal(ks[7], (E, DOUT), jnp.float32)}
    _L1_ffn_all = _L1_ffn_setup()
    _L1_ffn_in = {k: v for k, v in _L1_ffn_all.items() if k in ('gamma', 'beta', 'Wr', 'br', 'W1', 'b1', 'W2', 'b2')}
    del _L1_ffn_all
    return {'x': x, 'src': src, 'dst': dst, 'edge_weight': edge_weight, 'L0_gnn_W': _L0_gnn_in['W'], 'L0_mix_Wq': _L0_mix_in['Wq'], 'L0_mix_Wkv': _L0_mix_in['Wkv'], 'L0_mix_Wproj': _L0_mix_in['Wproj'], 'L0_mix_bproj': _L0_mix_in['bproj'], 'L0_ffn_W_fx': _L0_ffn_in['W_fx'], 'L0_ffn_b_fx': _L0_ffn_in['b_fx'], 'L0_ffn_W_x': _L0_ffn_in['W_x'], 'L0_ffn_b_x': _L0_ffn_in['b_x'], 'L0_ffn_W_slice': _L0_ffn_in['W_slice'], 'L0_ffn_b_slice': _L0_ffn_in['b_slice'], 'L0_ffn_W_q': _L0_ffn_in['W_q'], 'L0_ffn_W_k': _L0_ffn_in['W_k'], 'L0_ffn_W_v': _L0_ffn_in['W_v'], 'L0_ffn_W_out': _L0_ffn_in['W_out'], 'L0_ffn_b_out': _L0_ffn_in['b_out'], 'L0_ffn_temperature': _L0_ffn_in['temperature'], 'L1_gnn_c1_w1': _L1_gnn_in['c1_w1'], 'L1_gnn_c1_b1': _L1_gnn_in['c1_b1'], 'L1_gnn_c1_w2': _L1_gnn_in['c1_w2'], 'L1_gnn_c1_b2': _L1_gnn_in['c1_b2'], 'L1_gnn_c1_g': _L1_gnn_in['c1_g'], 'L1_gnn_c1_b': _L1_gnn_in['c1_b'], 'L1_gnn_bn1_g': _L1_gnn_in['bn1_g'], 'L1_gnn_bn1_b': _L1_gnn_in['bn1_b'], 'L1_gnn_c2_w1': _L1_gnn_in['c2_w1'], 'L1_gnn_c2_b1': _L1_gnn_in['c2_b1'], 'L1_gnn_c2_w2': _L1_gnn_in['c2_w2'], 'L1_gnn_c2_b2': _L1_gnn_in['c2_b2'], 'L1_gnn_c2_g': _L1_gnn_in['c2_g'], 'L1_gnn_c2_b': _L1_gnn_in['c2_b'], 'L1_gnn_bn2_g': _L1_gnn_in['bn2_g'], 'L1_gnn_bn2_b': _L1_gnn_in['bn2_b'], 'L1_mix_wq': _L1_mix_in['wq'], 'L1_mix_wk': _L1_mix_in['wk'], 'L1_mix_wv': _L1_mix_in['wv'], 'L1_mix_wo': _L1_mix_in['wo'], 'L1_mix_bo': _L1_mix_in['bo'], 'L1_mix_ln_k_g': _L1_mix_in['ln_k_g'], 'L1_mix_ln_k_b': _L1_mix_in['ln_k_b'], 'L1_mix_ln_v_g': _L1_mix_in['ln_v_g'], 'L1_mix_ln_v_b': _L1_mix_in['ln_v_b'], 'L1_ffn_gamma': _L1_ffn_in['gamma'], 'L1_ffn_beta': _L1_ffn_in['beta'], 'L1_ffn_Wr': _L1_ffn_in['Wr'], 'L1_ffn_br': _L1_ffn_in['br'], 'L1_ffn_W1': _L1_ffn_in['W1'], 'L1_ffn_b1': _L1_ffn_in['b1'], 'L1_ffn_W2': _L1_ffn_in['W2'], 'L1_ffn_b2': _L1_ffn_in['b2']}

def reference(x, src, dst, edge_weight, L0_gnn_W, L0_mix_Wq, L0_mix_Wkv, L0_mix_Wproj, L0_mix_bproj, L0_ffn_W_fx, L0_ffn_b_fx, L0_ffn_W_x, L0_ffn_b_x, L0_ffn_W_slice, L0_ffn_b_slice, L0_ffn_W_q, L0_ffn_W_k, L0_ffn_W_v, L0_ffn_W_out, L0_ffn_b_out, L0_ffn_temperature, L1_gnn_c1_w1, L1_gnn_c1_b1, L1_gnn_c1_w2, L1_gnn_c1_b2, L1_gnn_c1_g, L1_gnn_c1_b, L1_gnn_bn1_g, L1_gnn_bn1_b, L1_gnn_c2_w1, L1_gnn_c2_b1, L1_gnn_c2_w2, L1_gnn_c2_b2, L1_gnn_c2_g, L1_gnn_c2_b, L1_gnn_bn2_g, L1_gnn_bn2_b, L1_mix_wq, L1_mix_wk, L1_mix_wv, L1_mix_wo, L1_mix_bo, L1_mix_ln_k_g, L1_mix_ln_k_b, L1_mix_ln_v_g, L1_mix_ln_v_b, L1_ffn_gamma, L1_ffn_beta, L1_ffn_Wr, L1_ffn_br, L1_ffn_W1, L1_ffn_b1, L1_ffn_W2, L1_ffn_b2):
    import jax
    import jax.numpy as jnp

    def _L0_gnn_ref(x, W, edge_index):
        import jax, jax.numpy as jnp
        import numpy as np
        N_NODES = 6250
        N = x.shape[0]
        src, dst = (edge_index[0], edge_index[1])
        h = x @ W
        deg = jax.ops.segment_sum(jnp.ones_like(dst, dtype=h.dtype), dst, num_segments=N)
        deg_inv_sqrt = jnp.where(deg > 0, jax.lax.rsqrt(jnp.maximum(deg, 1)), 0.0)
        norm = deg_inv_sqrt[src] * deg_inv_sqrt[dst]
        msgs = h[src] * norm[:, None]
        out = jax.ops.segment_sum(msgs, dst, num_segments=N)
        return out

    def _L0_mix_ref(x, Wq, Wkv, Wproj, bproj):
        import jax, jax.numpy as jnp
        import numpy as np
        NUM_HEADS = 8
        B, N, C = x.shape
        h = NUM_HEADS
        d = C // h
        q = jnp.einsum('bnc,oc->bno', x, Wq).reshape(B, N, h, d).transpose(0, 2, 1, 3)
        kv = jnp.einsum('bnc,oc->bno', x, Wkv).reshape(B, N, 2, h, d)
        k = kv[:, :, 0].transpose(0, 2, 1, 3)
        v = kv[:, :, 1].transpose(0, 2, 1, 3)
        q = jax.nn.elu(q) + 1.0
        k = jax.nn.elu(k) + 1.0
        k_sum = k.sum(axis=2)
        D_inv = 1.0 / jnp.maximum(jnp.einsum('bhnd,bhd->bhn', q, k_sum), 1e-06)
        context = jnp.einsum('bhnd,bhne->bhde', k, v)
        attn = jnp.einsum('bhnd,bhde->bhne', q, context) * D_inv[..., None]
        out = attn.transpose(0, 2, 1, 3).reshape(B, N, C)
        out = jnp.einsum('bnc,oc->bno', out, Wproj) + bproj
        return out

    def _L0_ffn_ref(x, W_fx, b_fx, W_x, b_x, W_slice, b_slice, W_q, W_k, W_v, W_out, b_out, temperature):
        import jax, jax.numpy as jnp
        import numpy as np
        DIM = 256
        H = 8
        D = 64
        G = 64
        INNER = H * D
        SCALE = D ** (-0.5)
        B, N, _ = x.shape
        fx_mid = (x @ W_fx + b_fx).reshape(B, N, H, D).transpose(0, 2, 1, 3)
        x_mid = (x @ W_x + b_x).reshape(B, N, H, D).transpose(0, 2, 1, 3)
        temp = jnp.clip(temperature, 0.1, 5.0)
        slice_weights = jax.nn.softmax((x_mid @ W_slice + b_slice) / temp, axis=-1)
        slice_norm = slice_weights.sum(axis=2)
        slice_token = jnp.einsum('bhnc,bhng->bhgc', fx_mid, slice_weights)
        slice_token = slice_token / (slice_norm[..., None] + 1e-05)
        q = slice_token @ W_q
        k = slice_token @ W_k
        v = slice_token @ W_v
        attn = jax.nn.softmax(jnp.einsum('bhgc,bhkc->bhgk', q, k) * SCALE, axis=-1)
        out_slice = jnp.einsum('bhgk,bhkc->bhgc', attn, v)
        out_x = jnp.einsum('bhgc,bhng->bhnc', out_slice, slice_weights)
        out_x = out_x.transpose(0, 2, 1, 3).reshape(B, N, INNER)
        return out_x @ W_out + b_out

    def _L1_gnn_ref(x, hyperedge_index, hyperedge_weight, c1_w1, c1_b1, c1_w2, c1_b2, c1_g, c1_b, bn1_g, bn1_b, c2_w1, c2_b1, c2_w2, c2_b2, c2_g, c2_b, bn2_g, bn2_b):
        import jax, jax.numpy as jnp
        import numpy as np
        EPS = 1e-05

        def _bn(x, gamma, beta):
            m = jnp.mean(x, axis=0)
            v = jnp.mean((x - m) ** 2, axis=0)
            return gamma * (x - m) * jax.lax.rsqrt(v + EPS) + beta

        def _hconv(x, src, dst, ew, w1, b1, w2, b2, g, b):
            h = jax.nn.relu(x @ w1 + b1)
            msg = ew[:, None] * h[src]
            agg = jax.ops.segment_sum(msg, dst, num_segments=x.shape[0])
            h = agg @ w2 + b2
            return jax.nn.relu(_bn(h, g, b))
        src, dst = (hyperedge_index[0], hyperedge_index[1])
        residual = x
        h = _hconv(x, src, dst, hyperedge_weight, c1_w1, c1_b1, c1_w2, c1_b2, c1_g, c1_b)
        h = jax.nn.relu(_bn(h, bn1_g, bn1_b))
        h = _hconv(h, src, dst, hyperedge_weight, c2_w1, c2_b1, c2_w2, c2_b2, c2_g, c2_b)
        h = _bn(h, bn2_g, bn2_b)
        return jax.nn.relu(h + residual)

    def _L1_mix_ref(seq, wq, wk, wv, wo, bo, ln_k_g, ln_k_b, ln_v_g, ln_v_b):
        import jax, jax.numpy as jnp
        import numpy as np
        import math
        EMBED = 256
        HEADS = 4
        HEAD_DIM = EMBED // HEADS
        OUT_DIM = 256
        LN_EPS = 1e-05

        def _qkv_init(key):
            spread = math.sqrt(3.0 / EMBED)
            gain, delta = (0.01, 0.01)
            w = jax.random.uniform(key, (EMBED, EMBED), minval=-spread, maxval=spread) * gain
            return w + delta * jnp.eye(EMBED, dtype=w.dtype)

        def _layer_norm(x, g, b):
            mu = jnp.mean(x, axis=-1, keepdims=True)
            var = jnp.mean(jnp.square(x - mu), axis=-1, keepdims=True)
            return (x - mu) * jax.lax.rsqrt(var + LN_EPS) * g + b

        def _split_heads(x, B, S):
            return x.reshape(B, S, HEADS, HEAD_DIM).transpose(0, 2, 1, 3)
        B, S, _ = seq.shape
        q = _split_heads(seq @ wq.T, B, S)
        k = _split_heads(seq @ wk.T, B, S)
        v = _split_heads(seq @ wv.T, B, S)
        k = _layer_norm(k, ln_k_g, ln_k_b)
        v = _layer_norm(v, ln_v_g, ln_v_b)
        kv = jnp.einsum('bhsd,bhse->bhde', k, v) / S
        ga = jnp.einsum('bhsd,bhde->bhse', q, kv)
        ga = ga.transpose(0, 2, 1, 3).reshape(B, S, EMBED)
        return ga @ wo.T + bo

    def _L1_ffn_ref(x, gamma, beta, Wr, br, W1, b1, W2, b2):
        import jax, jax.numpy as jnp
        import numpy as np
        E = 8
        K = 2
        D = 256
        H = 512
        DOUT = 256
        EPS = 1e-05
        mu = jnp.mean(x, axis=-1, keepdims=True)
        var = jnp.mean(jnp.square(x - mu), axis=-1, keepdims=True)
        xn = (x - mu) * jax.lax.rsqrt(var + EPS) * gamma + beta
        logits = jnp.einsum('bsd,de->bse', xn, Wr) + br
        top_vals, top_idx = jax.lax.top_k(logits, K)
        w = jax.nn.softmax(top_vals, axis=-1)
        w_full = jnp.einsum('bsk,bske->bse', w, jax.nn.one_hot(top_idx, E, dtype=w.dtype))
        y = jnp.zeros(x.shape[:-1] + (DOUT,), x.dtype)
        for e in range(E):
            h = jax.nn.gelu(jnp.einsum('bsd,dh->bsh', xn, W1[e]) + b1[e], approximate=False)
            y_e = jnp.einsum('bsh,hd->bsd', h, W2[e]) + b2[e]
            y = y + y_e * w_full[..., e, None]
        return y
    edge_index = jnp.stack([src, dst])
    xn = _layernorm(x, axis=-1)
    x = x + _L0_gnn_ref(xn, L0_gnn_W, edge_index) + _L0_mix_ref(xn[None], L0_mix_Wq, L0_mix_Wkv, L0_mix_Wproj, L0_mix_bproj)[0]
    x = x + _L0_ffn_ref(_layernorm(x, axis=-1)[None], L0_ffn_W_fx, L0_ffn_b_fx, L0_ffn_W_x, L0_ffn_b_x, L0_ffn_W_slice, L0_ffn_b_slice, L0_ffn_W_q, L0_ffn_W_k, L0_ffn_W_v, L0_ffn_W_out, L0_ffn_b_out, L0_ffn_temperature)[0]
    xn = _layernorm(x, axis=-1)
    x = x + _L1_gnn_ref(xn, edge_index, edge_weight, L1_gnn_c1_w1, L1_gnn_c1_b1, L1_gnn_c1_w2, L1_gnn_c1_b2, L1_gnn_c1_g, L1_gnn_c1_b, L1_gnn_bn1_g, L1_gnn_bn1_b, L1_gnn_c2_w1, L1_gnn_c2_b1, L1_gnn_c2_w2, L1_gnn_c2_b2, L1_gnn_c2_g, L1_gnn_c2_b, L1_gnn_bn2_g, L1_gnn_bn2_b) + _L1_mix_ref(xn[None], L1_mix_wq, L1_mix_wk, L1_mix_wv, L1_mix_wo, L1_mix_bo, L1_mix_ln_k_g, L1_mix_ln_k_b, L1_mix_ln_v_g, L1_mix_ln_v_b)[0]
    x = x + _L1_ffn_ref(_layernorm(x, axis=-1)[None], L1_ffn_gamma, L1_ffn_beta, L1_ffn_Wr, L1_ffn_br, L1_ffn_W1, L1_ffn_b1, L1_ffn_W2, L1_ffn_b2)[0]
    return x

_drawn_inputs = setup_inputs


def setup_inputs(seed=0):
    import zlib

    import numpy as np

    out = dict(_drawn_inputs(seed))
    spreads = {'L0_mix_bproj': (0.0, 0.1),
     'L0_ffn_b_fx': (0.0, 0.1),
     'L0_ffn_b_x': (0.0, 0.8),
     'L0_ffn_b_slice': (0.0, 0.8),
     'L0_ffn_b_out': (0.0, 0.1),
     'L0_ffn_temperature': (0.5, 0.6),
     'L1_gnn_c1_b1': (0.0, 0.1),
     'L1_gnn_c1_b2': (0.0, 2.0),
     'L1_gnn_c1_g': (1.0, 0.6),
     'L1_gnn_c1_b': (0.0, 0.32),
     'L1_gnn_bn1_g': (1.0, 0.2),
     'L1_gnn_bn1_b': (0.0, 0.338),
     'L1_gnn_c2_b1': (0.0, 0.1),
     'L1_gnn_c2_b2': (0.0, 2.0),
     'L1_gnn_c2_g': (1.0, 0.6),
     'L1_gnn_c2_b': (0.0, 0.323),
     'L1_gnn_bn2_g': (1.0, 0.2),
     'L1_gnn_bn2_b': (0.0, 0.356),
     'L1_mix_ln_k_g': (1.0, 0.6),
     'L1_mix_ln_k_b': (0.0, 0.8),
     'L1_mix_ln_v_g': (1.0, 0.6),
     'L1_mix_ln_v_b': (0.0, 0.8),
     'L1_ffn_br': (0.0, 0.347)}
    factors = {'L0_mix_Wq': 8.0,
     'L0_mix_Wkv': 8.0,
     'L0_mix_Wproj': 8.0,
     'L0_ffn_W_x': 8.0,
     'L0_ffn_W_slice': 8.0,
     'L0_ffn_W_q': 8.0,
     'L0_ffn_W_k': 8.0,
     'L1_mix_wq': 8.0,
     'L1_mix_wk': 8.0,
     'L1_mix_wv': 8.0,
     'L1_mix_wo': 8.0,
     'L1_mix_bo': 2.717,
     'L1_ffn_gamma': 8.0,
     'L1_ffn_beta': 8.0,
     'L1_ffn_b1': 48.882,
     'L1_ffn_b2': 7.244}
    for name, (base, spread) in spreads.items():
        noise = np.random.default_rng([zlib.crc32(name.encode()), seed]).standard_normal(out[name].shape)
        drawn = base * np.exp(spread * noise) if base else spread * noise
        out[name] = jnp.asarray(drawn.astype(out[name].dtype))
    for name, factor in factors.items():
        out[name] = (out[name] * factor).astype(out[name].dtype)
    return out
```

```python
import concourse.bass as bass
from concourse import mybir
from contextlib import ExitStack, contextmanager

F32 = mybir.dt.float32
I32 = mybir.dt.int32
I16 = mybir.dt.int16
BF16 = mybir.dt.bfloat16
ALU = mybir.AluOpType
ACT = mybir.ActivationFunctionType
AX = mybir.AxisListType

P = 128
NODES = 6250
EDGES = 200000
C = 256
KC = C // P
TILES = -(-NODES // P)
LAST = NODES - (TILES - 1) * P
PADDED = TILES * P
SUB = 8
TRIPS = -(-EDGES // (P * SUB * 4))
GROUPS = 4 * TRIPS
WINDOW = 64
EPS = 1e-5
HEADS0, HD0 = 8, 32
SLICES, SH = 64, 8
HEADS1, HD1 = 4, 64
EXPERTS, HID = 8, 512
FT = HID // P


class Core:
    pass


def start_at_two(engine, *sems):
    for s in sems:
        engine.sem_inc(s, 2)


def ready(engine, sem, t):
    engine.wait_ge(sem, t + 3)


def free(engine, sem, t):
    engine.wait_ge(sem, t + 1)


def carry(engine, k):
    engine.sem_inc(k.carried, 1)


def pipelined(engine, head, tail):
    head(0, 0, 0)
    with engine.Fori(0, TILES // 2) as i:
        head(2 * i + 1, 1, i)
        tail(2 * i, 0, P)
        head(2 * i + 2, 0, i + 1)
        tail(2 * i + 1, 1, P)
    tail(TILES - 1, 0, LAST)


def pipelined_chunks(engine, count, head, tail):
    head(0, 0, 0)
    with engine.Fori(0, count // 2 - 1) as i:
        head(2 * i + 1, 1, i)
        tail(2 * i, 0, False)
        head(2 * i + 2, 0, i + 1)
        tail(2 * i + 1, 1, False)
    head(count - 1, 1, count // 2 - 1)
    tail(count - 2, 0, False)
    tail(count - 1, 1, True)


def no_head(t, u, i):
    pass


def no_tail(t, u, rows):
    pass


def table_rows(k, t):
    return k.table[t * P:(t + 1) * P, :] if isinstance(t, int) else k.table[bass.ds(t * P, P), :]


def col(buf, t):
    return buf[:, t:t + 1] if isinstance(t, int) else buf[:, bass.ds(t, 1)]


@contextmanager
def stage(nc):
    sems = []
    with ExitStack() as ctx:
        def sem(name):
            sems.append(ctx.enter_context(nc.semaphore(name)))
            return sems[-1]

        sb = lambda name, shape, dt=F32: ctx.enter_context(nc.sbuf_tensor(name, shape, dt))
        pb = lambda name, shape=(P, 512), dt=F32: ctx.enter_context(nc.psum_tensor(name, list(shape), dt))
        yield sb, pb, sem
        with nc.Block() as block:
            @block.gpsimd
            def _(pool):
                for s in sems:
                    pool.sem_clear(s)


def at(buf, t):
    if isinstance(t, int):
        return buf[:, t, :]
    return buf[:, bass.ds(t, 1), :].rearrange("p a n -> p (a n)")


def nodes(k, t, tiles=1):
    return k.sums_t[:, :, t * P:(t + tiles) * P] if isinstance(t, int) else k.sums_t[:, :, bass.ds(t * P, tiles * P)]


def setup_stage(nc, k):
    with stage(nc) as (sb, pb, sem):
        dst = sb("dst", [P, GROUPS * SUB], I32)
        dst_f = sb("dst_f", [P, GROUPS * SUB])
        part = sb("part", [P, 2, GROUPS * SUB], I32)
        low = sb("low", [P, GROUPS * SUB], BF16)
        high = sb("high", [P, GROUPS * SUB], BF16)
        count_b = sb("count_b", [P, P, 16], BF16)
        low_hot = [sb(f"low_hot{u}", [P, P, 16], BF16) for u in range(2)]
        high_hot = [sb(f"high_hot{u}", [P, TILES, 16], BF16) for u in range(2)]
        ends = sb("ends", [P, 2, GROUPS])
        ends_t = sb("ends_t", [GROUPS // 2, 2, 2])
        ends_i = sb("ends_i", [GROUPS // 2, 2, 2], I32)
        deg = sb("deg", [P, TILES])
        root = sb("root", [P, TILES])
        linked = sb("linked", [P, TILES])
        turned = pb("turned")
        deg_ps = pb("deg_ps")
        s_load, s_x, s_zero, s_const, s_iota = (sem(n) for n in ("dst_loaded", "x_loaded", "zeroed", "const_ready", "iota_ready"))
        s_f, s_part, s_lh, s_ends, s_turned, s_red, s_int, s_win = (sem(n) for n in (
            "dst_float", "parts_int", "parts_ready", "ends_ready", "ends_turned", "ends_reduced", "bounds_ready", "bounds_moved"))
        s_hot, s_free, s_deg, s_degs, s_r, s_half = (sem(n) for n in ("hot_ready", "hot_free", "deg_ready", "deg_copied", "root_ready", "half_ready"))
        with nc.Block() as block:
            @block.sync
            def _(sp):
                sp.dma_start(dst[:, :], k.ins["dst_cols"]).then_inc(s_load, 16)
                sp.dma_start(k.x[:, :, :], k.ins["x_in"].rearrange("(t p) c -> p t c", p=P)).then_inc(s_x, 16)
                sp.wait_ge(s_int, 2)
                sp.dma_start(k.win_dram, ends_i[:, :, :].rearrange("i j e -> i (j e)")).then_inc(s_win, 16)
                sp.wait_ge(s_win, 16)
                sp.dma_start(k.windows[0:1, :], k.win_dram.rearrange("(a i) e -> a (i e)", a=1)).then_inc(s_win, 16)
                sp.wait_ge(s_win, 32)
                sp.wait_ge(s_x, 16)

            @block.gpsimd
            def _(pool):
                nc.gpsimd.memset(k.ident[:, :], 0.0).then_inc(s_zero, 1)
                nc.gpsimd.memset(k.ones[:, :], 1.0).then_inc(s_const, 1)
                pool.wait_ge(s_zero, 1)
                nc.gpsimd.affine_select(out=k.ident[:, :], in_=k.ident[:, :], compare_op=ALU.not_equal, fill=1.0, base=0,
                                        pattern=[[-1, P]], channel_multiplier=1).then_inc(s_const, 1)
                nc.gpsimd.iota(count_b[:, :, :], pattern=[[1, P], [0, 16]], base=0, channel_multiplier=0,
                               allow_small_or_imprecise_dtypes=True).then_inc(s_iota, 1)
                nc.gpsimd.memset(k.zero_wide[:, :], 0.0)
                nc.gpsimd.memset(k.zero_b[:, :], 0.0).then_inc(s_const, 1)
                nc.gpsimd.memset(k.half[:, :], -0.5).then_inc(s_half, 1)
                pool.wait_ge(s_degs, 1)
                pool.wait_ge(s_half, 1)
                nc.gpsimd.tensor_tensor(root[:, :], deg[:, :], k.half[:,0:1].to_broadcast([P,TILES]), ALU.pow).then_inc(s_r, 1)

            @block.vector
            def _(dve):
                dve.wait_ge(s_load, 16)
                nc.vector.tensor_copy(dst_f[:, :], dst[:, :]).then_inc(s_f, 1)
                nc.vector.tensor_scalar(part[:, 0, :], dst[:, :], P - 1, None, ALU.bitwise_and).then_inc(s_part, 1)
                nc.vector.tensor_scalar(part[:, 1, :], dst[:, :], 7, None, ALU.arith_shift_right).then_inc(s_part, 1)
                dve.wait_ge(s_f, 1)
                by_group = dst_f[:, :].rearrange("p (g k) -> p g k", k=SUB)
                nc.vector.tensor_reduce(ends[:, 0, :], by_group, AX.X, ALU.min).then_inc(s_ends, 1)
                nc.vector.tensor_reduce(ends[:, 1, :], by_group, AX.X, ALU.max).then_inc(s_ends, 1)
                dve.wait_ge(s_part, 2)
                nc.vector.tensor_copy(low[:, :], part[:, 0, :]).then_inc(s_lh, 1)
                nc.vector.tensor_copy(high[:, :], part[:, 1, :]).then_inc(s_lh, 1)
                dve.wait_ge(s_turned, 1)
                ends_ps = turned[0:GROUPS // 2, :].rearrange("i (e j p) -> i e j p", e=2, j=2)
                nc.vector.tensor_reduce(ends_t[:, :, 0], ends_ps[:, 0], AX.X, ALU.min).then_inc(s_red, 1)
                nc.vector.tensor_reduce(ends_t[:, :, 1], ends_ps[:, 1], AX.X, ALU.max).then_inc(s_red, 1)
                dve.wait_ge(s_red, 2)
                nc.vector.tensor_copy(ends_i[:, :, 0], ends_t[:, :, 0]).then_inc(s_int, 1)
                nc.vector.tensor_scalar(ends_i[:, :, 1], ends_t[:, :, 1], 1.0, None, ALU.add).then_inc(s_int, 1)
                dve.wait_ge(s_lh, 2)
                dve.wait_ge(s_iota, 1)
                with dve.Fori(0, TRIPS) as i:
                    for u in range(2):
                        cols = bass.ds(32 * i + 16 * u, 16)
                        dve.wait_ge(s_free, 2 * i + u + 1)
                        nc.vector.tensor_tensor(low_hot[u][:, :, :], count_b[:, :, :],
                                                low[:, cols].unsqueeze(1).to_broadcast([P, P, 16]), ALU.is_equal)
                        nc.vector.tensor_tensor(high_hot[u][:, :, :], count_b[:, 0:TILES, :],
                                                high[:, cols].unsqueeze(1).to_broadcast([P, TILES, 16]),
                                                ALU.is_equal).then_inc(s_hot, 1)
                dve.wait_ge(s_deg, 1)
                nc.vector.tensor_scalar(deg[:, :], deg_ps[:, 0:TILES], 1.0, None, ALU.max).then_inc(s_degs, 1)
                nc.vector.tensor_scalar(linked[:, :], deg_ps[:, 0:TILES], 0.0, None, ALU.is_gt).then_inc(s_r, 1)
                dve.wait_ge(s_r, 2)
                nc.vector.tensor_tensor(k.norm[:, :], root[:, :], linked[:, :], ALU.mult).then_inc(s_r, 1)

            @block.tensor
            def _(pe):
                pe.sem_inc(s_free, 2)
                pe.wait_ge(s_const, 3)
                pe.wait_ge(s_ends, 2)
                for e in range(2):
                    for j in range(2):
                        last = nc.tensor.transpose(turned[0:GROUPS // 2, P * (2 * e + j):P * (2 * e + j + 1)],
                                                   ends[:, e, j::2], k.ident[:, :])
                last.then_inc(s_turned, 1)
                nc.tensor.matmul(deg_ps[:, 0:TILES], k.zero_b[:, :], k.zero_b[:, 0:TILES], start=True, stop=False, skip_group_check=True)
                with pe.Fori(0, TRIPS) as i:
                    for u in range(2):
                        pe.wait_ge(s_hot, 2 * i + u + 1)
                        for m in range(16):
                            last = nc.tensor.matmul(deg_ps[:, 0:TILES], low_hot[u][:, :, m], high_hot[u][:, :, m],
                                                    start=False, stop=False, skip_group_check=True)
                        last.then_inc(s_free, 1)
                nc.tensor.matmul(deg_ps[:, 0:TILES], k.zero_b[:, :], k.zero_b[:, 0:TILES], start=False, stop=True,
                                 skip_group_check=True).then_inc(s_deg, 1)


def edge_stage(nc, k, name, weighted, turn):
    gathered = turn * 256 * TRIPS
    with stage(nc) as (sb, pb, sem):
        edge = [sb(f"{name}_edge{b}", [P, 3, 16], I32) for b in range(2)]
        dest = [sb(f"{name}_dest{b}", [P, 16]) for b in range(2)]
        rows = sb(f"{name}_rows", [P, 2, SUB, C])
        hot = sb(f"{name}_hot", [P, 2, SUB, WINDOW])
        total = [pb(f"{name}_total{j}") for j in range(2)]
        s_edge = [sem(f"{name}_edges_loaded{b}") for b in range(2)]
        s_free = [sem(f"{name}_slots_free{j}") for j in range(2)]
        s_turn, s_dest, s_hot, s_total, s_added = (sem(f"{name}_{n}") for n in ("gather_turn", "dest_float", "hot_ready", "total_ready", "total_added"))
        with nc.Block() as block:
            @block.sync
            def _(sp):
                with sp.Fori(0, TRIPS) as i:
                    for b in range(2):
                        for j in range(2):
                            sp.wait_ge(s_free[j], 2 * i + b + 1)
                        sp.dma_start(edge[b][:, :, :],
                                     k.ins["edges"][bass.ds(2 * i + b, 1), :, :, :].rearrange("a p f m -> (a p) f m")).then_inc(s_edge[b], 16)

            @block.gpsimd
            def _(pool):
                with pool.Fori(0, TRIPS) as i:
                    for b in range(2):
                        pool.wait_ge(s_edge[b], 16 * i + 16)
                        for j in range(2):
                            pool.wait_ge(s_free[j], 2 * i + b + 2)
                            pool.sem_inc(s_turn, 1)
                            for m in range(SUB):
                                nc.gpsimd.indirect_dma_start(
                                    out=rows[:, j, m, :], out_offset=None, in_=k.table,
                                    in_offset=bass.IndirectOffsetOnAxis(ap=edge[b][:, 0, SUB * j + m:SUB * j + m + 1], axis=0),
                                ).then_inc(k.s_rows[j], 16)

            @block.vector
            def _(dve):
                dve.sem_inc(s_total, 1)
                nc.vector.memset(total[1][:, 0:KC * WINDOW], 0.0)
                nc.vector.memset(k.sums_t[:, :, :], 0.0).then_inc(s_added, 1)
                visit = dve.alloc_register(f"{name}_dve_visit")
                before = dve.alloc_register(f"{name}_dve_before")
                dve.reg_mov(visit, 1)
                dve.reg_mov(before, 0)

                def build(b, j, w):
                    for m in range(SUB):
                        at_m = slice(SUB * j + m, SUB * j + m + 1)
                        weight = edge[b][:, 2, at_m].bitcast(F32) if weighted else 1.0
                        last = nc.vector.tensor_scalar(hot[:, j, m, :], k.node_id[:, bass.ds(w, WINDOW)], dest[b][:, at_m], weight,
                                                       ALU.is_equal, ALU.mult)
                    last.then_inc(s_hot, 1)

                def add(j, v):
                    window = dve.snap(before, min_val=0, max_val=PADDED - 1)
                    dve.wait_ge(s_total, v)
                    dve.wait_ge(s_added, v)
                    out = k.sums_t[:, :, bass.ds(window, WINDOW)]
                    nc.vector.tensor_tensor(out, out, total[j][:, 0:KC * WINDOW].rearrange("p (a n) -> p a n", a=KC), ALU.add).then_inc(s_added, 1)

                with dve.Fori(0, TRIPS) as i:
                    for b in range(2):
                        dve.wait_ge(s_edge[b], 16 * i + 16)
                        nc.vector.tensor_copy(dest[b][:, :], edge[b][:, 1, :]).then_inc(s_dest, 1)
                        for j in range(2):
                            first = dve.value_load(k.windows[0:1, bass.ds(8 * i + 4 * b + 2 * j, 1)], min_val=0, max_val=PADDED - 1)
                            end = dve.value_load(k.windows[0:1, bass.ds(8 * i + 4 * b + 2 * j + 1, 1)], min_val=1, max_val=PADDED)
                            v = dve.snap(visit, min_val=1, max_val=1 << 20)
                            if j == 0:
                                dve.wait_ge(s_dest, 2 * i + b + 1)
                            build(b, j, first)
                            add(1 - j, v)
                            dve.reg_mov(before, first)
                            dve.reg_add(visit, visit, 1)
                            with dve.If(end > first + WINDOW):
                                with dve.Fori(first + WINDOW, end, WINDOW) as w:
                                    v = dve.snap(visit, min_val=1, max_val=1 << 20)
                                    add(j, v)
                                    build(b, j, w)
                                    dve.reg_mov(before, w)
                                    dve.reg_add(visit, visit, 1)
                add(1, dve.snap(visit, min_val=1, max_val=1 << 20))

            @block.tensor
            def _(pe):
                for j in range(2):
                    pe.sem_inc(s_free[j], 2)
                visit = pe.alloc_register(f"{name}_pe_visit")
                pe.reg_mov(visit, 1)

                def multiply(j):
                    for a in range(KC):
                        for m in range(SUB):
                            last = nc.tensor.matmul(total[j][:, a * WINDOW:(a + 1) * WINDOW], rows[:, j, m, a * P:(a + 1) * P], hot[:, j, m, :],
                                                    start=(m == 0), stop=(m == SUB - 1))
                    last.then_inc(s_total, 1)

                with pe.Fori(0, TRIPS) as i:
                    for b in range(2):
                        for j in range(2):
                            first = pe.value_load(k.windows[0:1, bass.ds(8 * i + 4 * b + 2 * j, 1)], min_val=0, max_val=PADDED - 1)
                            end = pe.value_load(k.windows[0:1, bass.ds(8 * i + 4 * b + 2 * j + 1, 1)], min_val=1, max_val=PADDED)
                            v = pe.snap(visit, min_val=1, max_val=1 << 20)
                            pe.wait_ge(s_hot, v)
                            pe.wait_ge(k.s_rows[j], gathered + 256 * i + 128 * b + 128)
                            multiply(j)
                            pe.reg_add(visit, visit, 1)
                            with pe.If(end > first + WINDOW):
                                with pe.Fori(first + WINDOW, end, WINDOW) as w:
                                    v = pe.snap(visit, min_val=1, max_val=1 << 20)
                                    pe.wait_ge(s_hot, v)
                                    multiply(j)
                                    pe.reg_add(visit, visit, 1)
                            pe.wait_ge(s_total, pe.snap(visit, min_val=1, max_val=1 << 20))
                            pe.sem_inc(s_free[j], 1)


def residents(nc, k, ctx):
    sb = lambda name, shape, dt=F32: ctx.enter_context(nc.sbuf_tensor(name, shape, dt))
    k.carried = ctx.enter_context(nc.semaphore("carried_waits"))
    k.s_rows = [ctx.enter_context(nc.semaphore(f"rows_gathered{j}")) for j in range(2)]
    k.x = sb("x", [P, TILES, C])
    k.windows = sb("windows", [1, 2 * GROUPS], I32)
    k.norm = sb("norm", [P, TILES])
    k.ident = sb("ident", [P, P])
    k.ones = sb("ones", [P, P])
    k.half = sb("half", [P, 1])
    k.zero_b = sb("zero_b", [P, P], BF16)
    k.zero_wide = sb("zero_wide", [P, 512], BF16)
    k.raw = sb("raw", [P, TILES, 6])
    k.mean = sb("mean", [P, TILES])
    k.moment = sb("moment", [P, 2, TILES])
    k.rstd = sb("rstd", [P, TILES])
    k.key_sum = sb("key_sum", [P, C])
    k.mix0 = sb("mix0", [P, KC, C])
    k.slices = sb("slices", [P, 4, C])
    k.bn_scale = sb("bn_scale", [P, KC])
    k.bn_shift = sb("bn_shift", [P, KC])
    k.gate = sb("gate", [P, TILES, EXPERTS])
    k.mix1 = sb("mix1", [P, KC, C])


def wide_residents(nc, k, ctx):
    wide = ctx.enter_context(nc.sbuf_tensor("wide", [P, TILES * 2 * C + KC * WINDOW], F32))
    n = KC * (PADDED + WINDOW)
    k.sums_t = wide[:, 0:n].rearrange("p (a n) -> p a n", a=KC)
    k.rows = wide[:, n:n + TILES * C].rearrange("p (t c) -> p t c", c=C)
    k.soft = wide[:, 0:TILES * 2 * C].rearrange("p (t c) -> p t c", c=2 * C)


def graph_residents(nc, k, ctx):
    k.node_id = ctx.enter_context(nc.sbuf_tensor("node_id", [P, PADDED + WINDOW], I16))


def row_stats(nc, k, t):
    return nc.vector.bn_stats(at(k.raw, t), at(k.x, t))


def row_moments(nc, dve, k, s_step):
    done = [0]

    def step(instruction):
        instruction.then_inc(s_step, 1)
        done[0] += 1
        dve.wait_ge(s_step, done[0])

    step(nc.vector.tensor_tensor(k.moment[:, 0, :], k.raw[:, :, 1], k.raw[:, :, 4], ALU.add))
    step(nc.vector.tensor_scalar(k.mean[:, :], k.moment[:, 0, :], 0.5, None, ALU.mult))
    step(nc.vector.tensor_tensor(k.moment[:, 0, :], k.raw[:, :, 1], k.mean[:, :], ALU.subtract))
    step(nc.vector.tensor_tensor(k.moment[:, 0, :], k.moment[:, 0, :], k.moment[:, 0, :], ALU.mult))
    step(nc.vector.tensor_tensor(k.moment[:, 1, :], k.raw[:, :, 2], k.raw[:, :, 5], ALU.add))
    step(nc.vector.scalar_tensor_tensor(k.moment[:, 1, :], k.moment[:, 1, :], 1.0 / C, k.moment[:, 0, :], ALU.mult, ALU.add))
    step(nc.vector.tensor_scalar(k.moment[:, 0, :], k.moment[:, 1, :], EPS, None, ALU.add))


MOMENTS = 7


def row_scale(nc, pool, k, s_step, s_rstd):
    pool.wait_ge(s_step, MOMENTS)
    nc.gpsimd.tensor_tensor(k.rstd[:, :], k.moment[:, 0, :], k.half[:, 0:1].to_broadcast([P, TILES]), ALU.pow).then_inc(s_rstd, 1)


def normalise(nc, k, out, t):
    return nc.vector.tensor_scalar(out, at(k.x, t), col(k.mean, t), col(k.rstd, t), ALU.subtract, ALU.mult)


def first_stats_stage(nc, k):
    with stage(nc) as (sb, pb, sem):
        s_stats, s_step, s_rstd = (sem(f"in_{n}") for n in ("stats", "moment_steps", "rstd"))
        with nc.Block() as block:
            @block.vector
            def _(dve):
                with dve.Fori(0, TILES) as t:
                    row_stats(nc, k, t).then_inc(s_stats, 1)
                dve.wait_ge(s_stats, TILES)
                row_moments(nc, dve, k, s_step)

            @block.gpsimd
            def _(pool):
                nc.gpsimd.iota(k.node_id[:, :], pattern=[[1, PADDED + WINDOW]], base=0, channel_multiplier=0,
                               allow_small_or_imprecise_dtypes=True)
                row_scale(nc, pool, k, s_step, s_rstd)


def keys_stage(nc, k):
    with stage(nc) as (sb, pb, sem):
        w = sb("ky_w", [P, KC, 2 * C])
        w_proj = sb("ky_wproj", [P, KC, C])
        xn = [sb(f"ky_xn{u}", [P, C]) for u in range(2)]
        xt = [sb(f"ky_xt{u}", [P, KC, P]) for u in range(2)]
        row = [sb(f"ky_row{u}", [P, C]) for u in range(2)]
        neg = [sb(f"ky_neg{u}", [P, C]) for u in range(2)]
        exp = [sb(f"ky_exp{u}", [P, C]) for u in range(2)]
        key = [sb(f"ky_key{u}", [P, C]) for u in range(2)]
        val = [sb(f"ky_val{u}", [P, C]) for u in range(2)]
        blocks = sb("ky_blocks", [P, P])
        ctx_t = sb("ky_ctx_t", [P, KC, P])
        turned = [pb(f"ky_turned{u}") for u in range(2)]
        kv = [pb(f"ky_kv{u}") for u in range(2)]
        context = pb("ky_context")
        keysum = pb("ky_keysum")
        proj = pb("ky_proj")
        s_stored = [sem(f"ky_table_stored{u}") for u in range(2)]
        s_w, s_done, s_ctx, s_m = (sem(f"ky_{n}") for n in ("weights_loaded", "context_ready", "context_masked", "mix_ready"))
        s_xn, s_kept, s_turned, s_xt, s_row, s_kv, s_neg, s_exp, s_val, s_key, s_sum = (sem(f"ky_{n}") for n in (
            "rows_ready", "rows_kept", "rows_turned", "turned_copied", "table_row", "kv_ready", "negative_ready",
            "exp_ready", "value_copied", "key_ready", "context_added"))
        with nc.Block() as block:
            @block.sync
            def _(sp):
                sp.dma_start(w[:, :, :], k.ins["L0_mix_WkvT"].rearrange("(k p) n -> p k n", p=P)).then_inc(s_w, 16)
                sp.dma_start(w_proj[:, :, :], k.ins["L0_mix_WprojT"].rearrange("(k p) n -> p k n", p=P)).then_inc(s_w, 16)
                sp.dma_start(blocks[:, :], k.ins["blocks32"]).then_inc(s_w, 16)
                for u in range(2):
                    sp.sem_inc(s_stored[u], 16)

                def head(t, u, i):
                    ready(sp, s_row, t)
                    sp.dma_start(table_rows(k, t), row[u][:, :]).then_inc(s_stored[u], 16)

                pipelined(sp, head, no_tail)
                sp.wait_ge(s_stored[0], 16 + 16 * (TILES // 2 + 1))
                sp.wait_ge(s_stored[1], 16 + 16 * (TILES // 2))

            @block.gpsimd
            def _(pool):
                start_at_two(pool, s_kept)

                def head(t, u, i):
                    ready(pool, s_xn, t)
                    nc.gpsimd.tensor_copy(at(k.rows, t), xn[u][:, :]).then_inc(s_kept, 1)

                pipelined(pool, head, no_tail)

            @block.vector
            def _(dve):
                start_at_two(dve, s_xn, s_neg, s_key)

                def head(t, u, i):
                    free(dve, s_turned, t)
                    free(dve, s_row, t)
                    free(dve, s_kept, t)
                    normalise(nc, k, xn[u][:, :], t).then_inc(s_xn, 1)

                def tail(t, u, rows):
                    ready(dve, s_kv, t)
                    free(dve, s_exp, t)
                    nc.vector.tensor_scalar(neg[u][:, :], kv[u][:, 0:C], 0.0, None, ALU.min).then_inc(s_neg, 1)
                    ready(dve, s_exp, t)
                    ready(dve, s_val, t)
                    free(dve, s_sum, t)
                    nc.vector.scalar_tensor_tensor(key[u][:, :], kv[u][:, 0:C], 0.0, exp[u][:, :], ALU.max, ALU.add).then_inc(s_key, 1)

                pipelined(dve, head, tail)
                dve.wait_ge(s_done, 1)
                dve.wait_ge(s_w, 48)
                for a in range(KC):
                    nc.vector.tensor_tensor(ctx_t[:, a, :], context[:, a * P:(a + 1) * P], blocks[:, :], ALU.mult).then_inc(s_ctx, 1)
                nc.vector.tensor_copy(k.key_sum[:, :], keysum[:, 0:C])
                dve.wait_ge(s_m, 1)
                nc.vector.tensor_copy(k.mix0[:, :, :].rearrange("p k n -> p (k n)"), proj[:, :])

            @block.scalar
            def _(act):
                start_at_two(act, s_xt, s_row, s_exp, s_val)

                def head(t, u, i):
                    ready(act, s_xn, t)
                    act.wait_ge(s_stored[u], 16 * i + 16)
                    nc.scalar.activation(row[u][:, :], xn[u][:, :], ACT.Copy, scale=col(k.norm, t)).then_inc(s_row, 1)
                    ready(act, s_turned, t)
                    free(act, s_kv, t)
                    nc.scalar.activation(xt[u][:, :, :].rearrange("p k n -> p (k n)"), turned[u][:, 0:C], ACT.Copy).then_inc(s_xt, 1)

                def tail(t, u, rows):
                    ready(act, s_neg, t)
                    free(act, s_sum, t)
                    nc.scalar.activation(val[u][:, :], kv[u][:, C:2 * C], ACT.Copy).then_inc(s_val, 1)
                    free(act, s_key, t)
                    nc.scalar.activation(exp[u][:, :], neg[u][:, :], ACT.Exp).then_inc(s_exp, 1)

                pipelined(act, head, tail)

            @block.tensor
            def _(pe):
                start_at_two(pe, s_turned, s_kv, s_sum)
                for bank in (context, keysum):
                    nc.tensor.matmul(bank[:, 0:C], k.zero_b[:, :], k.zero_wide[:, 0:C], start=True, stop=False, skip_group_check=True)
                pe.wait_ge(s_w, 48)

                def head(t, u, i):
                    ready(pe, s_xn, t)
                    free(pe, s_xt, t)
                    for a in range(KC):
                        last = nc.tensor.transpose(turned[u][:, a * P:(a + 1) * P], xn[u][:, a * P:(a + 1) * P], k.ident[:, :])
                    last.then_inc(s_turned, 1)
                    ready(pe, s_xt, t)
                    free(pe, s_key, t)
                    free(pe, s_val, t)
                    for a in range(KC):
                        last = nc.tensor.matmul(kv[u][:, :], xt[u][:, a, :], w[:, a, :], start=(a == 0), stop=(a == KC - 1))
                    last.then_inc(s_kv, 1)

                def tail(t, u, rows):
                    ready(pe, s_key, t)
                    ready(pe, s_val, t)
                    stop = rows == LAST
                    nc.tensor.matmul(keysum[:, 0:C], k.ones[0:rows, :], key[u][0:rows, :], start=False, stop=stop, skip_group_check=True)
                    for a in range(KC):
                        half = slice(a * P, (a + 1) * P)
                        last = nc.tensor.matmul(context[:, half], val[u][0:rows, half], key[u][0:rows, half], start=False, stop=stop,
                                                skip_group_check=True)
                    last.then_inc(s_sum, 1)

                pipelined(pe, head, tail)
                ready(pe, s_sum, TILES - 1)
                pe.sem_inc(s_done, 1)
                pe.wait_ge(s_ctx, KC)
                for a in range(KC):
                    last = nc.tensor.matmul(proj[:, a * C:(a + 1) * C], ctx_t[:, a, :], w_proj[:, a, :], start=True, stop=True)
                last.then_inc(s_m, 1)


def first_update_stage(nc, k):
    with stage(nc) as (sb, pb, sem):
        wq = sb("fu_wq", [P, KC, C])
        wg = sb("fu_wg", [P, KC, C])
        bias = sb("fu_bias", [P, C])
        rows_in = [sb(f"fu_rows{u}", [P, C]) for u in range(2)]
        rows_t = [sb(f"fu_rows_t{u}", [P, KC, P]) for u in range(2)]
        agg_t = [sb(f"fu_sums_t{u}", [P, KC, P]) for u in range(2)]
        neg = [sb(f"fu_neg{u}", [P, C]) for u in range(2)]
        exp = [sb(f"fu_exp{u}", [P, C]) for u in range(2)]
        phi = [sb(f"fu_phi{u}", [P, C]) for u in range(2)]
        prod = [sb(f"fu_prod{u}", [P, C]) for u in range(2)]
        den = [sb(f"fu_den{u}", [P, 3, HEADS0]) for u in range(2)]
        qn = [sb(f"fu_qn{u}", [P, C]) for u in range(2)]
        qn_t = [sb(f"fu_qn_t{u}", [P, KC, P]) for u in range(2)]
        attended = [sb(f"fu_attended{u}", [P, C]) for u in range(2)]
        turned = [pb(f"fu_turned{u}") for u in range(2)]
        query = [pb(f"fu_query{u}") for u in range(2)]
        q_turned = [pb(f"fu_q_turned{u}") for u in range(2)]
        out = [pb(f"fu_out{u}") for u in range(2)]
        s_w = sem("fu_weights_loaded")
        s_turned, s_rows_t, s_agg, s_q, s_neg, s_exp, s_phi, s_prod, s_sum, s_max, s_den, s_qn, s_qt, s_qnt, s_out, s_add, s_x, s_stats = (
            sem(f"fu_{n}") for n in ("rows_turned", "turned_copied", "sums_copied", "query_ready", "negative_ready", "exp_ready", "phi_ready",
                                     "product_ready", "denominator_summed", "denominator_guarded", "denominator_inverted", "query_scaled",
                                     "query_turned", "query_copied", "out_ready", "out_added", "x_updated", "stats_ready"))
        s_step, s_rstd, s_rows, s_att = (sem(f"fu_{n}") for n in ("moment_steps", "rstd", "rows_copied", "attention_biased"))
        with nc.Block() as block:
            @block.sync
            def _(sp):
                sp.dma_start(wq[:, :, :], k.ins["L0_mix_WqT"].rearrange("(k p) n -> p k n", p=P)).then_inc(s_w, 16)
                sp.dma_start(wg[:, :, :], k.ins["L0_gnn_W"].rearrange("(k p) n -> p k n", p=P)).then_inc(s_w, 16)
                sp.dma_start(bias[:, :], k.ins["L0_mix_bproj"].partition_broadcast(P)).then_inc(s_w, 16)

            @block.gpsimd
            def _(pool):
                start_at_two(pool, s_rows)

                def head(t, u, i):
                    free(pool, s_turned, t)
                    nc.gpsimd.tensor_copy(rows_in[u][:, :], at(k.rows, t)).then_inc(s_rows, 1)

                pipelined(pool, head, no_tail)
                row_scale(nc, pool, k, s_step, s_rstd)

            @block.vector
            def _(dve):
                start_at_two(dve, s_neg, s_phi, s_prod, s_sum, s_max, s_den, s_qn, s_att, s_add, s_x, s_stats)
                dve.wait_ge(s_w, 48)

                def head(t, u, i):
                    ready(dve, s_q, t)
                    free(dve, s_exp, t)
                    nc.vector.tensor_scalar(neg[u][:, :], query[u][:, 0:C], 0.0, None, ALU.min).then_inc(s_neg, 1)
                    ready(dve, s_exp, t)
                    free(dve, s_qn, t)
                    nc.vector.scalar_tensor_tensor(phi[u][:, :], query[u][:, 0:C], 0.0, exp[u][:, :], ALU.max, ALU.add).then_inc(s_phi, 1)
                    ready(dve, s_phi, t)
                    nc.vector.tensor_tensor(prod[u][:, :], phi[u][:, :], k.key_sum[:, :], ALU.mult).then_inc(s_prod, 1)
                    ready(dve, s_prod, t)
                    nc.vector.tensor_reduce(den[u][:, 0, :], prod[u][:, :].rearrange("p (h d) -> p h d", h=HEADS0), AX.X, ALU.add).then_inc(s_sum, 1)
                    ready(dve, s_sum, t)
                    nc.vector.tensor_scalar(den[u][:, 1, :], den[u][:, 0, :], 1e-6, None, ALU.max).then_inc(s_max, 1)
                    ready(dve, s_max, t)
                    nc.vector.reciprocal(den[u][:, 2, :], den[u][:, 1, :]).then_inc(s_den, 1)
                    ready(dve, s_den, t)
                    free(dve, s_qt, t)
                    nc.vector.tensor_tensor(qn[u][:, :].rearrange("p (h d) -> p h d", h=HEADS0),
                                            phi[u][:, :].rearrange("p (h d) -> p h d", h=HEADS0),
                                            den[u][:, 2, :].unsqueeze(2).to_broadcast([P, HEADS0, HD0]), ALU.mult).then_inc(s_qn, 1)

                def tail(t, u, rows):
                    ready(dve, s_out, t)
                    nc.vector.tensor_tensor(attended[u][:, :], out[u][:, 0:C], bias[:, :], ALU.add).then_inc(s_att, 1)
                    carry(dve, k)
                    nc.vector.scalar_tensor_tensor(at(k.x, t), out[u][:, C:2 * C], col(k.norm, t), at(k.x, t), ALU.mult, ALU.add).then_inc(s_add, 1)
                    ready(dve, s_att, t)
                    ready(dve, s_add, t)
                    nc.vector.tensor_tensor(at(k.x, t), at(k.x, t), attended[u][:, :], ALU.add).then_inc(s_x, 1)
                    ready(dve, s_x, t)
                    carry(dve, k)
                    row_stats(nc, k, t).then_inc(s_stats, 1)

                pipelined(dve, head, tail)
                ready(dve, s_stats, TILES - 1)
                row_moments(nc, dve, k, s_step)

            @block.scalar
            def _(act):
                start_at_two(act, s_agg, s_rows_t, s_exp, s_qnt)

                def head(t, u, i):
                    ready(act, s_turned, t)
                    free(act, s_q, t)
                    nc.scalar.activation(rows_t[u][:, :, :].rearrange("p k n -> p (k n)"), turned[u][:, 0:C], ACT.Copy).then_inc(s_rows_t, 1)
                    free(act, s_out, t)
                    nc.scalar.activation(agg_t[u][:, :, :], nodes(k, t), ACT.Copy).then_inc(s_agg, 1)
                    ready(act, s_neg, t)
                    nc.scalar.activation(exp[u][:, :], neg[u][:, :], ACT.Exp).then_inc(s_exp, 1)

                def tail(t, u, rows):
                    ready(act, s_qt, t)
                    free(act, s_out, t)
                    nc.scalar.activation(qn_t[u][:, :, :].rearrange("p k n -> p (k n)"), q_turned[u][:, 0:C], ACT.Copy).then_inc(s_qnt, 1)

                pipelined(act, head, tail)

            @block.tensor
            def _(pe):
                start_at_two(pe, s_turned, s_q, s_qt, s_out)
                pe.wait_ge(s_w, 48)

                def head(t, u, i):
                    ready(pe, s_rows, t)
                    free(pe, s_rows_t, t)
                    for a in range(KC):
                        last = nc.tensor.transpose(turned[u][:, a * P:(a + 1) * P], rows_in[u][:, a * P:(a + 1) * P], k.ident[:, :])
                    last.then_inc(s_turned, 1)
                    ready(pe, s_rows_t, t)
                    free(pe, s_phi, t)
                    for a in range(KC):
                        last = nc.tensor.matmul(query[u][:, 0:C], rows_t[u][:, a, :], wq[:, a, :], start=(a == 0), stop=(a == KC - 1))
                    last.then_inc(s_q, 1)

                def tail(t, u, rows):
                    ready(pe, s_qn, t)
                    free(pe, s_qnt, t)
                    for a in range(KC):
                        last = nc.tensor.transpose(q_turned[u][:, a * P:(a + 1) * P], qn[u][:, a * P:(a + 1) * P], k.ident[:, :])
                    last.then_inc(s_qt, 1)
                    free(pe, s_add, t)
                    ready(pe, s_agg, t)
                    for a in range(KC):
                        nc.tensor.matmul(out[u][:, C:2 * C], agg_t[u][:, a, :], wg[:, a, :], start=(a == 0), stop=(a == KC - 1))
                    ready(pe, s_qnt, t)
                    for a in range(KC):
                        last = nc.tensor.matmul(out[u][:, 0:C], qn_t[u][:, a, :], k.mix0[:, a, :], start=(a == 0), stop=(a == KC - 1))
                    last.then_inc(s_out, 1)

                pipelined(pe, head, tail)


def slice_weights_stage(nc, k):
    with stage(nc) as (sb, pb, sem):
        wx_t = sb("sl_wx_t", [P, 4, C])
        pair = sb("sl_pair", [P, P])
        bx = sb("sl_bx", [P, 4])
        bx_wide = sb("sl_bx_wide", [P, 4, P])
        b_slice = sb("sl_b", [P, 2 * C])
        temp = sb("sl_temp", [P, SH])
        clipped = sb("sl_clipped", [P, SH])
        inv = sb("sl_inv", [P, SH])
        summed = sb("sl_summed", [P, 2 * C])
        mats = [pb(f"sl_mat{a}") for a in range(KC)]
        row = pb("sl_row")
        s_w, s_clip, s_inv, s_wide, s_mat, s_b = (sem(f"sl_{n}") for n in ("loaded", "clipped", "inverted", "bias_wide", "products", "bias_summed"))
        with nc.Block() as block:
            @block.sync
            def _(sp):
                sp.dma_start(wx_t[:, :, :], k.ins["L0_ffn_W_xT"].rearrange("(q p) c -> p q c", p=P)).then_inc(s_w, 16)
                sp.dma_start(pair[:, :], k.ins["pair_slice"]).then_inc(s_w, 16)
                sp.dma_start(bx[:, :], k.ins["L0_ffn_b_x4"]).then_inc(s_w, 16)
                sp.dma_start(b_slice[:, :], k.ins["b_slice8"].partition_broadcast(P)).then_inc(s_w, 16)
                sp.dma_start(temp[:, :], k.ins["temperature"].partition_broadcast(P)).then_inc(s_w, 16)

            @block.vector
            def _(dve):
                dve.wait_ge(s_w, 80)
                nc.vector.tensor_scalar(clipped[:, :], temp[:, :], 0.1, 5.0, ALU.max, ALU.min).then_inc(s_clip, 1)
                for q in range(4):
                    last = nc.vector.tensor_scalar(bx_wide[:, q, :], k.ones[:, :], bx[:, q:q + 1], None, ALU.mult)
                last.then_inc(s_wide, 1)
                dve.wait_ge(s_clip, 1)
                nc.vector.reciprocal(inv[:, :], clipped[:, :]).then_inc(s_inv, 1)
                dve.wait_ge(s_mat, 1)
                dve.wait_ge(s_inv, 1)
                inv_wide = inv[:, :].unsqueeze(2).to_broadcast([P, SH, SLICES])
                for a in range(KC):
                    nc.vector.tensor_tensor(k.w_slice[:, a, :].rearrange("p (h g) -> p h g", h=SH),
                                            mats[a][:, :].rearrange("p (h g) -> p h g", h=SH), inv_wide, ALU.mult)
                nc.vector.tensor_tensor(summed[:, :], row[:, :], b_slice[:, :], ALU.add).then_inc(s_b, 1)
                dve.wait_ge(s_b, 1)
                nc.vector.tensor_tensor(k.b_slice[:, :].rearrange("p (h g) -> p h g", h=SH),
                                        summed[:, :].rearrange("p (h g) -> p h g", h=SH), inv_wide, ALU.mult)

            @block.tensor
            def _(pe):
                pe.wait_ge(s_w, 80)
                pe.wait_ge(s_wide, 1)
                for q in range(4):
                    cols = slice(q * P, (q + 1) * P)
                    for a in range(KC):
                        nc.tensor.matmul(mats[a][:, cols], wx_t[:, q, a * P:(a + 1) * P], pair[:, :], start=True, stop=True)
                    last = nc.tensor.matmul(row[:, cols], bx_wide[:, q, :], pair[:, :], start=True, stop=True)
                last.then_inc(s_mat, 1)


def slices_stage(nc, k, token, logits):
    with stage(nc) as (sb, pb, sem):
        xn = [sb(f"sw_xn{u}", [P, C + 1]) for u in range(2)]
        xt = [sb(f"sw_xt{u}", [P, KC, P]) for u in range(2)]
        logit = [sb(f"sw_logit{u}", [P, 2 * C]) for u in range(2)]
        top = [sb(f"sw_top{u}", [P, SH]) for u in range(2)]
        exp = [sb(f"sw_exp{u}", [P, 2 * C]) for u in range(2)]
        den = [sb(f"sw_den{u}", [P, 2, SH]) for u in range(2)]
        soft = [sb(f"sw_soft{u}", [P, 2 * C]) for u in range(2)]
        turned = [pb(f"sw_turned{u}") for u in range(2)]
        s_one, s_xn, s_turned, s_xt, s_lg, s_biased, s_top, s_off, s_exp, s_sum, s_inv, s_soft, s_kept, s_tok = (sem(f"sw_{n}") for n in (
            "ones_set", "rows_ready", "rows_turned", "turned_copied", "logits_ready", "bias_added", "maximum_ready", "maximum_subtracted",
            "exp_ready", "exp_summed", "sum_inverted", "softmax_ready", "softmax_kept", "tokens_added"))
        by_head = lambda ap: ap.rearrange("p (h g) -> p h g", h=SH)
        wide = lambda ap: ap.unsqueeze(2).to_broadcast([P, SH, SLICES])
        with nc.Block() as block:
            @block.gpsimd
            def _(pool):
                start_at_two(pool, s_kept)

                def head(t, u, i):
                    pass

                def tail(t, u, rows):
                    ready(pool, s_soft, t)
                    nc.gpsimd.tensor_copy(at(k.soft, t), soft[u][:, :]).then_inc(s_kept, 1)

                pipelined(pool, head, tail)

            @block.vector
            def _(dve):
                start_at_two(dve, s_xn, s_biased, s_top, s_off, s_sum, s_inv, s_soft)
                for u in range(2):
                    nc.vector.memset(xn[u][:, C:C + 1], 1.0).then_inc(s_one, 1)

                def head(t, u, i):
                    free(dve, s_tok, t)
                    normalise(nc, k, xn[u][:, 0:C], t).then_inc(s_xn, 1)

                def tail(t, u, rows):
                    ready(dve, s_lg, t)
                    free(dve, s_off, t)
                    nc.vector.tensor_tensor(logit[u][:, :], logits[u][:, :], k.b_slice[:, :], ALU.add).then_inc(s_biased, 1)
                    ready(dve, s_biased, t)
                    nc.vector.tensor_reduce(top[u][:, :], by_head(logit[u][:, :]), AX.X, ALU.max).then_inc(s_top, 1)
                    ready(dve, s_top, t)
                    free(dve, s_soft, t)
                    nc.vector.tensor_tensor(by_head(logit[u][:, :]), by_head(logit[u][:, :]), wide(top[u][:, :]), ALU.subtract).then_inc(s_off, 1)
                    ready(dve, s_exp, t)
                    nc.vector.tensor_reduce(den[u][:, 0, :], by_head(exp[u][:, :]), AX.X, ALU.add).then_inc(s_sum, 1)
                    ready(dve, s_sum, t)
                    nc.vector.reciprocal(den[u][:, 1, :], den[u][:, 0, :]).then_inc(s_inv, 1)
                    ready(dve, s_inv, t)
                    free(dve, s_tok, t)
                    free(dve, s_kept, t)
                    nc.vector.tensor_tensor(by_head(soft[u][:, :]), by_head(exp[u][:, :]), wide(den[u][:, 1, :]), ALU.mult).then_inc(s_soft, 1)

                pipelined(dve, head, tail)

            @block.scalar
            def _(act):
                start_at_two(act, s_xt, s_exp)

                def head(t, u, i):
                    ready(act, s_turned, t)
                    free(act, s_lg, t)
                    nc.scalar.activation(xt[u][:, :, :].rearrange("p k n -> p (k n)"), turned[u][:, 0:C], ACT.Copy).then_inc(s_xt, 1)

                def tail(t, u, rows):
                    ready(act, s_off, t)
                    free(act, s_soft, t)
                    nc.scalar.activation(exp[u][:, :], logit[u][:, :], ACT.Exp).then_inc(s_exp, 1)

                pipelined(act, head, tail)

            @block.tensor
            def _(pe):
                start_at_two(pe, s_turned, s_lg, s_tok)
                for q in range(4):
                    nc.tensor.matmul(token[q][:, 0:C + 1], k.zero_b[:, :], k.zero_wide[:, 0:C + 1], start=True, stop=False, skip_group_check=True)

                def head(t, u, i):
                    ready(pe, s_xn, t)
                    free(pe, s_xt, t)
                    for a in range(KC):
                        last = nc.tensor.transpose(turned[u][:, a * P:(a + 1) * P], xn[u][:, a * P:(a + 1) * P], k.ident[:, :])
                    last.then_inc(s_turned, 1)
                    ready(pe, s_xt, t)
                    free(pe, s_biased, t)
                    for a in range(KC):
                        last = nc.tensor.matmul(logits[u][:, :], xt[u][:, a, :], k.w_slice[:, a, :], start=(a == 0), stop=(a == KC - 1))
                    last.then_inc(s_lg, 1)

                def tail(t, u, rows):
                    ready(pe, s_soft, t)
                    pe.wait_ge(s_one, 2)
                    for q in range(4):
                        last = nc.tensor.matmul(token[q][:, 0:C + 1], soft[u][0:rows, q * P:(q + 1) * P], xn[u][0:rows, :], start=False,
                                                stop=(rows == LAST), skip_group_check=True)
                    last.then_inc(s_tok, 1)

                pipelined(pe, head, tail)


def slices_and_attention(nc, k):
    with stage(nc) as (sb, pb, sem):
        token = [pb(f"sw_token{q}") for q in range(4)]
        logits = [pb(f"sw_logits{u}") for u in range(2)]
        slices_stage(nc, k, token, logits)
        slice_attention(nc, k, token, logits)


def slice_attention(nc, k, token, ps):
    with stage(nc) as (sb, pb, sem):
        w_fx = sb("sa_wfx", [P, KC, 2 * C])
        b_fx = sb("sa_bfx", [P, 4, P])
        pairs = sb("sa_pairs", [P, 3, P])
        w_out = sb("sa_wout", [P, 4, C])
        mask = sb("sa_mask", [P, P])
        tok = sb("sa_tok", [P, 4, C + 1])
        tok_t = sb("sa_tok_t", [P, 2, P])
        den = sb("sa_den", [P, 2])
        bterm = sb("sa_bterm", [P, P])
        fx = sb("sa_fx", [P, P])
        fx2 = sb("sa_fx2", [P, P])
        st = sb("sa_st", [P, P])
        st_t = sb("sa_st_t", [P, P])
        q_t = sb("sa_q_t", [P, P])
        k_t = sb("sa_k_t", [P, P])
        v = sb("sa_v", [P, P])
        sc = sb("sa_sc", [P, HD1])
        stat = sb("sa_stat", [P, 3])
        ex = sb("sa_ex", [P, HD1])
        att = sb("sa_att", [P, P])
        att_t = sb("sa_att_t", [P, P])
        o_t = sb("sa_o_t", [P, P])
        s_w, s_v, s_p, s_a = (sem(f"sa_{n}") for n in ("weights_loaded", "vector_steps", "tensor_steps", "exp_steps"))
        V, T = 20, 8
        with nc.Block() as block:
            @block.sync
            def _(sp):
                sp.dma_start(w_fx[:, :, :], k.ins["L0_ffn_W_fx"].rearrange("(k p) n -> p k n", p=P)).then_inc(s_w, 16)
                sp.dma_start(b_fx[:, :, :].rearrange("p q d -> p (q d)"), k.ins["L0_ffn_b_fx"].partition_broadcast(P)).then_inc(s_w, 16)
                sp.dma_start(pairs[:, :, :], k.ins["pair_qkv"].rearrange("i p d -> p i d")).then_inc(s_w, 16)
                sp.dma_start(w_out[:, :, :], k.ins["L0_ffn_W_out"].rearrange("(q p) c -> p q c", p=P)).then_inc(s_w, 16)
                sp.dma_start(mask[:, :], k.ins["blocks64"]).then_inc(s_w, 16)

            @block.vector
            def _(dve):
                nc.vector.memset(att[:, :], 0.0).then_inc(s_v, 1)
                for q in range(4):
                    last = nc.vector.tensor_copy(tok[:, q, :], token[q][:, 0:C + 1])
                last.then_inc(s_v, 1)
                dve.wait_ge(s_w, 80)
                for q in range(4):
                    done = [2 + V * q]

                    def step(instruction):
                        instruction.then_inc(s_v, 1)
                        done[0] += 1
                        dve.wait_ge(s_v, done[0])

                    dve.wait_ge(s_v, 2 + V * q)
                    step(nc.vector.tensor_scalar(den[:, 0:1], tok[:, q, C:C + 1], 1e-5, None, ALU.add))
                    step(nc.vector.reciprocal(den[:, 1:2], den[:, 0:1]))
                    step(nc.vector.tensor_scalar(bterm[:, :], b_fx[:, q, :], tok[:, q, C:C + 1], None, ALU.mult))
                    dve.wait_ge(s_p, T * q + 1)
                    step(nc.vector.tensor_copy(tok_t[:, :, :].rearrange("p a g -> p (a g)"), ps[0][:, 0:C]))
                    dve.wait_ge(s_p, T * q + 2)
                    step(nc.vector.tensor_tensor(fx[:, :], ps[1][:, 0:P], bterm[:, :], ALU.add))
                    step(nc.vector.tensor_scalar(fx2[:, :], fx[:, :], den[:, 1:2], None, ALU.mult))
                    step(nc.vector.tensor_tensor(st[:, :], fx2[:, :], mask[:, :], ALU.mult))
                    dve.wait_ge(s_p, T * q + 3)
                    step(nc.vector.tensor_copy(st_t[:, :], ps[0][:, 0:P]))
                    dve.wait_ge(s_p, T * q + 4)
                    step(nc.vector.tensor_copy(q_t[:, :], ps[1][:, 0:P]))
                    step(nc.vector.tensor_copy(k_t[:, :], ps[1][:, P:2 * P]))
                    step(nc.vector.tensor_copy(v[:, :], ps[1][:, 2 * P:3 * P]))
                    dve.wait_ge(s_p, T * q + 5)
                    nc.vector.tensor_scalar(sc[0:64, :], ps[0][0:64, 0:64], 64 ** -0.5, None, ALU.mult)
                    step(nc.vector.tensor_scalar(sc[64:P, :], ps[0][64:P, 64:P], 64 ** -0.5, None, ALU.mult))
                    step(nc.vector.tensor_reduce(stat[:, 0:1], sc[:, :], AX.X, ALU.max))
                    step(nc.vector.tensor_scalar(sc[:, :], sc[:, :], stat[:, 0:1], None, ALU.subtract))
                    dve.wait_ge(s_a, q + 1)
                    step(nc.vector.tensor_reduce(stat[:, 1:2], ex[:, :], AX.X, ALU.add))
                    step(nc.vector.reciprocal(stat[:, 2:3], stat[:, 1:2]))
                    nc.vector.tensor_scalar(att[0:64, 0:64], ex[0:64, :], stat[0:64, 2:3], None, ALU.mult)
                    step(nc.vector.tensor_scalar(att[64:P, 64:P], ex[64:P, :], stat[64:P, 2:3], None, ALU.mult))
                    dve.wait_ge(s_p, T * q + 6)
                    step(nc.vector.tensor_copy(att_t[:, :], ps[1][:, 0:P]))
                    dve.wait_ge(s_p, T * q + 7)
                    step(nc.vector.tensor_copy(o_t[:, :], ps[0][:, 0:P]))
                    dve.wait_ge(s_p, T * q + 8)
                    step(nc.vector.tensor_copy(k.slices[:, q, :], ps[1][:, 0:C]))
                    assert done[0] == 2 + V * (q + 1)

            @block.scalar
            def _(act):
                for q in range(4):
                    act.wait_ge(s_v, 2 + V * q + 14)
                    nc.scalar.activation(ex[:, :], sc[:, :], ACT.Exp).then_inc(s_a, 1)

            @block.tensor
            def _(pe):
                pe.wait_ge(s_w, 80)
                for q in range(4):
                    base = 2 + V * q
                    pair = slice(q * P, (q + 1) * P)
                    pe.wait_ge(s_v, base)
                    for a in range(KC):
                        last = nc.tensor.transpose(ps[0][:, a * P:(a + 1) * P], tok[:, q, a * P:(a + 1) * P], k.ident[:, :])
                    last.then_inc(s_p, 1)
                    pe.wait_ge(s_v, base + 4)
                    for a in range(KC):
                        last = nc.tensor.matmul(ps[1][:, 0:P], tok_t[:, a, :], w_fx[:, a, pair], start=(a == 0), stop=(a == KC - 1))
                    last.then_inc(s_p, 1)
                    pe.wait_ge(s_v, base + 7)
                    nc.tensor.transpose(ps[0][:, 0:P], st[:, :], k.ident[:, :]).then_inc(s_p, 1)
                    pe.wait_ge(s_v, base + 8)
                    nc.tensor.matmul(ps[1][:, 0:P], pairs[:, 0, :], st_t[:, :], start=True, stop=True)
                    nc.tensor.matmul(ps[1][:, P:2 * P], pairs[:, 1, :], st_t[:, :], start=True, stop=True)
                    nc.tensor.matmul(ps[1][:, 2 * P:3 * P], st_t[:, :], pairs[:, 2, :], start=True, stop=True).then_inc(s_p, 1)
                    pe.wait_ge(s_v, base + 11)
                    nc.tensor.matmul(ps[0][:, 0:P], q_t[:, :], k_t[:, :], start=True, stop=True).then_inc(s_p, 1)
                    pe.wait_ge(s_v, base + 17)
                    nc.tensor.transpose(ps[1][:, 0:P], att[:, :], k.ident[:, :]).then_inc(s_p, 1)
                    pe.wait_ge(s_v, base + 18)
                    nc.tensor.matmul(ps[0][:, 0:P], v[:, :], att_t[:, :], start=True, stop=True).then_inc(s_p, 1)
                    pe.wait_ge(s_v, base + 19)
                    nc.tensor.matmul(ps[1][:, 0:C], o_t[:, :], w_out[:, q, :], start=True, stop=True).then_inc(s_p, 1)


def second_update_stage(nc, k):
    with stage(nc) as (sb, pb, sem):
        bias = sb("su_bias", [P, C])
        soft = [sb(f"su_soft{u}", [P, 2 * C]) for u in range(2)]
        soft_t = [sb(f"su_soft_t{u}", [P, 4, P]) for u in range(2)]
        turned = [pb(f"su_turned{u}") for u in range(2)]
        out = [pb(f"su_out{u}") for u in range(2)]
        s_w = sem("su_bias_loaded")
        s_soft, s_turned, s_copied, s_out, s_add, s_x, s_stats, s_step, s_rstd = (sem(f"su_{n}") for n in (
            "softmax_copied", "softmax_turned", "turned_copied", "out_ready", "out_added", "x_updated", "stats_ready", "moment_steps", "rstd"))
        with nc.Block() as block:
            @block.sync
            def _(sp):
                sp.dma_start(bias[:, :], k.ins["L0_ffn_b_out"].partition_broadcast(P)).then_inc(s_w, 16)

            @block.gpsimd
            def _(pool):
                start_at_two(pool, s_soft)

                def head(t, u, i):
                    free(pool, s_turned, t)
                    nc.gpsimd.tensor_copy(soft[u][:, :], at(k.soft, t)).then_inc(s_soft, 1)

                pipelined(pool, head, no_tail)
                row_scale(nc, pool, k, s_step, s_rstd)

            @block.vector
            def _(dve):
                start_at_two(dve, s_add, s_x, s_stats)
                dve.wait_ge(s_w, 16)

                def tail(t, u, rows):
                    ready(dve, s_out, t)
                    nc.vector.tensor_tensor(at(k.x, t), at(k.x, t), out[u][:, 0:C], ALU.add).then_inc(s_add, 1)
                    ready(dve, s_add, t)
                    nc.vector.tensor_tensor(at(k.x, t), at(k.x, t), bias[:, :], ALU.add).then_inc(s_x, 1)
                    ready(dve, s_x, t)
                    carry(dve, k)
                    row_stats(nc, k, t).then_inc(s_stats, 1)

                pipelined(dve, no_head, tail)
                ready(dve, s_stats, TILES - 1)
                row_moments(nc, dve, k, s_step)

            @block.scalar
            def _(act):
                start_at_two(act, s_copied)

                def head(t, u, i):
                    ready(act, s_turned, t)
                    free(act, s_out, t)
                    nc.scalar.activation(soft_t[u][:, :, :].rearrange("p k n -> p (k n)"), turned[u][:, :], ACT.Copy).then_inc(s_copied, 1)

                pipelined(act, head, no_tail)

            @block.tensor
            def _(pe):
                start_at_two(pe, s_turned, s_out)

                def head(t, u, i):
                    ready(pe, s_soft, t)
                    free(pe, s_copied, t)
                    for a in range(4):
                        last = nc.tensor.transpose(turned[u][:, a * P:(a + 1) * P], soft[u][:, a * P:(a + 1) * P], k.ident[:, :])
                    last.then_inc(s_turned, 1)

                def tail(t, u, rows):
                    ready(pe, s_copied, t)
                    free(pe, s_add, t)
                    for q in range(4):
                        last = nc.tensor.matmul(out[u][:, 0:C], soft_t[u][:, q, :], k.slices[:, q, :], start=(q == 0), stop=(q == 3))
                    last.then_inc(s_out, 1)

                pipelined(pe, head, tail)


def layer1_and_attention(nc, k):
    with stage(nc) as (sb, pb, sem):
        hk = [pb(f"la_hk{u}") for u in range(2)]
        product = pb("la_product")
        keysum = pb("la_keysum")
        layer1_stage(nc, k, hk, product, keysum)
        attention_matrix(nc, k, product, keysum, hk)


def layer1_stage(nc, k, hk, product, keysum):
    with stage(nc) as (sb, pb, sem):
        w = sb("la_w", [P, KC, 3 * C])
        b1 = sb("la_b1", [P, C])
        xn = [sb(f"la_xn{u}", [P, C]) for u in range(2)]
        xt = [sb(f"la_xt{u}", [P, KC, P]) for u in range(2)]
        pre = [sb(f"la_pre{u}", [P, C]) for u in range(2)]
        row = [sb(f"la_row{u}", [P, C]) for u in range(2)]
        bn = [sb(f"la_bn{u}", [P, 8, 6]) for u in range(2)]
        mv = [sb(f"la_mv{u}", [P, 8, 2]) for u in range(2)]
        rs = [sb(f"la_rs{u}", [P, 8]) for u in range(2)]
        kv = [sb(f"la_kv{u}", [P, 2 * C]) for u in range(2)]
        turned = [pb(f"la_turned{u}") for u in range(2)]
        vp = [pb(f"la_v{u}") for u in range(2)]
        s_stored = [sem(f"la_table_stored{u}") for u in range(2)]
        s_w = sem("la_weights_loaded")
        s_xn, s_kept, s_turned, s_xt, s_h, s_pre, s_row, s_bn, s_mv, s_eps, s_rs, s_mid, s_kv, s_sum = (sem(f"la_{n}") for n in (
            "rows_ready", "rows_kept", "rows_turned", "turned_copied", "products_ready", "bias_added", "table_row", "bn_ready", "variance_ready",
            "eps_added", "scale_ready", "mean_subtracted", "kv_ready", "product_added"))
        by_head = lambda ap: ap.rearrange("p (h d) -> p h d", d=HD1)
        wide = lambda ap: ap.unsqueeze(2).to_broadcast([P, 4, HD1])
        with nc.Block() as block:
            @block.sync
            def _(sp):
                sp.dma_start(w[:, :, 0:C], k.ins["L1_gnn_c1_w1"].rearrange("(k p) n -> p k n", p=P)).then_inc(s_w, 16)
                sp.dma_start(w[:, :, C:3 * C], k.ins["L1_mix_wkvT"].rearrange("(k p) n -> p k n", p=P)).then_inc(s_w, 16)
                sp.dma_start(b1[:, :], k.ins["L1_gnn_c1_b1"].partition_broadcast(P)).then_inc(s_w, 16)
                for u in range(2):
                    sp.sem_inc(s_stored[u], 16)

                def tail(t, u, rows):
                    ready(sp, s_row, t)
                    sp.dma_start(table_rows(k, t), row[u][:, :]).then_inc(s_stored[u], 16)

                pipelined(sp, no_head, tail)
                sp.wait_ge(s_stored[0], 16 + 16 * (TILES // 2 + 1))
                sp.wait_ge(s_stored[1], 16 + 16 * (TILES // 2))

            @block.gpsimd
            def _(pool):
                start_at_two(pool, s_kept, s_eps, s_rs)

                def head(t, u, i):
                    ready(pool, s_xn, t)
                    nc.gpsimd.tensor_copy(at(k.rows, t), xn[u][:, :]).then_inc(s_kept, 1)

                def tail(t, u, rows):
                    ready(pool, s_mv, t)
                    carry(pool, k)
                    nc.gpsimd.tensor_scalar(rs[u][:, :], mv[u][:, :, 1], EPS, None, ALU.add).then_inc(s_eps, 1)
                    ready(pool, s_eps, t)
                    nc.gpsimd.tensor_tensor(rs[u][:, :], rs[u][:, :], k.half[:, 0:1].to_broadcast([P, 8]), ALU.pow).then_inc(s_rs, 1)

                pipelined(pool, head, tail)

            @block.vector
            def _(dve):
                start_at_two(dve, s_xn, s_pre, s_bn, s_mv, s_mid, s_kv)
                dve.wait_ge(s_w, 48)

                def head(t, u, i):
                    free(dve, s_turned, t)
                    free(dve, s_kept, t)
                    normalise(nc, k, xn[u][:, :], t).then_inc(s_xn, 1)

                def tail(t, u, rows):
                    ready(dve, s_h, t)
                    free(dve, s_row, t)
                    nc.vector.tensor_tensor(pre[u][:, :], hk[u][:, 0:C], b1[:, :], ALU.add).then_inc(s_pre, 1)
                    for h in range(8):
                        src = hk[u][:, C + HD1 * h:C + HD1 * (h + 1)] if h < 4 else vp[u][:, HD1 * (h - 4):HD1 * (h - 3)]
                        last = nc.vector.bn_stats(bn[u][:, h, :], src)
                    last.then_inc(s_bn, 1)
                    ready(dve, s_bn, t)
                    free(dve, s_kv, t)
                    carry(dve, k)
                    for h in range(8):
                        last = nc.vector.bn_aggr(mv[u][:, h, :], bn[u][:, h, :])
                    last.then_inc(s_mv, 1)
                    ready(dve, s_mv, t)
                    free(dve, s_sum, t)
                    nc.vector.tensor_tensor(by_head(kv[u][:, 0:C]), by_head(hk[u][:, C:2 * C]), wide(mv[u][:, 0:4, 0]), ALU.subtract)
                    nc.vector.tensor_tensor(by_head(kv[u][:, C:2 * C]), by_head(vp[u][:, 0:C]), wide(mv[u][:, 4:8, 0]), ALU.subtract).then_inc(s_mid, 1)
                    ready(dve, s_mid, t)
                    ready(dve, s_rs, t)
                    nc.vector.tensor_tensor(by_head(kv[u][:, :]), by_head(kv[u][:, :]), rs[u][:, :].unsqueeze(2).to_broadcast([P, 8, HD1]),
                                            ALU.mult).then_inc(s_kv, 1)

                pipelined(dve, head, tail)

            @block.scalar
            def _(act):
                start_at_two(act, s_xt, s_row)

                def head(t, u, i):
                    ready(act, s_turned, t)
                    free(act, s_h, t)
                    nc.scalar.activation(xt[u][:, :, :].rearrange("p k n -> p (k n)"), turned[u][:, 0:C], ACT.Copy).then_inc(s_xt, 1)
                    act.wait_ge(s_stored[u], 16 * i + 16)

                def tail(t, u, rows):
                    ready(act, s_pre, t)
                    nc.scalar.activation(row[u][:, :], pre[u][:, :], ACT.Relu).then_inc(s_row, 1)

                pipelined(act, head, tail)

            @block.tensor
            def _(pe):
                start_at_two(pe, s_turned, s_h, s_sum)
                for bank in (product, keysum):
                    nc.tensor.matmul(bank[:, 0:C + KC], k.zero_b[:, :], k.zero_wide[:, 0:C + KC], start=True, stop=False, skip_group_check=True)
                pe.wait_ge(s_w, 48)

                def head(t, u, i):
                    ready(pe, s_xn, t)
                    free(pe, s_xt, t)
                    for a in range(KC):
                        last = nc.tensor.transpose(turned[u][:, a * P:(a + 1) * P], xn[u][:, a * P:(a + 1) * P], k.ident[:, :])
                    last.then_inc(s_turned, 1)
                    ready(pe, s_xt, t)
                    free(pe, s_mid, t)
                    for a in range(KC):
                        nc.tensor.matmul(hk[u][:, :], xt[u][:, a, :], w[:, a, 0:2 * C], start=(a == 0), stop=(a == KC - 1))
                    for a in range(KC):
                        last = nc.tensor.matmul(vp[u][:, 0:C], xt[u][:, a, :], w[:, a, 2 * C:3 * C], start=(a == 0), stop=(a == KC - 1))
                    last.then_inc(s_h, 1)

                def tail(t, u, rows):
                    ready(pe, s_kv, t)
                    stop = rows == LAST
                    nc.tensor.matmul(keysum[:, 0:C], k.ones[0:rows, :], kv[u][0:rows, 0:C], start=False, stop=stop, skip_group_check=True)
                    for a in range(KC):
                        values = kv[u][0:rows, C + a * P:C + (a + 1) * P]
                        nc.tensor.matmul(product[:, a * P:(a + 1) * P], values, kv[u][0:rows, a * P:(a + 1) * P], start=False, stop=stop,
                                         skip_group_check=True)
                        last = nc.tensor.matmul(product[:, C + a:C + a + 1], values, k.ones[0:rows, 0:1], start=False, stop=stop,
                                                skip_group_check=True)
                    last.then_inc(s_sum, 1)

                pipelined(pe, head, tail)


def attention_matrix(nc, k, product, keysum, ps):
    with stage(nc) as (sb, pb, sem):
        wq = sb("am_wq", [P, KC, C])
        wo = sb("am_wo", [P, KC, C])
        key_rows = sb("am_key_rows", [P, 2, P])
        val_cols = sb("am_val_cols", [P, 2])
        mask = sb("am_mask", [P, P])
        t0 = sb("am_t0", [P, KC, P])
        t1 = sb("am_t1", [P, KC, P])
        t2 = sb("am_t2", [P, KC, P])
        t3 = sb("am_t3", [P, KC, P])
        kv_t = sb("am_kv_t", [P, KC, P])
        half = sb("am_half", [P, KC, C])
        s_w, s_v, s_p = (sem(f"am_{n}") for n in ("weights_loaded", "vector_steps", "tensor_steps"))
        with nc.Block() as block:
            @block.sync
            def _(sp):
                sp.dma_start(wq[:, :, :], k.ins["L1_mix_wq"].rearrange("(k p) n -> p k n", p=P)).then_inc(s_w, 16)
                sp.dma_start(wo[:, :, :], k.ins["L1_mix_woT"].rearrange("(k p) n -> p k n", p=P)).then_inc(s_w, 16)
                sp.dma_start(key_rows[:, 0, :], k.ins["key_g2"].partition_broadcast(P)).then_inc(s_w, 16)
                sp.dma_start(key_rows[:, 1, :], k.ins["key_b2"].partition_broadcast(P)).then_inc(s_w, 16)
                sp.dma_start(val_cols[:, :], k.ins["val_gb2"]).then_inc(s_w, 16)
                sp.dma_start(mask[:, :], k.ins["blocks64"]).then_inc(s_w, 16)

            @block.vector
            def _(dve):
                dve.wait_ge(s_w, 96)
                for a in range(KC):
                    part = slice(a * P, (a + 1) * P)
                    gk, bk = key_rows[:, 0, :], key_rows[:, 1, :]
                    gv, bv = val_cols[:, 0:1], val_cols[:, 1:2]
                    done = [9 * a]

                    def step(instruction):
                        instruction.then_inc(s_v, 1)
                        done[0] += 1
                        dve.wait_ge(s_v, done[0])

                    step(nc.vector.tensor_scalar(t0[:, a, :], product[:, part], gv, None, ALU.mult))
                    step(nc.vector.tensor_scalar(t1[:, a, :], keysum[:, part], bv, None, ALU.mult))
                    step(nc.vector.tensor_tensor(t0[:, a, :], t0[:, a, :], t1[:, a, :], ALU.add))
                    step(nc.vector.tensor_tensor(t0[:, a, :], t0[:, a, :], gk, ALU.mult))
                    step(nc.vector.tensor_scalar(t2[:, a, 0:1], product[:, C + a:C + a + 1], gv, None, ALU.mult))
                    step(nc.vector.scalar_tensor_tensor(t3[:, a, 0:1], bv, float(NODES), t2[:, a, 0:1], ALU.mult, ALU.add))
                    step(nc.vector.scalar_tensor_tensor(t1[:, a, :], bk, t3[:, a, 0:1], t0[:, a, :], ALU.mult, ALU.add))
                    step(nc.vector.scalar_tensor_tensor(kv_t[:, a, :], t1[:, a, :], 1.0 / NODES, mask[:, :], ALU.mult, ALU.mult))
                    dve.wait_ge(s_p, a + 1)
                    step(nc.vector.tensor_copy(half[:, a, :], ps[0][:, a * C:(a + 1) * C]))
                dve.wait_ge(s_p, KC + 1)
                nc.vector.tensor_copy(k.mix1[:, :, :].rearrange("p k n -> p (k n)"), ps[1][:, :])

            @block.tensor
            def _(pe):
                pe.wait_ge(s_w, 96)
                for a in range(KC):
                    pe.wait_ge(s_v, 9 * a + 8)
                    nc.tensor.matmul(ps[0][:, a * C:(a + 1) * C], kv_t[:, a, :], wo[:, a, :], start=True, stop=True).then_inc(s_p, 1)
                pe.wait_ge(s_v, 9 * KC)
                for b in range(KC):
                    for a in range(KC):
                        last = nc.tensor.matmul(ps[1][:, b * C:(b + 1) * C], wq[:, a, b * P:(b + 1) * P], half[:, a, :], start=(a == 0), stop=(a == KC - 1))
                last.then_inc(s_p, 1)


def node_stats_scale(nc, k, name, stats, gamma, beta, scale, shift):
    with stage(nc) as (sb, pb, sem):
        mv = sb(f"{name}_mv", [P, KC, 2])
        par = sb(f"{name}_par", [P, 2, KC])
        tmp = sb(f"{name}_tmp", [P, 3, KC])
        s_w, s_v, s_p = (sem(f"{name}_{n}") for n in ("parameters", "vector_steps", "pool_steps"))
        with nc.Block() as block:
            @block.sync
            def _(sp):
                sp.dma_start(par[:, 0, :], gamma).then_inc(s_w, 16)
                sp.dma_start(par[:, 1, :], beta).then_inc(s_w, 16)

            @block.gpsimd
            def _(pool):
                pool.wait_ge(s_v, 1)
                nc.gpsimd.tensor_scalar(tmp[:, 0, :], mv[:, :, 1], EPS, None, ALU.add).then_inc(s_p, 1)
                pool.wait_ge(s_p, 1)
                nc.gpsimd.tensor_tensor(tmp[:, 1, :], tmp[:, 0, :], k.half[:, 0:1].to_broadcast([P, KC]), ALU.pow).then_inc(s_p, 1)

            @block.vector
            def _(dve):
                for a in range(KC):
                    last = nc.vector.bn_aggr(mv[:, a, :], stats[:, a, :, :].rearrange("p t s -> p (t s)"))
                last.then_inc(s_v, 1)
                dve.wait_ge(s_w, 32)
                dve.wait_ge(s_p, 2)
                nc.vector.tensor_tensor(scale, tmp[:, 1, :], par[:, 0, :], ALU.mult).then_inc(s_v, 1)
                dve.wait_ge(s_v, 2)
                nc.vector.tensor_tensor(tmp[:, 2, :], scale, mv[:, :, 0], ALU.mult).then_inc(s_v, 1)
                dve.wait_ge(s_v, 3)
                nc.vector.tensor_tensor(shift, par[:, 1, :], tmp[:, 2, :], ALU.subtract)


def convolve_stage(nc, k, name, w2_in, b2_in, gamma1, beta1, gamma2, beta2, scale, shift):
    CHUNK = 448
    CHUNKS = PADDED // CHUNK
    SHORT = NODES - (CHUNKS - 1) * CHUNK
    chunk = lambda c: k.sums_t[:, :, c * CHUNK:(c + 1) * CHUNK] if isinstance(c, int) else k.sums_t[:, :, bass.ds(c * CHUNK, CHUNK)]
    with stage(nc) as (sb, pb, sem):
        w2 = sb(f"{name}_w2", [P, KC, C])
        b2 = sb(f"{name}_b2", [P, KC])
        stats = sb(f"{name}_stats", [P, KC, CHUNKS, 6])
        scale1 = sb(f"{name}_scale1", [P, KC])
        shift1 = sb(f"{name}_shift1", [P, KC])
        out = [[pb(f"{name}_out{u}{a}") for a in range(KC)] for u in range(2)]
        s_w = sem(f"{name}_weights_loaded")
        s_out, s_h, s_stats = (sem(f"{name}_{n}") for n in ("out_ready", "h_ready", "stats_ready"))
        with nc.Block() as block:
            @block.sync
            def _(sp):
                sp.dma_start(w2[:, :, :], w2_in.rearrange("(k p) n -> p k n", p=P)).then_inc(s_w, 16)
                sp.dma_start(b2[:, :], b2_in).then_inc(s_w, 16)

            @block.vector
            def _(dve):
                def tail(c, u, last_chunk):
                    ready(dve, s_h, c)
                    chunk_stats = stats[:, :, c:c + 1, :] if isinstance(c, int) else stats[:, :, bass.ds(c, 1), :]
                    carry(dve, k)
                    for a in range(KC):
                        last = nc.vector.bn_stats(chunk_stats[:, a, 0, :], chunk(c)[:, a, 0:SHORT if last_chunk else CHUNK])
                    last.then_inc(s_stats, 1)

                pipelined_chunks(dve, CHUNKS, no_head, tail)

            @block.scalar
            def _(act):
                start_at_two(act, s_h)
                act.wait_ge(s_w, 32)

                def tail(c, u, last_chunk):
                    ready(act, s_out, c)
                    for a in range(KC):
                        last = nc.scalar.activation(chunk(c)[:, a, :], out[u][a][:, 0:CHUNK], ACT.Identity, bias=b2[:, a:a + 1])
                    last.then_inc(s_h, 1)

                pipelined_chunks(act, CHUNKS, no_head, tail)

            @block.tensor
            def _(pe):
                start_at_two(pe, s_out)
                pe.wait_ge(s_w, 32)

                def head(c, u, i):
                    free(pe, s_h, c)
                    for a in range(KC):
                        for b in range(KC):
                            last = nc.tensor.matmul(out[u][a][:, 0:CHUNK], w2[:, b, a * P:(a + 1) * P], chunk(c)[:, b, :], start=(b == 0), stop=(b == KC - 1))
                    last.then_inc(s_out, 1)

                pipelined_chunks(pe, CHUNKS, head, no_tail)

        node_stats_scale(nc, k, f"{name}_bn1", stats, gamma1, beta1, scale1[:, :], shift1[:, :])
        s_y = sem(f"{name}_relu_ready")
        with nc.Block() as block:
            @block.scalar
            def _(act):
                for c in range(CHUNKS):
                    for a in range(KC):
                        part = chunk(c)[:, a, :]
                        last = nc.scalar.activation(part, part, ACT.Relu, bias=shift1[:, a:a + 1], scale=scale1[:, a:a + 1])
                    last.then_inc(s_y, 1)

            @block.vector
            def _(dve):
                for c in range(CHUNKS):
                    dve.wait_ge(s_y, c + 1)
                    for a in range(KC):
                        nc.vector.bn_stats(stats[:, a, c, :], chunk(c)[:, a, 0:SHORT if c == CHUNKS - 1 else CHUNK])
        node_stats_scale(nc, k, f"{name}_bn2", stats, gamma2, beta2, scale[:, :], shift[:, :])


def table2_stage(nc, k, scale, shift):
    with stage(nc) as (sb, pb, sem):
        w1 = sb("tb_w1", [P, KC, C])
        b1 = sb("tb_b1", [P, C])
        h_t = [sb(f"tb_h_t{u}", [P, KC, P]) for u in range(2)]
        pre = [sb(f"tb_pre{u}", [P, C]) for u in range(2)]
        row = [sb(f"tb_row{u}", [P, C]) for u in range(2)]
        out = [pb(f"tb_out{u}") for u in range(2)]
        s_stored = [sem(f"tb_table_stored{u}") for u in range(2)]
        s_w, s_h, s_out, s_pre, s_row = (sem(f"tb_{n}") for n in ("weights_loaded", "h_ready", "out_ready", "bias_added", "table_row"))
        with nc.Block() as block:
            @block.sync
            def _(sp):
                sp.dma_start(w1[:, :, :], k.ins["L1_gnn_c2_w1"].rearrange("(k p) n -> p k n", p=P)).then_inc(s_w, 16)
                sp.dma_start(b1[:, :], k.ins["L1_gnn_c2_b1"].partition_broadcast(P)).then_inc(s_w, 16)
                for u in range(2):
                    sp.sem_inc(s_stored[u], 16)

                def tail(t, u, rows):
                    ready(sp, s_row, t)
                    sp.dma_start(table_rows(k, t), row[u][:, :]).then_inc(s_stored[u], 16)

                pipelined(sp, no_head, tail)
                sp.wait_ge(s_stored[0], 16 + 16 * (TILES // 2 + 1))
                sp.wait_ge(s_stored[1], 16 + 16 * (TILES // 2))

            @block.vector
            def _(dve):
                start_at_two(dve, s_pre)
                dve.wait_ge(s_w, 32)

                def tail(t, u, rows):
                    ready(dve, s_out, t)
                    free(dve, s_row, t)
                    nc.vector.tensor_tensor(pre[u][:, :], out[u][:, 0:C], b1[:, :], ALU.add).then_inc(s_pre, 1)

                pipelined(dve, no_head, tail)

            @block.scalar
            def _(act):
                start_at_two(act, s_h, s_row)

                def head(t, u, i):
                    free(act, s_out, t)
                    for a in range(KC):
                        last = nc.scalar.activation(h_t[u][:, a, :], nodes(k, t)[:, a, :], ACT.Relu, bias=shift[:, a:a + 1], scale=scale[:, a:a + 1])
                    last.then_inc(s_h, 1)
                    act.wait_ge(s_stored[u], 16 * i + 16)

                def tail(t, u, rows):
                    ready(act, s_pre, t)
                    nc.scalar.activation(row[u][:, :], pre[u][:, :], ACT.Relu).then_inc(s_row, 1)

                pipelined(act, head, tail)

            @block.tensor
            def _(pe):
                start_at_two(pe, s_out)
                pe.wait_ge(s_w, 32)

                def head(t, u, i):
                    ready(pe, s_h, t)
                    free(pe, s_pre, t)
                    for a in range(KC):
                        last = nc.tensor.matmul(out[u][:, 0:C], h_t[u][:, a, :], w1[:, a, :], start=(a == 0), stop=(a == KC - 1))
                    last.then_inc(s_out, 1)

                pipelined(pe, head, no_tail)


def third_update_stage(nc, k, scale, shift):
    with stage(nc) as (sb, pb, sem):
        bias = sb("tu_bias", [P, C])
        h_t = [sb(f"tu_h_t{u}", [P, KC, P]) for u in range(2)]
        xn = [sb(f"tu_xn{u}", [P, C]) for u in range(2)]
        xt = [sb(f"tu_xt{u}", [P, KC, P]) for u in range(2)]
        res = [sb(f"tu_res{u}", [P, C]) for u in range(2)]
        turned = [pb(f"tu_turned{u}") for u in range(2)]
        x_turned = [pb(f"tu_x_turned{u}") for u in range(2)]
        out = [pb(f"tu_out{u}") for u in range(2)]
        s_w = sem("tu_bias_loaded")
        s_h, s_xn, s_turned, s_xt, s_out, s_res, s_relu, s_add, s_x, s_stats, s_step, s_rstd = (sem(f"tu_{n}") for n in (
            "h_ready", "rows_copied", "turned", "rows_turned_copied", "out_ready", "residual_added", "relu_added", "out_added", "x_updated",
            "stats_ready", "moment_steps", "rstd"))
        with nc.Block() as block:
            @block.sync
            def _(sp):
                sp.dma_start(bias[:, :], k.ins["L1_mix_bo"].partition_broadcast(P)).then_inc(s_w, 16)

            @block.gpsimd
            def _(pool):
                start_at_two(pool, s_xn)

                def head(t, u, i):
                    free(pool, s_turned, t)
                    free(pool, s_res, t)
                    nc.gpsimd.tensor_copy(xn[u][:, :], at(k.rows, t)).then_inc(s_xn, 1)

                pipelined(pool, head, no_tail)
                row_scale(nc, pool, k, s_step, s_rstd)

            @block.vector
            def _(dve):
                start_at_two(dve, s_res, s_relu, s_add, s_x, s_stats)
                dve.wait_ge(s_w, 16)

                def head(t, u, i):
                    ready(dve, s_turned, t)
                    ready(dve, s_xn, t)
                    free(dve, s_relu, t)
                    nc.vector.tensor_tensor(res[u][:, :], turned[u][:, 0:C], xn[u][:, :], ALU.add).then_inc(s_res, 1)

                def tail(t, u, rows):
                    ready(dve, s_res, t)
                    nc.vector.scalar_tensor_tensor(at(k.x, t), res[u][:, :], 0.0, at(k.x, t), ALU.max, ALU.add).then_inc(s_relu, 1)
                    ready(dve, s_relu, t)
                    ready(dve, s_out, t)
                    nc.vector.tensor_tensor(at(k.x, t), at(k.x, t), out[u][:, 0:C], ALU.add).then_inc(s_add, 1)
                    ready(dve, s_add, t)
                    nc.vector.tensor_tensor(at(k.x, t), at(k.x, t), bias[:, :], ALU.add).then_inc(s_x, 1)
                    ready(dve, s_x, t)
                    carry(dve, k)
                    row_stats(nc, k, t).then_inc(s_stats, 1)

                pipelined(dve, head, tail)
                ready(dve, s_stats, TILES - 1)
                row_moments(nc, dve, k, s_step)

            @block.scalar
            def _(act):
                start_at_two(act, s_h, s_xt)

                def head(t, u, i):
                    free(act, s_turned, t)
                    for a in range(KC):
                        last = nc.scalar.activation(h_t[u][:, a, :], nodes(k, t)[:, a, :], ACT.Identity, bias=shift[:, a:a + 1], scale=scale[:, a:a + 1])
                    last.then_inc(s_h, 1)
                    ready(act, s_turned, t)
                    free(act, s_out, t)
                    nc.scalar.activation(xt[u][:, :, :].rearrange("p k n -> p (k n)"), x_turned[u][:, 0:C], ACT.Copy).then_inc(s_xt, 1)

                pipelined(act, head, no_tail)

            @block.tensor
            def _(pe):
                start_at_two(pe, s_turned, s_out)

                def head(t, u, i):
                    ready(pe, s_h, t)
                    ready(pe, s_xn, t)
                    free(pe, s_xt, t)
                    free(pe, s_res, t)
                    for a in range(KC):
                        nc.tensor.transpose(turned[u][:, a * P:(a + 1) * P], h_t[u][:, a, :], k.ident[:, :])
                    for a in range(KC):
                        last = nc.tensor.transpose(x_turned[u][:, a * P:(a + 1) * P], xn[u][:, a * P:(a + 1) * P], k.ident[:, :])
                    last.then_inc(s_turned, 1)

                def tail(t, u, rows):
                    ready(pe, s_xt, t)
                    free(pe, s_add, t)
                    for a in range(KC):
                        last = nc.tensor.matmul(out[u][:, 0:C], xt[u][:, a, :], k.mix1[:, a, :], start=(a == 0), stop=(a == KC - 1))
                    last.then_inc(s_out, 1)

                pipelined(pe, head, tail)


def router_stage(nc, k):
    E = EXPERTS
    with stage(nc) as (sb, pb, sem):
        wr = sb("ro_wr", [P, KC, E])
        br = sb("ro_br", [P, E])
        gb = sb("ro_gb", [P, 2, C])
        z = [sb(f"ro_z{u}", [P, C]) for u in range(2)]
        zg = [sb(f"ro_zg{u}", [P, C]) for u in range(2)]
        xn = [sb(f"ro_xn{u}", [P, C]) for u in range(2)]
        xt = [sb(f"ro_xt{u}", [P, KC, P]) for u in range(2)]
        logit = sb("ro_logit", [P, TILES, E])
        turned = [pb(f"ro_turned{u}") for u in range(2)]
        logits = [pb(f"ro_logits{u}") for u in range(2)]
        s_w = sem("ro_weights_loaded")
        s_z, s_zg, s_xn, s_turned, s_xt, s_kept, s_lg, s_logit = (sem(f"ro_{n}") for n in (
            "z_ready", "scaled", "rows_ready", "rows_turned", "turned_copied", "turned_kept", "logits_ready", "bias_added"))
        with nc.Block() as block:
            @block.sync
            def _(sp):
                sp.dma_start(wr[:, :, :], k.ins["L1_ffn_Wr"].rearrange("(k p) n -> p k n", p=P)).then_inc(s_w, 16)
                sp.dma_start(br[:, :], k.ins["L1_ffn_br"].partition_broadcast(P)).then_inc(s_w, 16)
                sp.dma_start(gb[:, 0, :], k.ins["L1_ffn_gamma"].partition_broadcast(P)).then_inc(s_w, 16)
                sp.dma_start(gb[:, 1, :], k.ins["L1_ffn_beta"].partition_broadcast(P)).then_inc(s_w, 16)

            @block.gpsimd
            def _(pool):
                start_at_two(pool, s_kept)

                def head(t, u, i):
                    ready(pool, s_xt, t)
                    nc.gpsimd.tensor_copy(nodes(k, t), xt[u][:, :, :]).then_inc(s_kept, 1)

                pipelined(pool, head, no_tail)

            @block.vector
            def _(dve):
                start_at_two(dve, s_z, s_zg, s_xn, s_logit)
                dve.wait_ge(s_w, 64)

                def head(t, u, i):
                    free(dve, s_zg, t)
                    normalise(nc, k, z[u][:, :], t).then_inc(s_z, 1)
                    ready(dve, s_z, t)
                    free(dve, s_xn, t)
                    nc.vector.tensor_tensor(zg[u][:, :], z[u][:, :], gb[:, 0, :], ALU.mult).then_inc(s_zg, 1)
                    ready(dve, s_zg, t)
                    free(dve, s_turned, t)
                    nc.vector.tensor_tensor(xn[u][:, :], zg[u][:, :], gb[:, 1, :], ALU.add).then_inc(s_xn, 1)

                def tail(t, u, rows):
                    ready(dve, s_lg, t)
                    nc.vector.tensor_tensor(at(logit, t), logits[u][:, 0:E], br[:, :], ALU.add).then_inc(s_logit, 1)

                pipelined(dve, head, tail)

            @block.scalar
            def _(act):
                start_at_two(act, s_xt)

                def head(t, u, i):
                    ready(act, s_turned, t)
                    free(act, s_kept, t)
                    free(act, s_lg, t)
                    nc.scalar.activation(xt[u][:, :, :].rearrange("p k n -> p (k n)"), turned[u][:, 0:C], ACT.Copy).then_inc(s_xt, 1)

                pipelined(act, head, no_tail)

            @block.tensor
            def _(pe):
                start_at_two(pe, s_turned, s_lg)
                pe.wait_ge(s_w, 64)

                def head(t, u, i):
                    ready(pe, s_xn, t)
                    free(pe, s_xt, t)
                    for a in range(KC):
                        last = nc.tensor.transpose(turned[u][:, a * P:(a + 1) * P], xn[u][:, a * P:(a + 1) * P], k.ident[:, :])
                    last.then_inc(s_turned, 1)

                def tail(t, u, rows):
                    ready(pe, s_xt, t)
                    free(pe, s_logit, t)
                    for a in range(KC):
                        last = nc.tensor.matmul(logits[u][:, 0:E], xt[u][:, a, :], wr[:, a, :], start=(a == 0), stop=(a == KC - 1))
                    last.then_inc(s_lg, 1)

                pipelined(pe, head, tail)

        rank = sb("ro_rank", [P, TILES, E])
        cmp = sb("ro_cmp", [P, TILES, E])
        top = sb("ro_top", [P, TILES])
        exp = sb("ro_exp", [P, TILES, E])
        den = sb("ro_den", [P, 2, TILES])
        s_v, s_e = sem("ro_vector_steps"), sem("ro_exp_ready")
        with nc.Block() as block:
            @block.vector
            def _(dve):
                done = [0]

                def step(instruction):
                    instruction.then_inc(s_v, 1)
                    done[0] += 1
                    dve.wait_ge(s_v, done[0])

                step(nc.vector.tensor_reduce(top[:, :], logit[:, :, :], AX.X, ALU.max))
                step(nc.vector.tensor_tensor(exp[:, :, :], logit[:, :, :], top[:, :].unsqueeze(2).to_broadcast([P, TILES, E]), ALU.subtract))
                step(nc.vector.memset(rank[:, :, :], 0.0))
                for other in range(E):
                    them = logit[:, :, other:other + 1]
                    if other:
                        step(nc.vector.tensor_tensor(cmp[:, :, 0:other], them.to_broadcast([P, TILES, other]), logit[:, :, 0:other], ALU.is_gt))
                        step(nc.vector.tensor_tensor(rank[:, :, 0:other], rank[:, :, 0:other], cmp[:, :, 0:other], ALU.add))
                    if other < E - 1:
                        n = E - 1 - other
                        step(nc.vector.tensor_tensor(cmp[:, :, 0:n], them.to_broadcast([P, TILES, n]), logit[:, :, other + 1:E], ALU.is_ge))
                        step(nc.vector.tensor_tensor(rank[:, :, other + 1:E], rank[:, :, other + 1:E], cmp[:, :, 0:n], ALU.add))
                step(nc.vector.tensor_scalar(rank[:, :, :], rank[:, :, :], 2.0, None, ALU.is_lt))
                dve.wait_ge(s_e, 1)
                step(nc.vector.tensor_tensor(rank[:, :, :], rank[:, :, :], exp[:, :, :], ALU.mult))
                step(nc.vector.tensor_reduce(den[:, 0, :], rank[:, :, :], AX.X, ALU.add))
                step(nc.vector.reciprocal(den[:, 1, :], den[:, 0, :]))
                step(nc.vector.tensor_tensor(k.gate[:, :, :], rank[:, :, :], den[:, 1, :].unsqueeze(2).to_broadcast([P, TILES, E]), ALU.mult))

            @block.scalar
            def _(act):
                act.wait_ge(s_v, 2)
                nc.scalar.activation(exp[:, :, :], exp[:, :, :], ACT.Exp).then_inc(s_e, 1)


def experts_stage(nc, k):
    CH = 4
    CHUNKS = TILES // CH
    with stage(nc) as (sb, pb, sem):
        w1 = [sb(f"ex_w1_{v}", [P, KC, HID]) for v in range(2)]
        w2 = [sb(f"ex_w2_{v}", [P, FT, C]) for v in range(2)]
        b1 = sb("ex_b1", [P, EXPERTS, FT])
        b2 = [sb(f"ex_b2_{v}", [P, C]) for v in range(2)]
        gate = [sb(f"ex_gate{v}", [P, TILES]) for v in range(2)]
        b1v = [sb(f"ex_b1_{v}", [P, FT]) for v in range(2)]
        hid = sb("ex_hid", [P, FT, CH * P])
        y = [sb(f"ex_y{u}", [P, C]) for u in range(2)]
        up = [pb(f"ex_up{f}") for f in range(FT)]
        down = [pb(f"ex_down{n}") for n in range(CH)]
        s_w = [sem(f"ex_weights_loaded{v}") for v in range(2)]
        s_out, s_gate = sem("ex_stored"), sem("ex_gate_copied")
        s_up, s_hid, s_down, s_y, s_x, s_use, s_b1 = (sem(f"ex_{n}") for n in (
            "up_ready", "hidden_ready", "down_ready", "bias_added", "x_updated", "weights_used", "small_copied"))
        UP, TL = FT * (CHUNKS + 1), TILES
        with nc.Block() as block:
            @block.sync
            def _(sp):
                sp.dma_start(b1[:, :, :], k.ins["L1_ffn_b1c"]).then_inc(s_out, 16)
                with sp.Fori(0, EXPERTS // 2) as r:
                    for v in range(2):
                        sp.wait_ge(s_use, 2 * r + v + 1)
                        e = 2 * r + v
                        sp.dma_start(w1[v][:, :, :], k.ins["L1_ffn_W1"][bass.ds(e, 1), :, :].rearrange("a (k p) n -> p (a k) n", p=P)).then_inc(s_w[v], 16)
                        sp.dma_start(w2[v][:, :, :], k.ins["L1_ffn_W2"][bass.ds(e, 1), :, :].rearrange("a (k p) n -> p (a k) n", p=P)).then_inc(s_w[v], 16)
                        sp.dma_start(b2[v][:, :], k.ins["L1_ffn_b2"][bass.ds(e, 1), :].rearrange("a n -> (a n)").partition_broadcast(P)).then_inc(s_w[v], 16)

            @block.vector
            def _(dve):
                dve.sem_inc(s_use, 2)
                dve.sem_inc(s_y, 2)
                dve.sem_inc(s_x, 4)
                with dve.Fori(0, EXPERTS // 2) as r:
                    for v in range(2):
                        e = 2 * r + v
                        dve.wait_ge(s_w[v], 48 * r + 48)
                        nc.vector.tensor_copy(gate[v][:, :], k.gate[:, :, bass.ds(e, 1)].rearrange("p t a -> p (t a)")).then_inc(s_gate, 1)
                        dve.wait_ge(s_gate, e + 1)
                        carry(dve, k)

                        def tiles(first, count):
                            for n in range(count):
                                u = n % 2
                                t = first + n
                                seq = TL * e + t
                                dve.wait_ge(s_down, seq + 2)
                                dve.wait_ge(s_x, seq + (4 if n == 0 else 3))
                                nc.vector.tensor_tensor(y[u][:, :], down[n][:, 0:C], b2[v][:, :], ALU.add).then_inc(s_y, 1)
                                dve.wait_ge(s_y, seq + 3)
                                nc.vector.scalar_tensor_tensor(at(k.x, t), y[u][:, :], col(gate[v], t), at(k.x, t), ALU.mult, ALU.add).then_inc(s_x, 1)

                        with dve.Fori(0, CHUNKS) as c:
                            tiles(CH * c, CH)
                        tiles(CH * CHUNKS, TILES - CH * CHUNKS)
                        dve.wait_ge(s_x, TL * e + TL + 4)
                        dve.sem_inc(s_use, 1)

            @block.scalar
            def _(act):
                act.sem_inc(s_hid, FT)
                act.wait_ge(s_out, 16)
                with act.Fori(0, EXPERTS // 2) as r:
                    for v in range(2):
                        e = 2 * r + v
                        nc.scalar.activation(b1v[v][:, :], b1[:, bass.ds(e, 1), :].rearrange("p a f -> p (a f)"), ACT.Copy).then_inc(s_b1, 1)
                        act.wait_ge(s_b1, e + 1)

                        def chunk(c, tiles):
                            for f in range(FT):
                                act.wait_ge(s_up, UP * e + FT * c + f + 1)
                                if f == 0:
                                    act.wait_ge(s_down, TL * e + CH * c + 1)
                                nc.scalar.activation(hid[:, f, 0:tiles * P], up[f][:, 0:tiles * P], ACT.Gelu, bias=b1v[v][:, f:f + 1]).then_inc(s_hid, 1)

                        with act.Fori(0, CHUNKS) as c:
                            chunk(c, CH)
                        chunk(CHUNKS, TILES - CH * CHUNKS)

            @block.tensor
            def _(pe):
                pe.sem_inc(s_down, 1)
                with pe.Fori(0, EXPERTS // 2) as r:
                    for v in range(2):
                        e = 2 * r + v
                        pe.wait_ge(s_w[v], 48 * r + 48)
                        carry(pe, k)

                        def chunk(c, tiles):
                            seq = UP * e + FT * c
                            rows = nodes(k, CH * c, tiles)
                            for f in range(FT):
                                pe.wait_ge(s_hid, seq + f + 1)
                                for a in range(KC):
                                    last = nc.tensor.matmul(up[f][:, 0:tiles * P], w1[v][:, a, f * P:(f + 1) * P], rows[:, a, :],
                                                            start=(a == 0), stop=(a == KC - 1))
                                last.then_inc(s_up, 1)
                            for n in range(tiles):
                                pe.wait_ge(s_x, TL * e + CH * c + n + (4 if n == 0 else 1))
                                if n == 0:
                                    pe.wait_ge(s_hid, seq + 2 * FT)
                                for f in range(FT):
                                    last = nc.tensor.matmul(down[n][:, 0:C], hid[:, f, n * P:(n + 1) * P], w2[v][:, f, :], start=(f == 0), stop=(f == FT - 1))
                                last.then_inc(s_down, 1)

                        with pe.Fori(0, CHUNKS) as c:
                            chunk(c, CH)
                        chunk(CHUNKS, TILES - CH * CHUNKS)

        with nc.Block() as block:
            @block.sync
            def _(sp):
                whole = (TILES - 1) * P
                sp.dma_start(k.out[0:whole, :].rearrange("(t p) c -> p t c", p=P), k.x[:, 0:TILES - 1, :]).then_inc(s_out, 16)
                sp.dma_start(k.out[whole:NODES, :], k.x[0:LAST, TILES - 1, :]).then_inc(s_out, 16)
                sp.wait_ge(s_out, 48)


_INS = ["x_in", "edges", "dst_cols", "blocks32", "blocks64",
        "L0_gnn_W", "L0_mix_WqT", "L0_mix_WkvT", "L0_mix_WprojT", "L0_mix_bproj",
        "L0_ffn_W_fx", "L0_ffn_b_fx", "L0_ffn_W_xT", "L0_ffn_b_x4", "pair_slice", "b_slice8", "pair_qkv", "L0_ffn_W_out", "L0_ffn_b_out",
        "temperature",
        "L1_gnn_c1_w1", "L1_gnn_c1_b1", "L1_gnn_c1_w2", "L1_gnn_c2_w1", "L1_gnn_c2_b1", "L1_gnn_c2_w2", "bn_rows",
        "L1_mix_wq", "L1_mix_wkvT", "L1_mix_woT", "L1_mix_bo", "key_g2", "key_b2", "val_gb2",
        "L1_ffn_gamma", "L1_ffn_beta", "L1_ffn_Wr", "L1_ffn_br", "L1_ffn_W1", "L1_ffn_b1c", "L1_ffn_W2", "L1_ffn_b2"]


def gps_two_layers(nc, ins, out):
    k = Core()
    k.ins = ins
    k.out = out
    k.table = nc.dram_tensor("table", [PADDED, C], F32).ap()
    k.win_dram = nc.dram_tensor("window_bounds", [GROUPS // 2, 4], I32).ap()
    bn = [k.ins["bn_rows"][i] for i in range(10)]
    with ExitStack() as ctx:
        residents(nc, k, ctx)
        setup_stage(nc, k)
        wide_residents(nc, k, ctx)
        with ExitStack() as graph:
            graph_residents(nc, k, graph)
            first_stats_stage(nc, k)
            keys_stage(nc, k)
            edge_stage(nc, k, "e0", False, 0)
            first_update_stage(nc, k)
            with ExitStack() as ffn:
                k.w_slice = ffn.enter_context(nc.sbuf_tensor("w_slice", [P, KC, 2 * C], F32))
                k.b_slice = ffn.enter_context(nc.sbuf_tensor("b_slice", [P, 2 * C], F32))
                slice_weights_stage(nc, k)
                slices_and_attention(nc, k)
            second_update_stage(nc, k)
            layer1_and_attention(nc, k)
            edge_stage(nc, k, "e1", True, 1)
            convolve_stage(nc, k, "c1", k.ins["L1_gnn_c1_w2"], bn[0], bn[1], bn[2], bn[3], bn[4], k.bn_scale, k.bn_shift)
            table2_stage(nc, k, k.bn_scale, k.bn_shift)
            edge_stage(nc, k, "e2", True, 2)
            convolve_stage(nc, k, "c2", k.ins["L1_gnn_c2_w2"], bn[5], bn[6], bn[7], bn[8], bn[9], k.bn_scale, k.bn_shift)
            third_update_stage(nc, k, k.bn_scale, k.bn_shift)
            router_stage(nc, k)
        experts_stage(nc, k)


def kernel(**inputs):
    import numpy as np
    import concourse.bacc as bacc
    from concourse.bass_utils import run_bass_kernel_spmd as run

    i = {n: np.asarray(a) for n, a in inputs.items()}

    def by_column(a, fill):
        flat = np.full(GROUPS * SUB * P, fill, a.dtype)
        flat[:EDGES] = a
        return flat.reshape(GROUPS * SUB, P)

    def twice(w):
        m = np.zeros((P, P), w.dtype)
        m[:64, :64] = w
        m[64:, 64:] = w
        return m

    def blocks(n):
        return np.kron(np.eye(P // n, dtype=np.float32), np.ones((n, n), np.float32))

    src, dst, weight = (by_column(a, f) for a, f in ((i["src"], 0), (i["dst"], PADDED - 1), (i["edge_weight"], 0)))
    edges = np.stack([a.view(np.int32).reshape(2 * TRIPS, 16, P) for a in (src, dst, weight)], 1)
    x = np.zeros((PADDED, C), i["x"].dtype)
    x[:NODES] = i["x"]
    channels = lambda a: a.reshape(KC, P).T
    arrays = {
        "x_in": x, "edges": edges.transpose(0, 3, 1, 2), "dst_cols": dst.T, "blocks32": blocks(32), "blocks64": blocks(64),
        "L0_mix_WqT": i["L0_mix_Wq"].T, "L0_mix_WkvT": i["L0_mix_Wkv"].T, "L0_mix_WprojT": i["L0_mix_Wproj"].T,
        "L0_ffn_W_xT": i["L0_ffn_W_x"].T, "L0_ffn_b_x4": i["L0_ffn_b_x"].reshape(4, P).T, "pair_slice": twice(i["L0_ffn_W_slice"]),
        "b_slice8": np.tile(i["L0_ffn_b_slice"], SH), "pair_qkv": np.stack([twice(i["L0_ffn_W_" + n]) for n in "qkv"]),
        "temperature": i["L0_ffn_temperature"].reshape(-1),
        "bn_rows": np.stack([channels(i["L1_gnn_" + n]) for n in ("c1_b2", "c1_g", "c1_b", "bn1_g", "bn1_b", "c2_b2", "c2_g", "c2_b", "bn2_g", "bn2_b")]),
        "L1_mix_wkvT": np.concatenate([i["L1_mix_wk"].T, i["L1_mix_wv"].T], 1), "L1_mix_woT": i["L1_mix_wo"].T,
        "key_g2": np.tile(i["L1_mix_ln_k_g"], 2), "key_b2": np.tile(i["L1_mix_ln_k_b"], 2),
        "val_gb2": np.stack([np.tile(i["L1_mix_ln_v_g"], 2), np.tile(i["L1_mix_ln_v_b"], 2)], 1),
        "L1_ffn_b1c": i["L1_ffn_b1"].reshape(EXPERTS, FT, P).transpose(2, 0, 1),
    }
    arrays = {n: np.ascontiguousarray(arrays.get(n, i.get(n))) for n in _INS}
    nc = bacc.Bacc("TRN2", target_bir_lowering=False, num_devices=1)
    ins = {n: nc.dram_tensor(f"in_{n}", a.shape, mybir.dt.from_np(a.dtype), kind="ExternalInput").ap() for n, a in arrays.items()}
    out = nc.dram_tensor("out", (NODES, C), F32, kind="ExternalOutput").ap()
    gps_two_layers(nc, ins, out)
    got = run(nc, [{f"in_{n}": a for n, a in arrays.items()}], core_ids=[0])
    return got.results[0]["out"]
```

```python
import concourse.bass as bass
from concourse import mybir
from contextlib import ExitStack, contextmanager

F32 = mybir.dt.float32
I32 = mybir.dt.int32
I16 = mybir.dt.int16
BF16 = mybir.dt.bfloat16
ALU = mybir.AluOpType
ACT = mybir.ActivationFunctionType
AX = mybir.AxisListType

P = 128
NODES = 6250
EDGES = 200000
C = 256
KC = C // P
TILES = -(-NODES // P)
LAST = NODES - (TILES - 1) * P
PADDED = TILES * P
SUB = 8
TRIPS = -(-EDGES // (P * SUB * 4))
GROUPS = 4 * TRIPS
WINDOW = 64
EPS = 1e-5
HEADS0, HD0 = 8, 32
SLICES, SH = 64, 8
HEADS1, HD1 = 4, 64
EXPERTS, HID = 8, 512
FT = HID // P
SLOT_TILES = (2 * PADDED + EXPERTS * (P - 1)) // P
SLOT_TILES += SLOT_TILES % 2


class Core:
    pass


def start_at_two(engine, *sems):
    for s in sems:
        engine.sem_inc(s, 2)


def ready(engine, sem, t):
    engine.wait_ge(sem, t + 3)


def free(engine, sem, t):
    engine.wait_ge(sem, t + 1)


def carry(engine, k):
    engine.sem_inc(k.carried, 1)


def pipelined(engine, head, tail, ahead=1, middle=None, late=None):
    def heads(t, u, i):
        head(t, u, i)
        if late:
            late(t, u, i)

    def step(t, u, i, then):
        head(t + ahead, then, i)
        if middle:
            middle(t, u, P)
        if late:
            late(t + ahead, then, i)
        tail(t, u, P)

    def end(t, u, rows):
        if middle:
            middle(t, u, rows)
        tail(t, u, rows)

    for t in range(ahead):
        heads(t, t, 0)
    if ahead == 1:
        with engine.Fori(0, TILES // 2) as i:
            step(2 * i, 0, i, 1)
            step(2 * i + 1, 1, i + 1, 0)
    else:
        with engine.Fori(0, TILES // 2 - 1) as i:
            step(2 * i, 0, i + 1, 0)
            step(2 * i + 1, 1, i + 1, 1)
        step(TILES - 3, 0, TILES // 2, 0)
        end(TILES - 2, 1, P)
    end(TILES - 1, 0, LAST)


def pipelined_chunks(engine, count, head, tail):
    head(0, 0, 0)
    with engine.Fori(0, count // 2 - 1) as i:
        head(2 * i + 1, 1, i)
        tail(2 * i, 0, False)
        head(2 * i + 2, 0, i + 1)
        tail(2 * i + 1, 1, False)
    head(count - 1, 1, count // 2 - 1)
    tail(count - 2, 0, False)
    tail(count - 1, 1, True)


def interleaved(engine, count, head_a, head_b, tail_a, tail_b):
    def step(t, u):
        head_a(t + 1, 1 - u)
        tail_a(t, u)
        head_b(t + 1, 1 - u)
        tail_b(t, u)

    head_a(0, 0)
    head_b(0, 0)
    with engine.Fori(0, count // 2 - 1) as i:
        step(2 * i, 0)
        step(2 * i + 1, 1)
    step(count - 2, 0)
    tail_a(count - 1, 1)
    tail_b(count - 1, 1)


def nothing(t, u):
    pass


def no_head(t, u, i):
    pass


def no_tail(t, u, rows):
    pass


def table_rows(k, t):
    return k.table[t * P:(t + 1) * P, :] if isinstance(t, int) else k.table[bass.ds(t * P, P), :]


def col(buf, t):
    return buf[:, t:t + 1] if isinstance(t, int) else buf[:, bass.ds(t, 1)]


@contextmanager
def stage(nc):
    sems = []
    with ExitStack() as ctx:
        def sem(name):
            sems.append(ctx.enter_context(nc.semaphore(name)))
            return sems[-1]

        sb = lambda name, shape, dt=F32: ctx.enter_context(nc.sbuf_tensor(name, shape, dt))
        pb = lambda name, shape=(P, 512), dt=F32: ctx.enter_context(nc.psum_tensor(name, list(shape), dt))
        yield sb, pb, sem
        with nc.Block() as block:
            @block.gpsimd
            def _(pool):
                for s in sems:
                    pool.sem_clear(s)


def at(buf, t):
    if isinstance(t, int):
        return buf[:, t, :]
    return buf[:, bass.ds(t, 1), :].rearrange("p a n -> p (a n)")


def nodes(k, t, tiles=1):
    return k.sums_t[:, :, t * P:(t + tiles) * P] if isinstance(t, int) else k.sums_t[:, :, bass.ds(t * P, tiles * P)]


def setup_stage(nc, k):
    with stage(nc) as (sb, pb, sem):
        dst = sb("dst", [P, GROUPS * SUB], I32)
        dst_f = sb("dst_f", [P, GROUPS * SUB])
        part = sb("part", [P, 2, GROUPS * SUB], I32)
        low = sb("low", [P, GROUPS * SUB], BF16)
        high = sb("high", [P, GROUPS * SUB], BF16)
        count_b = sb("count_b", [P, P, 16], BF16)
        low_hot = [sb(f"low_hot{u}", [P, P, 16], BF16) for u in range(2)]
        high_hot = [sb(f"high_hot{u}", [P, TILES, 16], BF16) for u in range(2)]
        ends = sb("ends", [P, 2, GROUPS])
        ends_t = sb("ends_t", [GROUPS // 2, 2, 2])
        ends_i = sb("ends_i", [GROUPS // 2, 2, 2], I32)
        deg = sb("deg", [P, TILES])
        root = sb("root", [P, TILES])
        linked = sb("linked", [P, TILES])
        turned = pb("turned")
        deg_ps = pb("deg_ps")
        s_load, s_x, s_zero, s_const, s_iota = (sem(n) for n in ("dst_loaded", "x_loaded", "zeroed", "const_ready", "iota_ready"))
        s_f, s_part, s_lh, s_ends, s_turned, s_red, s_int, s_win = (sem(n) for n in (
            "dst_float", "parts_int", "parts_ready", "ends_ready", "ends_turned", "ends_reduced", "bounds_ready", "bounds_moved"))
        s_hot, s_free, s_deg, s_degs, s_r, s_half = (sem(n) for n in ("hot_ready", "hot_free", "deg_ready", "deg_copied", "root_ready", "half_ready"))
        with nc.Block() as block:
            @block.sync
            def _(sp):
                sp.dma_start(dst[:, :], k.ins["dst_cols"]).then_inc(s_load, 16)
                sp.dma_start(k.x[:, :, :], k.ins["x_in"].rearrange("(t p) c -> p t c", p=P)).then_inc(s_x, 16)
                sp.wait_ge(s_int, 2)
                sp.dma_start(k.win_dram, ends_i[:, :, :].rearrange("i j e -> i (j e)")).then_inc(s_win, 16)
                sp.wait_ge(s_win, 16)
                sp.dma_start(k.windows[0:1, :], k.win_dram.rearrange("(a i) e -> a (i e)", a=1)).then_inc(s_win, 16)
                sp.wait_ge(s_win, 32)
                sp.wait_ge(s_x, 16)

            @block.gpsimd
            def _(pool):
                nc.gpsimd.memset(k.ident[:, :], 0.0).then_inc(s_zero, 1)
                nc.gpsimd.memset(k.ones[:, :], 1.0).then_inc(s_const, 1)
                pool.wait_ge(s_zero, 1)
                nc.gpsimd.affine_select(out=k.ident[:, :], in_=k.ident[:, :], compare_op=ALU.not_equal, fill=1.0, base=0,
                                        pattern=[[-1, P]], channel_multiplier=1).then_inc(s_const, 1)
                nc.gpsimd.iota(count_b[:, :, :], pattern=[[1, P], [0, 16]], base=0, channel_multiplier=0,
                               allow_small_or_imprecise_dtypes=True).then_inc(s_iota, 1)
                nc.gpsimd.memset(k.zero_wide[:, :], 0.0)
                nc.gpsimd.memset(k.zero_b[:, :], 0.0).then_inc(s_const, 1)
                nc.gpsimd.memset(k.half[:, :], -0.5).then_inc(s_half, 1)
                pool.wait_ge(s_degs, 1)
                pool.wait_ge(s_half, 1)
                nc.gpsimd.tensor_tensor(root[:, :], deg[:, :], k.half[:,0:1].to_broadcast([P,TILES]), ALU.pow).then_inc(s_r, 1)

            @block.vector
            def _(dve):
                dve.wait_ge(s_load, 16)
                nc.vector.tensor_copy(dst_f[:, :], dst[:, :]).then_inc(s_f, 1)
                nc.vector.tensor_scalar(part[:, 0, :], dst[:, :], P - 1, None, ALU.bitwise_and).then_inc(s_part, 1)
                nc.vector.tensor_scalar(part[:, 1, :], dst[:, :], 7, None, ALU.arith_shift_right).then_inc(s_part, 1)
                dve.wait_ge(s_f, 1)
                by_group = dst_f[:, :].rearrange("p (g k) -> p g k", k=SUB)
                nc.vector.tensor_reduce(ends[:, 0, :], by_group, AX.X, ALU.min).then_inc(s_ends, 1)
                nc.vector.tensor_reduce(ends[:, 1, :], by_group, AX.X, ALU.max).then_inc(s_ends, 1)
                dve.wait_ge(s_part, 2)
                nc.vector.tensor_copy(low[:, :], part[:, 0, :]).then_inc(s_lh, 1)
                nc.vector.tensor_copy(high[:, :], part[:, 1, :]).then_inc(s_lh, 1)
                dve.wait_ge(s_turned, 1)
                ends_ps = turned[0:GROUPS // 2, :].rearrange("i (e j p) -> i e j p", e=2, j=2)
                nc.vector.tensor_reduce(ends_t[:, :, 0], ends_ps[:, 0], AX.X, ALU.min).then_inc(s_red, 1)
                nc.vector.tensor_reduce(ends_t[:, :, 1], ends_ps[:, 1], AX.X, ALU.max).then_inc(s_red, 1)
                dve.wait_ge(s_red, 2)
                nc.vector.tensor_copy(ends_i[:, :, 0], ends_t[:, :, 0]).then_inc(s_int, 1)
                nc.vector.tensor_scalar(ends_i[:, :, 1], ends_t[:, :, 1], 1.0, None, ALU.add).then_inc(s_int, 1)
                dve.wait_ge(s_lh, 2)
                dve.wait_ge(s_iota, 1)
                with dve.Fori(0, TRIPS) as i:
                    for u in range(2):
                        cols = bass.ds(32 * i + 16 * u, 16)
                        dve.wait_ge(s_free, 2 * i + u + 1)
                        nc.vector.tensor_tensor(low_hot[u][:, :, :], count_b[:, :, :],
                                                low[:, cols].unsqueeze(1).to_broadcast([P, P, 16]), ALU.is_equal)
                        nc.vector.tensor_tensor(high_hot[u][:, :, :], count_b[:, 0:TILES, :],
                                                high[:, cols].unsqueeze(1).to_broadcast([P, TILES, 16]),
                                                ALU.is_equal).then_inc(s_hot, 1)
                dve.wait_ge(s_deg, 1)
                nc.vector.tensor_scalar(deg[:, :], deg_ps[:, 0:TILES], 1.0, None, ALU.max).then_inc(s_degs, 1)
                nc.vector.tensor_scalar(linked[:, :], deg_ps[:, 0:TILES], 0.0, None, ALU.is_gt).then_inc(s_r, 1)
                dve.wait_ge(s_r, 2)
                nc.vector.tensor_tensor(k.norm[:, :], root[:, :], linked[:, :], ALU.mult).then_inc(s_r, 1)

            @block.tensor
            def _(pe):
                pe.sem_inc(s_free, 2)
                pe.wait_ge(s_const, 3)
                pe.wait_ge(s_ends, 2)
                for e in range(2):
                    for j in range(2):
                        last = nc.tensor.transpose(turned[0:GROUPS // 2, P * (2 * e + j):P * (2 * e + j + 1)],
                                                   ends[:, e, j::2], k.ident[:, :])
                last.then_inc(s_turned, 1)
                nc.tensor.matmul(deg_ps[:, 0:TILES], k.zero_b[:, :], k.zero_b[:, 0:TILES], start=True, stop=False, skip_group_check=True)
                with pe.Fori(0, TRIPS) as i:
                    for u in range(2):
                        pe.wait_ge(s_hot, 2 * i + u + 1)
                        for m in range(16):
                            last = nc.tensor.matmul(deg_ps[:, 0:TILES], low_hot[u][:, :, m], high_hot[u][:, :, m],
                                                    start=False, stop=False, skip_group_check=True)
                        last.then_inc(s_free, 1)
                nc.tensor.matmul(deg_ps[:, 0:TILES], k.zero_b[:, :], k.zero_b[:, 0:TILES], start=False, stop=True,
                                 skip_group_check=True).then_inc(s_deg, 1)


def edge_stage(nc, k, name, weighted, turn):
    gathered = turn * 256 * TRIPS
    with stage(nc) as (sb, pb, sem):
        edge = [sb(f"{name}_edge{b}", [P, 3, 16], I32) for b in range(2)]
        dest = [sb(f"{name}_dest{b}", [P, 16]) for b in range(2)]
        rows = sb(f"{name}_rows", [P, 2, SUB, C])
        hot = sb(f"{name}_hot", [P, 2, SUB, WINDOW])
        total = [pb(f"{name}_total{j}") for j in range(2)]
        s_edge = [sem(f"{name}_edges_loaded{b}") for b in range(2)]
        s_free = [sem(f"{name}_slots_free{j}") for j in range(2)]
        s_turn, s_dest, s_hot, s_total, s_added = (sem(f"{name}_{n}") for n in ("gather_turn", "dest_float", "hot_ready", "total_ready", "total_added"))
        with nc.Block() as block:
            @block.sync
            def _(sp):
                with sp.Fori(0, TRIPS) as i:
                    for b in range(2):
                        for j in range(2):
                            sp.wait_ge(s_free[j], 2 * i + b + 1)
                        sp.dma_start(edge[b][:, :, :],
                                     k.ins["edges"][bass.ds(2 * i + b, 1), :, :, :].rearrange("a p f m -> (a p) f m")).then_inc(s_edge[b], 16)

            @block.gpsimd
            def _(pool):
                with pool.Fori(0, TRIPS) as i:
                    for b in range(2):
                        pool.wait_ge(s_edge[b], 16 * i + 16)
                        for j in range(2):
                            pool.wait_ge(s_free[j], 2 * i + b + 2)
                            pool.sem_inc(s_turn, 1)
                            for m in range(SUB):
                                nc.gpsimd.indirect_dma_start(
                                    out=rows[:, j, m, :], out_offset=None, in_=k.table,
                                    in_offset=bass.IndirectOffsetOnAxis(ap=edge[b][:, 0, SUB * j + m:SUB * j + m + 1], axis=0),
                                ).then_inc(k.s_rows[j], 16)

            @block.vector
            def _(dve):
                dve.sem_inc(s_total, 1)
                nc.vector.memset(total[1][:, 0:KC * WINDOW], 0.0)
                nc.vector.memset(k.sums_t[:, :, :], 0.0).then_inc(s_added, 1)
                visit = dve.alloc_register(f"{name}_dve_visit")
                before = dve.alloc_register(f"{name}_dve_before")
                dve.reg_mov(visit, 1)
                dve.reg_mov(before, 0)

                def build(b, j, w):
                    for m in range(SUB):
                        at_m = slice(SUB * j + m, SUB * j + m + 1)
                        weight = edge[b][:, 2, at_m].bitcast(F32) if weighted else 1.0
                        last = nc.vector.tensor_scalar(hot[:, j, m, :], k.node_id[:, bass.ds(w, WINDOW)], dest[b][:, at_m], weight,
                                                       ALU.is_equal, ALU.mult)
                    last.then_inc(s_hot, 1)

                def add(j, v):
                    window = dve.snap(before, min_val=0, max_val=PADDED - 1)
                    dve.wait_ge(s_total, v)
                    dve.wait_ge(s_added, v)
                    out = k.sums_t[:, :, bass.ds(window, WINDOW)]
                    nc.vector.tensor_tensor(out, out, total[j][:, 0:KC * WINDOW].rearrange("p (a n) -> p a n", a=KC), ALU.add).then_inc(s_added, 1)

                with dve.Fori(0, TRIPS) as i:
                    for b in range(2):
                        dve.wait_ge(s_edge[b], 16 * i + 16)
                        nc.vector.tensor_copy(dest[b][:, :], edge[b][:, 1, :]).then_inc(s_dest, 1)
                        for j in range(2):
                            first = dve.value_load(k.windows[0:1, bass.ds(8 * i + 4 * b + 2 * j, 1)], min_val=0, max_val=PADDED - 1)
                            end = dve.value_load(k.windows[0:1, bass.ds(8 * i + 4 * b + 2 * j + 1, 1)], min_val=1, max_val=PADDED)
                            v = dve.snap(visit, min_val=1, max_val=1 << 20)
                            if j == 0:
                                dve.wait_ge(s_dest, 2 * i + b + 1)
                            build(b, j, first)
                            add(1 - j, v)
                            dve.reg_mov(before, first)
                            dve.reg_add(visit, visit, 1)
                            with dve.If(end > first + WINDOW):
                                with dve.Fori(first + WINDOW, end, WINDOW) as w:
                                    v = dve.snap(visit, min_val=1, max_val=1 << 20)
                                    add(j, v)
                                    build(b, j, w)
                                    dve.reg_mov(before, w)
                                    dve.reg_add(visit, visit, 1)
                add(1, dve.snap(visit, min_val=1, max_val=1 << 20))

            @block.tensor
            def _(pe):
                for j in range(2):
                    pe.sem_inc(s_free[j], 2)
                visit = pe.alloc_register(f"{name}_pe_visit")
                pe.reg_mov(visit, 1)

                def multiply(j):
                    for a in range(KC):
                        for m in range(SUB):
                            last = nc.tensor.matmul(total[j][:, a * WINDOW:(a + 1) * WINDOW], rows[:, j, m, a * P:(a + 1) * P], hot[:, j, m, :],
                                                    start=(m == 0), stop=(m == SUB - 1))
                    last.then_inc(s_total, 1)

                with pe.Fori(0, TRIPS) as i:
                    for b in range(2):
                        for j in range(2):
                            first = pe.value_load(k.windows[0:1, bass.ds(8 * i + 4 * b + 2 * j, 1)], min_val=0, max_val=PADDED - 1)
                            end = pe.value_load(k.windows[0:1, bass.ds(8 * i + 4 * b + 2 * j + 1, 1)], min_val=1, max_val=PADDED)
                            v = pe.snap(visit, min_val=1, max_val=1 << 20)
                            pe.wait_ge(s_hot, v)
                            pe.wait_ge(k.s_rows[j], gathered + 256 * i + 128 * b + 128)
                            multiply(j)
                            pe.reg_add(visit, visit, 1)
                            with pe.If(end > first + WINDOW):
                                with pe.Fori(first + WINDOW, end, WINDOW) as w:
                                    v = pe.snap(visit, min_val=1, max_val=1 << 20)
                                    pe.wait_ge(s_hot, v)
                                    multiply(j)
                                    pe.reg_add(visit, visit, 1)
                            pe.wait_ge(s_total, pe.snap(visit, min_val=1, max_val=1 << 20))
                            pe.sem_inc(s_free[j], 1)


def residents(nc, k, ctx):
    sb = lambda name, shape, dt=F32: ctx.enter_context(nc.sbuf_tensor(name, shape, dt))
    k.carried = ctx.enter_context(nc.semaphore("carried_waits"))
    k.s_rows = [ctx.enter_context(nc.semaphore(f"rows_gathered{j}")) for j in range(2)]
    k.x = sb("x", [P, TILES, C])
    k.windows = sb("windows", [1, 2 * GROUPS], I32)
    k.norm = sb("norm", [P, TILES])
    k.ident = sb("ident", [P, P])
    k.ones = sb("ones", [P, P])
    k.half = sb("half", [P, 1])
    k.zero_b = sb("zero_b", [P, P], BF16)
    k.zero_wide = sb("zero_wide", [P, 512], BF16)
    k.raw = sb("raw", [P, TILES, 6])
    k.mean = sb("mean", [P, TILES])
    k.moment = sb("moment", [P, 2, TILES])
    k.rstd = sb("rstd", [P, TILES])
    k.key_sum = sb("key_sum", [P, C])
    k.mix0 = sb("mix0", [P, KC, C])
    k.slices = sb("slices", [P, 4, C])
    k.bn_scale = sb("bn_scale", [P, KC])
    k.bn_shift = sb("bn_shift", [P, KC])
    k.gate = sb("gate", [P, TILES, 2])
    k.slot = sb("slot", [P, TILES, 2], I32)
    k.expert_of = sb("expert_of", [P, SLOT_TILES], I32)
    k.s_scattered = [ctx.enter_context(nc.semaphore(f"rows_scattered{u}")) for u in range(2)]
    k.s_returned = [ctx.enter_context(nc.semaphore(f"rows_returned{u}")) for u in range(2)]
    k.s_stored = [ctx.enter_context(nc.semaphore(f"expert_rows_stored{u}")) for u in range(2)]
    k.mix1 = sb("mix1", [P, KC, C])


def wide_residents(nc, k, ctx):
    k.wide = wide = ctx.enter_context(nc.sbuf_tensor("wide", [P, TILES * 2 * C + KC * WINDOW], F32))
    n = KC * (PADDED + WINDOW)
    k.sums_t = wide[:, 0:n].rearrange("p (a n) -> p a n", a=KC)
    k.rows = wide[:, n:n + TILES * C].rearrange("p (t c) -> p t c", c=C)
    k.soft = wide[:, 0:TILES * 2 * C].rearrange("p (t c) -> p t c", c=2 * C)


def graph_residents(nc, k, ctx):
    k.node_id = ctx.enter_context(nc.sbuf_tensor("node_id", [P, PADDED + WINDOW], I16))


def row_stats(nc, k, t):
    return nc.vector.bn_stats(at(k.raw, t), at(k.x, t))


def row_moments(nc, dve, k, s_step):
    done = [0]

    def step(instruction):
        instruction.then_inc(s_step, 1)
        done[0] += 1
        dve.wait_ge(s_step, done[0])

    step(nc.vector.tensor_tensor(k.moment[:, 0, :], k.raw[:, :, 1], k.raw[:, :, 4], ALU.add))
    step(nc.vector.tensor_scalar(k.mean[:, :], k.moment[:, 0, :], 0.5, None, ALU.mult))
    step(nc.vector.tensor_tensor(k.moment[:, 0, :], k.raw[:, :, 1], k.mean[:, :], ALU.subtract))
    step(nc.vector.tensor_tensor(k.moment[:, 0, :], k.moment[:, 0, :], k.moment[:, 0, :], ALU.mult))
    step(nc.vector.tensor_tensor(k.moment[:, 1, :], k.raw[:, :, 2], k.raw[:, :, 5], ALU.add))
    step(nc.vector.scalar_tensor_tensor(k.moment[:, 1, :], k.moment[:, 1, :], 1.0 / C, k.moment[:, 0, :], ALU.mult, ALU.add))
    step(nc.vector.tensor_scalar(k.moment[:, 0, :], k.moment[:, 1, :], EPS, None, ALU.add))


MOMENTS = 7


def row_scale(nc, pool, k, s_step, s_rstd):
    pool.wait_ge(s_step, MOMENTS)
    nc.gpsimd.tensor_tensor(k.rstd[:, :], k.moment[:, 0, :], k.half[:, 0:1].to_broadcast([P, TILES]), ALU.pow).then_inc(s_rstd, 1)


def normalise(nc, k, out, t):
    return nc.vector.tensor_scalar(out, at(k.x, t), col(k.mean, t), col(k.rstd, t), ALU.subtract, ALU.mult)


def first_stats_stage(nc, k):
    with stage(nc) as (sb, pb, sem):
        s_stats, s_step, s_rstd = (sem(f"in_{n}") for n in ("stats", "moment_steps", "rstd"))
        with nc.Block() as block:
            @block.vector
            def _(dve):
                with dve.Fori(0, TILES) as t:
                    row_stats(nc, k, t).then_inc(s_stats, 1)
                dve.wait_ge(s_stats, TILES)
                row_moments(nc, dve, k, s_step)

            @block.gpsimd
            def _(pool):
                nc.gpsimd.iota(k.node_id[:, :], pattern=[[1, PADDED + WINDOW]], base=0, channel_multiplier=0,
                               allow_small_or_imprecise_dtypes=True)
                row_scale(nc, pool, k, s_step, s_rstd)


def keys_stage(nc, k):
    with stage(nc) as (sb, pb, sem):
        w = sb("ky_w", [P, KC, 2 * C])
        w_proj = sb("ky_wproj", [P, KC, C])
        xn = [sb(f"ky_xn{u}", [P, C]) for u in range(2)]
        xt = [sb(f"ky_xt{u}", [P, KC, P]) for u in range(2)]
        row = [sb(f"ky_row{u}", [P, C]) for u in range(2)]
        neg = [sb(f"ky_neg{u}", [P, C]) for u in range(2)]
        exp = [sb(f"ky_exp{u}", [P, C]) for u in range(2)]
        key = [sb(f"ky_key{u}", [P, C]) for u in range(2)]
        val = [sb(f"ky_val{u}", [P, C]) for u in range(2)]
        blocks = sb("ky_blocks", [P, P])
        ctx_t = sb("ky_ctx_t", [P, KC, P])
        turned = [pb(f"ky_turned{u}") for u in range(2)]
        kv = [pb(f"ky_kv{u}") for u in range(2)]
        context = pb("ky_context")
        keysum = pb("ky_keysum")
        proj = pb("ky_proj")
        s_stored = [sem(f"ky_table_stored{u}") for u in range(2)]
        s_w, s_done, s_ctx, s_m = (sem(f"ky_{n}") for n in ("weights_loaded", "context_ready", "context_masked", "mix_ready"))
        s_xn, s_kept, s_turned, s_xt, s_row, s_kv, s_neg, s_exp, s_val, s_key, s_sum = (sem(f"ky_{n}") for n in (
            "rows_ready", "rows_kept", "rows_turned", "turned_copied", "table_row", "kv_ready", "negative_ready",
            "exp_ready", "value_copied", "key_ready", "context_added"))
        with nc.Block() as block:
            @block.sync
            def _(sp):
                sp.dma_start(w[:, :, :], k.ins["L0_mix_WkvT"].rearrange("(k p) n -> p k n", p=P)).then_inc(s_w, 16)
                sp.dma_start(w_proj[:, :, :], k.ins["L0_mix_WprojT"].rearrange("(k p) n -> p k n", p=P)).then_inc(s_w, 16)
                sp.dma_start(blocks[:, :], k.ins["blocks32"]).then_inc(s_w, 16)
                for u in range(2):
                    sp.sem_inc(s_stored[u], 16)

                def head(t, u, i):
                    ready(sp, s_row, t)
                    sp.dma_start(table_rows(k, t), row[u][:, :]).then_inc(s_stored[u], 16)

                pipelined(sp, head, no_tail)
                sp.wait_ge(s_stored[0], 16 + 16 * (TILES // 2 + 1))
                sp.wait_ge(s_stored[1], 16 + 16 * (TILES // 2))

            @block.gpsimd
            def _(pool):
                start_at_two(pool, s_kept)

                def head(t, u, i):
                    ready(pool, s_xn, t)
                    nc.gpsimd.tensor_copy(at(k.rows, t), xn[u][:, :]).then_inc(s_kept, 1)

                pipelined(pool, head, no_tail)

            @block.vector
            def _(dve):
                start_at_two(dve, s_xn, s_neg, s_key)

                def head(t, u, i):
                    free(dve, s_turned, t)
                    free(dve, s_row, t)
                    free(dve, s_kept, t)
                    normalise(nc, k, xn[u][:, :], t).then_inc(s_xn, 1)

                def negative(t, u, rows):
                    ready(dve, s_kv, t)
                    free(dve, s_exp, t)
                    nc.vector.tensor_scalar(neg[u][:, :], kv[u][:, 0:C], 0.0, None, ALU.min).then_inc(s_neg, 1)

                def tail(t, u, rows):
                    ready(dve, s_exp, t)
                    ready(dve, s_val, t)
                    free(dve, s_sum, t)
                    nc.vector.scalar_tensor_tensor(key[u][:, :], kv[u][:, 0:C], 0.0, exp[u][:, :], ALU.max, ALU.add).then_inc(s_key, 1)

                pipelined(dve, no_head, tail, ahead=2, middle=negative, late=head)
                dve.wait_ge(s_done, 1)
                dve.wait_ge(s_w, 48)
                for a in range(KC):
                    nc.vector.tensor_tensor(ctx_t[:, a, :], context[:, a * P:(a + 1) * P], blocks[:, :], ALU.mult).then_inc(s_ctx, 1)
                nc.vector.tensor_copy(k.key_sum[:, :], keysum[:, 0:C])
                dve.wait_ge(s_m, 1)
                nc.vector.tensor_copy(k.mix0[:, :, :].rearrange("p k n -> p (k n)"), proj[:, :])

            @block.scalar
            def _(act):
                start_at_two(act, s_xt, s_row, s_exp, s_val)

                def head(t, u, i):
                    ready(act, s_turned, t)
                    free(act, s_kv, t)
                    nc.scalar.activation(xt[u][:, :, :].rearrange("p k n -> p (k n)"), turned[u][:, 0:C], ACT.Copy).then_inc(s_xt, 1)
                    ready(act, s_xn, t)
                    act.wait_ge(s_stored[u], 16 * i + 16)
                    nc.scalar.activation(row[u][:, :], xn[u][:, :], ACT.Copy, scale=col(k.norm, t)).then_inc(s_row, 1)

                def tail(t, u, rows):
                    ready(act, s_neg, t)
                    free(act, s_sum, t)
                    nc.scalar.activation(val[u][:, :], kv[u][:, C:2 * C], ACT.Copy).then_inc(s_val, 1)
                    free(act, s_key, t)
                    nc.scalar.activation(exp[u][:, :], neg[u][:, :], ACT.Exp).then_inc(s_exp, 1)

                pipelined(act, no_head, no_tail, ahead=2, middle=tail, late=head)

            @block.tensor
            def _(pe):
                start_at_two(pe, s_turned, s_kv, s_sum)
                for bank in (context, keysum):
                    nc.tensor.matmul(bank[:, 0:C], k.zero_b[:, :], k.zero_wide[:, 0:C], start=True, stop=False, skip_group_check=True)
                pe.wait_ge(s_w, 48)

                def head(t, u, i):
                    ready(pe, s_xn, t)
                    free(pe, s_xt, t)
                    for a in range(KC):
                        last = nc.tensor.transpose(turned[u][:, a * P:(a + 1) * P], xn[u][:, a * P:(a + 1) * P], k.ident[:, :])
                    last.then_inc(s_turned, 1)

                def keys_values(t, u, i):
                    ready(pe, s_xt, t)
                    free(pe, s_key, t)
                    free(pe, s_val, t)
                    for a in range(KC):
                        last = nc.tensor.matmul(kv[u][:, :], xt[u][:, a, :], w[:, a, :], start=(a == 0), stop=(a == KC - 1))
                    last.then_inc(s_kv, 1)

                def products(t, u, rows):
                    ready(pe, s_key, t)
                    ready(pe, s_val, t)
                    stop = rows == LAST
                    nc.tensor.matmul(keysum[:, 0:C], k.ones[0:rows, :], key[u][0:rows, :], start=False, stop=stop, skip_group_check=True)
                    for a in range(KC):
                        half = slice(a * P, (a + 1) * P)
                        last = nc.tensor.matmul(context[:, half], val[u][0:rows, half], key[u][0:rows, half], start=False, stop=stop,
                                                skip_group_check=True)
                    last.then_inc(s_sum, 1)

                pipelined(pe, head, no_tail, ahead=2, middle=products, late=keys_values)
                ready(pe, s_sum, TILES - 1)
                pe.sem_inc(s_done, 1)
                pe.wait_ge(s_ctx, KC)
                for a in range(KC):
                    last = nc.tensor.matmul(proj[:, a * C:(a + 1) * C], ctx_t[:, a, :], w_proj[:, a, :], start=True, stop=True)
                last.then_inc(s_m, 1)


def first_update_stage(nc, k):
    with stage(nc) as (sb, pb, sem):
        wq = sb("fu_wq", [P, KC, C])
        wg = sb("fu_wg", [P, KC, C])
        bias = sb("fu_bias", [P, C])
        rows_in = [sb(f"fu_rows{u}", [P, C]) for u in range(2)]
        rows_t = [sb(f"fu_rows_t{u}", [P, KC, P]) for u in range(2)]
        agg_t = [sb(f"fu_sums_t{u}", [P, KC, P]) for u in range(2)]
        neg = [sb(f"fu_neg{u}", [P, C]) for u in range(2)]
        exp = [sb(f"fu_exp{u}", [P, C]) for u in range(2)]
        phi = [sb(f"fu_phi{u}", [P, C]) for u in range(2)]
        prod = [sb(f"fu_prod{u}", [P, C]) for u in range(2)]
        den = [sb(f"fu_den{u}", [P, 3, HEADS0]) for u in range(2)]
        qn = [sb(f"fu_qn{u}", [P, C]) for u in range(2)]
        qn_t = [sb(f"fu_qn_t{u}", [P, KC, P]) for u in range(2)]
        attended = [sb(f"fu_attended{u}", [P, C]) for u in range(2)]
        turned = [pb(f"fu_turned{u}") for u in range(2)]
        query = [pb(f"fu_query{u}") for u in range(2)]
        q_turned = [pb(f"fu_q_turned{u}") for u in range(2)]
        out = [pb(f"fu_out{u}") for u in range(2)]
        s_w = sem("fu_weights_loaded")
        s_turned, s_rows_t, s_agg, s_q, s_neg, s_exp, s_phi, s_prod, s_sum, s_max, s_den, s_qn, s_qt, s_qnt, s_out, s_add, s_x, s_stats = (
            sem(f"fu_{n}") for n in ("rows_turned", "turned_copied", "sums_copied", "query_ready", "negative_ready", "exp_ready", "phi_ready",
                                     "product_ready", "denominator_summed", "denominator_guarded", "denominator_inverted", "query_scaled",
                                     "query_turned", "query_copied", "out_ready", "out_added", "x_updated", "stats_ready"))
        s_step, s_rstd, s_rows, s_att = (sem(f"fu_{n}") for n in ("moment_steps", "rstd", "rows_copied", "attention_biased"))
        with nc.Block() as block:
            @block.sync
            def _(sp):
                sp.dma_start(wq[:, :, :], k.ins["L0_mix_WqT"].rearrange("(k p) n -> p k n", p=P)).then_inc(s_w, 16)
                sp.dma_start(wg[:, :, :], k.ins["L0_gnn_W"].rearrange("(k p) n -> p k n", p=P)).then_inc(s_w, 16)
                sp.dma_start(bias[:, :], k.ins["L0_mix_bproj"].partition_broadcast(P)).then_inc(s_w, 16)

            @block.gpsimd
            def _(pool):
                start_at_two(pool, s_rows)

                def head(t, u, i):
                    free(pool, s_turned, t)
                    nc.gpsimd.tensor_copy(rows_in[u][:, :], at(k.rows, t)).then_inc(s_rows, 1)

                pipelined(pool, head, no_tail)
                row_scale(nc, pool, k, s_step, s_rstd)

            @block.vector
            def _(dve):
                start_at_two(dve, s_neg, s_phi, s_prod, s_sum, s_max, s_den, s_qn, s_att, s_add, s_x, s_stats)
                dve.wait_ge(s_w, 48)

                def head(t, u, i):
                    ready(dve, s_q, t)
                    free(dve, s_exp, t)
                    nc.vector.tensor_scalar(neg[u][:, :], query[u][:, 0:C], 0.0, None, ALU.min).then_inc(s_neg, 1)

                def rest(t, u, i):
                    ready(dve, s_exp, t)
                    free(dve, s_qn, t)
                    nc.vector.scalar_tensor_tensor(phi[u][:, :], query[u][:, 0:C], 0.0, exp[u][:, :], ALU.max, ALU.add).then_inc(s_phi, 1)
                    ready(dve, s_phi, t)
                    nc.vector.tensor_tensor(prod[u][:, :], phi[u][:, :], k.key_sum[:, :], ALU.mult).then_inc(s_prod, 1)
                    ready(dve, s_prod, t)
                    nc.vector.tensor_reduce(den[u][:, 0, :], prod[u][:, :].rearrange("p (h d) -> p h d", h=HEADS0), AX.X, ALU.add).then_inc(s_sum, 1)
                    ready(dve, s_sum, t)
                    nc.vector.tensor_scalar(den[u][:, 1, :], den[u][:, 0, :], 1e-6, None, ALU.max).then_inc(s_max, 1)
                    ready(dve, s_max, t)
                    nc.vector.reciprocal(den[u][:, 2, :], den[u][:, 1, :]).then_inc(s_den, 1)
                    ready(dve, s_den, t)
                    free(dve, s_qt, t)
                    nc.vector.tensor_tensor(qn[u][:, :].rearrange("p (h d) -> p h d", h=HEADS0),
                                            phi[u][:, :].rearrange("p (h d) -> p h d", h=HEADS0),
                                            den[u][:, 2, :].unsqueeze(2).to_broadcast([P, HEADS0, HD0]), ALU.mult).then_inc(s_qn, 1)

                def update(t, u, rows):
                    ready(dve, s_out, t)
                    nc.vector.tensor_tensor(attended[u][:, :], out[u][:, 0:C], bias[:, :], ALU.add).then_inc(s_att, 1)
                    carry(dve, k)
                    nc.vector.scalar_tensor_tensor(at(k.x, t), out[u][:, C:2 * C], col(k.norm, t), at(k.x, t), ALU.mult, ALU.add).then_inc(s_add, 1)
                    ready(dve, s_att, t)
                    ready(dve, s_add, t)
                    nc.vector.tensor_tensor(at(k.x, t), at(k.x, t), attended[u][:, :], ALU.add).then_inc(s_x, 1)
                    ready(dve, s_x, t)
                    carry(dve, k)
                    row_stats(nc, k, t).then_inc(s_stats, 1)

                pipelined(dve, head, no_tail, ahead=2, middle=update, late=rest)
                ready(dve, s_stats, TILES - 1)
                row_moments(nc, dve, k, s_step)

            @block.scalar
            def _(act):
                start_at_two(act, s_agg, s_rows_t, s_exp, s_qnt)

                def head(t, u, i):
                    ready(act, s_turned, t)
                    free(act, s_q, t)
                    nc.scalar.activation(rows_t[u][:, :, :].rearrange("p k n -> p (k n)"), turned[u][:, 0:C], ACT.Copy).then_inc(s_rows_t, 1)

                def sums_and_exp(t, u, i):
                    free(act, s_out, t)
                    nc.scalar.activation(agg_t[u][:, :, :], nodes(k, t), ACT.Copy).then_inc(s_agg, 1)
                    ready(act, s_neg, t)
                    nc.scalar.activation(exp[u][:, :], neg[u][:, :], ACT.Exp).then_inc(s_exp, 1)

                def copy_queries(t, u, rows):
                    ready(act, s_qt, t)
                    free(act, s_out, t)
                    nc.scalar.activation(qn_t[u][:, :, :].rearrange("p k n -> p (k n)"), q_turned[u][:, 0:C], ACT.Copy).then_inc(s_qnt, 1)

                pipelined(act, head, no_tail, ahead=2, middle=copy_queries, late=sums_and_exp)

            @block.tensor
            def _(pe):
                start_at_two(pe, s_turned, s_q, s_qt, s_out)
                pe.wait_ge(s_w, 48)

                def head(t, u, i):
                    ready(pe, s_rows, t)
                    free(pe, s_rows_t, t)
                    for a in range(KC):
                        last = nc.tensor.transpose(turned[u][:, a * P:(a + 1) * P], rows_in[u][:, a * P:(a + 1) * P], k.ident[:, :])
                    last.then_inc(s_turned, 1)

                def queries(t, u, i):
                    ready(pe, s_rows_t, t)
                    free(pe, s_phi, t)
                    for a in range(KC):
                        last = nc.tensor.matmul(query[u][:, 0:C], rows_t[u][:, a, :], wq[:, a, :], start=(a == 0), stop=(a == KC - 1))
                    last.then_inc(s_q, 1)

                def products(t, u, rows):
                    ready(pe, s_qn, t)
                    free(pe, s_qnt, t)
                    for a in range(KC):
                        last = nc.tensor.transpose(q_turned[u][:, a * P:(a + 1) * P], qn[u][:, a * P:(a + 1) * P], k.ident[:, :])
                    last.then_inc(s_qt, 1)
                    free(pe, s_add, t)
                    ready(pe, s_agg, t)
                    for a in range(KC):
                        nc.tensor.matmul(out[u][:, C:2 * C], agg_t[u][:, a, :], wg[:, a, :], start=(a == 0), stop=(a == KC - 1))
                    ready(pe, s_qnt, t)
                    for a in range(KC):
                        last = nc.tensor.matmul(out[u][:, 0:C], qn_t[u][:, a, :], k.mix0[:, a, :], start=(a == 0), stop=(a == KC - 1))
                    last.then_inc(s_out, 1)

                pipelined(pe, head, no_tail, ahead=2, middle=products, late=queries)


def slice_weights_stage(nc, k):
    with stage(nc) as (sb, pb, sem):
        wx_t = sb("sl_wx_t", [P, 4, C])
        pair = sb("sl_pair", [P, P])
        bx = sb("sl_bx", [P, 4])
        bx_wide = sb("sl_bx_wide", [P, 4, P])
        b_slice = sb("sl_b", [P, 2 * C])
        temp = sb("sl_temp", [P, SH])
        clipped = sb("sl_clipped", [P, SH])
        inv = sb("sl_inv", [P, SH])
        summed = sb("sl_summed", [P, 2 * C])
        mats = [pb(f"sl_mat{a}") for a in range(KC)]
        row = pb("sl_row")
        s_w, s_clip, s_inv, s_wide, s_mat, s_b = (sem(f"sl_{n}") for n in ("loaded", "clipped", "inverted", "bias_wide", "products", "bias_summed"))
        with nc.Block() as block:
            @block.sync
            def _(sp):
                sp.dma_start(wx_t[:, :, :], k.ins["L0_ffn_W_xT"].rearrange("(q p) c -> p q c", p=P)).then_inc(s_w, 16)
                sp.dma_start(pair[:, :], k.ins["pair_slice"]).then_inc(s_w, 16)
                sp.dma_start(bx[:, :], k.ins["L0_ffn_b_x4"]).then_inc(s_w, 16)
                sp.dma_start(b_slice[:, :], k.ins["b_slice8"].partition_broadcast(P)).then_inc(s_w, 16)
                sp.dma_start(temp[:, :], k.ins["temperature"].partition_broadcast(P)).then_inc(s_w, 16)

            @block.vector
            def _(dve):
                dve.wait_ge(s_w, 80)
                nc.vector.tensor_scalar(clipped[:, :], temp[:, :], 0.1, 5.0, ALU.max, ALU.min).then_inc(s_clip, 1)
                for q in range(4):
                    last = nc.vector.tensor_scalar(bx_wide[:, q, :], k.ones[:, :], bx[:, q:q + 1], None, ALU.mult)
                last.then_inc(s_wide, 1)
                dve.wait_ge(s_clip, 1)
                nc.vector.reciprocal(inv[:, :], clipped[:, :]).then_inc(s_inv, 1)
                dve.wait_ge(s_mat, 1)
                dve.wait_ge(s_inv, 1)
                inv_wide = inv[:, :].unsqueeze(2).to_broadcast([P, SH, SLICES])
                for a in range(KC):
                    nc.vector.tensor_tensor(k.w_slice[:, a, :].rearrange("p (h g) -> p h g", h=SH),
                                            mats[a][:, :].rearrange("p (h g) -> p h g", h=SH), inv_wide, ALU.mult)
                nc.vector.tensor_tensor(summed[:, :], row[:, :], b_slice[:, :], ALU.add).then_inc(s_b, 1)
                dve.wait_ge(s_b, 1)
                nc.vector.tensor_tensor(k.b_slice[:, :].rearrange("p (h g) -> p h g", h=SH),
                                        summed[:, :].rearrange("p (h g) -> p h g", h=SH), inv_wide, ALU.mult)

            @block.tensor
            def _(pe):
                pe.wait_ge(s_w, 80)
                pe.wait_ge(s_wide, 1)
                for q in range(4):
                    cols = slice(q * P, (q + 1) * P)
                    for a in range(KC):
                        nc.tensor.matmul(mats[a][:, cols], wx_t[:, q, a * P:(a + 1) * P], pair[:, :], start=True, stop=True)
                    last = nc.tensor.matmul(row[:, cols], bx_wide[:, q, :], pair[:, :], start=True, stop=True)
                last.then_inc(s_mat, 1)


def slices_stage(nc, k, token, logits):
    with stage(nc) as (sb, pb, sem):
        xn = [sb(f"sw_xn{u}", [P, C]) for u in range(2)]
        xk = [sb(f"sw_xk{u}", [P, C + 1]) for u in range(2)]
        xt = [sb(f"sw_xt{u}", [P, KC, P]) for u in range(2)]
        logit = [sb(f"sw_logit{u}", [P, 2 * C]) for u in range(2)]
        top = [sb(f"sw_top{u}", [P, SH]) for u in range(2)]
        exp = [sb(f"sw_exp{u}", [P, 2 * C]) for u in range(2)]
        den = [sb(f"sw_den{u}", [P, 2, SH]) for u in range(2)]
        soft = [sb(f"sw_soft{u}", [P, 2 * C]) for u in range(2)]
        turned = [pb(f"sw_turned{u}") for u in range(2)]
        s_one, s_xn, s_turned, s_xt, s_lg, s_biased, s_top, s_off, s_exp, s_sum, s_inv, s_soft, s_kept, s_tok, s_xk = (sem(f"sw_{n}") for n in (
            "ones_set", "rows_ready", "rows_turned", "turned_copied", "logits_ready", "bias_added", "maximum_ready", "maximum_subtracted",
            "exp_ready", "exp_summed", "sum_inverted", "softmax_ready", "softmax_kept", "tokens_added", "rows_copied"))
        by_head = lambda ap: ap.rearrange("p (h g) -> p h g", h=SH)
        wide = lambda ap: ap.unsqueeze(2).to_broadcast([P, SH, SLICES])
        with nc.Block() as block:
            @block.gpsimd
            def _(pool):
                start_at_two(pool, s_kept)

                def head(t, u, i):
                    pass

                def tail(t, u, rows):
                    ready(pool, s_soft, t)
                    nc.gpsimd.tensor_copy(at(k.soft, t), soft[u][:, :]).then_inc(s_kept, 1)

                pipelined(pool, head, tail)

            @block.vector
            def _(dve):
                start_at_two(dve, s_xn, s_biased, s_top, s_off, s_sum, s_inv, s_soft)
                for u in range(2):
                    nc.vector.memset(xk[u][:, C:C + 1], 1.0).then_inc(s_one, 1)

                def head(t, u, i):
                    free(dve, s_turned, t)
                    free(dve, s_xk, t)
                    normalise(nc, k, xn[u][:, :], t).then_inc(s_xn, 1)

                def logits_less_maximum(t, u, rows):
                    ready(dve, s_lg, t)
                    free(dve, s_off, t)
                    nc.vector.tensor_tensor(logit[u][:, :], logits[u][:, :], k.b_slice[:, :], ALU.add).then_inc(s_biased, 1)
                    ready(dve, s_biased, t)
                    nc.vector.tensor_reduce(top[u][:, :], by_head(logit[u][:, :]), AX.X, ALU.max).then_inc(s_top, 1)
                    ready(dve, s_top, t)
                    free(dve, s_soft, t)
                    nc.vector.tensor_tensor(by_head(logit[u][:, :]), by_head(logit[u][:, :]), wide(top[u][:, :]), ALU.subtract).then_inc(s_off, 1)

                def tail(t, u, rows):
                    ready(dve, s_exp, t)
                    nc.vector.tensor_reduce(den[u][:, 0, :], by_head(exp[u][:, :]), AX.X, ALU.add).then_inc(s_sum, 1)
                    ready(dve, s_sum, t)
                    nc.vector.reciprocal(den[u][:, 1, :], den[u][:, 0, :]).then_inc(s_inv, 1)
                    ready(dve, s_inv, t)
                    free(dve, s_tok, t)
                    free(dve, s_kept, t)
                    nc.vector.tensor_tensor(by_head(soft[u][:, :]), by_head(exp[u][:, :]), wide(den[u][:, 1, :]), ALU.mult).then_inc(s_soft, 1)

                pipelined(dve, no_head, tail, ahead=2, middle=logits_less_maximum, late=head)

            @block.scalar
            def _(act):
                start_at_two(act, s_xt, s_exp, s_xk)

                def head(t, u, i):
                    ready(act, s_turned, t)
                    free(act, s_lg, t)
                    nc.scalar.activation(xt[u][:, :, :].rearrange("p k n -> p (k n)"), turned[u][:, 0:C], ACT.Copy).then_inc(s_xt, 1)

                def copy_rows(t, u, i):
                    head(t, u, i)
                    ready(act, s_xn, t)
                    free(act, s_tok, t)
                    nc.scalar.activation(xk[u][:, 0:C], xn[u][:, :], ACT.Copy).then_inc(s_xk, 1)

                def exponentials(t, u, rows):
                    ready(act, s_off, t)
                    free(act, s_soft, t)
                    nc.scalar.activation(exp[u][:, :], logit[u][:, :], ACT.Exp).then_inc(s_exp, 1)

                pipelined(act, no_head, no_tail, ahead=2, middle=exponentials, late=copy_rows)

            @block.tensor
            def _(pe):
                start_at_two(pe, s_turned, s_lg, s_tok)
                for q in range(4):
                    nc.tensor.matmul(token[q][:, 0:C + 1], k.zero_b[:, :], k.zero_wide[:, 0:C + 1], start=True, stop=False, skip_group_check=True)

                def head(t, u, i):
                    ready(pe, s_xn, t)
                    free(pe, s_xt, t)
                    for a in range(KC):
                        last = nc.tensor.transpose(turned[u][:, a * P:(a + 1) * P], xn[u][:, a * P:(a + 1) * P], k.ident[:, :])
                    last.then_inc(s_turned, 1)

                def logit_products(t, u, i):
                    ready(pe, s_xt, t)
                    free(pe, s_biased, t)
                    for a in range(KC):
                        last = nc.tensor.matmul(logits[u][:, :], xt[u][:, a, :], k.w_slice[:, a, :], start=(a == 0), stop=(a == KC - 1))
                    last.then_inc(s_lg, 1)

                def add_tokens(t, u, rows):
                    ready(pe, s_xk, t)
                    ready(pe, s_soft, t)
                    pe.wait_ge(s_one, 2)
                    for q in range(4):
                        last = nc.tensor.matmul(token[q][:, 0:C + 1], soft[u][0:rows, q * P:(q + 1) * P], xk[u][0:rows, :], start=False,
                                                stop=(rows == LAST), skip_group_check=True)
                    last.then_inc(s_tok, 1)

                pipelined(pe, head, no_tail, ahead=2, middle=add_tokens, late=logit_products)


def slices_and_attention(nc, k):
    with stage(nc) as (sb, pb, sem):
        token = [pb(f"sw_token{q}") for q in range(4)]
        logits = [pb(f"sw_logits{u}") for u in range(2)]
        slices_stage(nc, k, token, logits)
        slice_attention(nc, k, token, logits)


def slice_attention(nc, k, token, ps):
    with stage(nc) as (sb, pb, sem):
        w_fx = sb("sa_wfx", [P, KC, 2 * C])
        b_fx = sb("sa_bfx", [P, 4, P])
        pairs = sb("sa_pairs", [P, 3, P])
        w_out = sb("sa_wout", [P, 4, C])
        mask = sb("sa_mask", [P, P])
        tok = sb("sa_tok", [P, 4, C + 1])
        tok_t = sb("sa_tok_t", [P, 2, P])
        den = sb("sa_den", [P, 2])
        bterm = sb("sa_bterm", [P, P])
        fx = sb("sa_fx", [P, P])
        fx2 = sb("sa_fx2", [P, P])
        st = sb("sa_st", [P, P])
        st_t = sb("sa_st_t", [P, P])
        q_t = sb("sa_q_t", [P, P])
        k_t = sb("sa_k_t", [P, P])
        v = sb("sa_v", [P, P])
        sc = sb("sa_sc", [P, HD1])
        stat = sb("sa_stat", [P, 3])
        ex = sb("sa_ex", [P, HD1])
        att = sb("sa_att", [P, P])
        att_t = sb("sa_att_t", [P, P])
        o_t = sb("sa_o_t", [P, P])
        s_w, s_v, s_p, s_a = (sem(f"sa_{n}") for n in ("weights_loaded", "vector_steps", "tensor_steps", "exp_steps"))
        V, T = 20, 8
        with nc.Block() as block:
            @block.sync
            def _(sp):
                sp.dma_start(w_fx[:, :, :], k.ins["L0_ffn_W_fx"].rearrange("(k p) n -> p k n", p=P)).then_inc(s_w, 16)
                sp.dma_start(b_fx[:, :, :].rearrange("p q d -> p (q d)"), k.ins["L0_ffn_b_fx"].partition_broadcast(P)).then_inc(s_w, 16)
                sp.dma_start(pairs[:, :, :], k.ins["pair_qkv"].rearrange("i p d -> p i d")).then_inc(s_w, 16)
                sp.dma_start(w_out[:, :, :], k.ins["L0_ffn_W_out"].rearrange("(q p) c -> p q c", p=P)).then_inc(s_w, 16)
                sp.dma_start(mask[:, :], k.ins["blocks64"]).then_inc(s_w, 16)

            @block.vector
            def _(dve):
                nc.vector.memset(att[:, :], 0.0).then_inc(s_v, 1)
                for q in range(4):
                    last = nc.vector.tensor_copy(tok[:, q, :], token[q][:, 0:C + 1])
                last.then_inc(s_v, 1)
                dve.wait_ge(s_w, 80)
                for q in range(4):
                    done = [2 + V * q]

                    def step(instruction):
                        instruction.then_inc(s_v, 1)
                        done[0] += 1
                        dve.wait_ge(s_v, done[0])

                    dve.wait_ge(s_v, 2 + V * q)
                    step(nc.vector.tensor_scalar(den[:, 0:1], tok[:, q, C:C + 1], 1e-5, None, ALU.add))
                    step(nc.vector.reciprocal(den[:, 1:2], den[:, 0:1]))
                    step(nc.vector.tensor_scalar(bterm[:, :], b_fx[:, q, :], tok[:, q, C:C + 1], None, ALU.mult))
                    dve.wait_ge(s_p, T * q + 1)
                    step(nc.vector.tensor_copy(tok_t[:, :, :].rearrange("p a g -> p (a g)"), ps[0][:, 0:C]))
                    dve.wait_ge(s_p, T * q + 2)
                    step(nc.vector.tensor_tensor(fx[:, :], ps[1][:, 0:P], bterm[:, :], ALU.add))
                    step(nc.vector.tensor_scalar(fx2[:, :], fx[:, :], den[:, 1:2], None, ALU.mult))
                    step(nc.vector.tensor_tensor(st[:, :], fx2[:, :], mask[:, :], ALU.mult))
                    dve.wait_ge(s_p, T * q + 3)
                    step(nc.vector.tensor_copy(st_t[:, :], ps[0][:, 0:P]))
                    dve.wait_ge(s_p, T * q + 4)
                    step(nc.vector.tensor_copy(q_t[:, :], ps[1][:, 0:P]))
                    step(nc.vector.tensor_copy(k_t[:, :], ps[1][:, P:2 * P]))
                    step(nc.vector.tensor_copy(v[:, :], ps[1][:, 2 * P:3 * P]))
                    dve.wait_ge(s_p, T * q + 5)
                    nc.vector.tensor_scalar(sc[0:64, :], ps[0][0:64, 0:64], 64 ** -0.5, None, ALU.mult)
                    step(nc.vector.tensor_scalar(sc[64:P, :], ps[0][64:P, 64:P], 64 ** -0.5, None, ALU.mult))
                    step(nc.vector.tensor_reduce(stat[:, 0:1], sc[:, :], AX.X, ALU.max))
                    step(nc.vector.tensor_scalar(sc[:, :], sc[:, :], stat[:, 0:1], None, ALU.subtract))
                    dve.wait_ge(s_a, q + 1)
                    step(nc.vector.tensor_reduce(stat[:, 1:2], ex[:, :], AX.X, ALU.add))
                    step(nc.vector.reciprocal(stat[:, 2:3], stat[:, 1:2]))
                    nc.vector.tensor_scalar(att[0:64, 0:64], ex[0:64, :], stat[0:64, 2:3], None, ALU.mult)
                    step(nc.vector.tensor_scalar(att[64:P, 64:P], ex[64:P, :], stat[64:P, 2:3], None, ALU.mult))
                    dve.wait_ge(s_p, T * q + 6)
                    step(nc.vector.tensor_copy(att_t[:, :], ps[1][:, 0:P]))
                    dve.wait_ge(s_p, T * q + 7)
                    step(nc.vector.tensor_copy(o_t[:, :], ps[0][:, 0:P]))
                    dve.wait_ge(s_p, T * q + 8)
                    step(nc.vector.tensor_copy(k.slices[:, q, :], ps[1][:, 0:C]))
                    assert done[0] == 2 + V * (q + 1)

            @block.scalar
            def _(act):
                for q in range(4):
                    act.wait_ge(s_v, 2 + V * q + 14)
                    nc.scalar.activation(ex[:, :], sc[:, :], ACT.Exp).then_inc(s_a, 1)

            @block.tensor
            def _(pe):
                pe.wait_ge(s_w, 80)
                for q in range(4):
                    base = 2 + V * q
                    pair = slice(q * P, (q + 1) * P)
                    pe.wait_ge(s_v, base)
                    for a in range(KC):
                        last = nc.tensor.transpose(ps[0][:, a * P:(a + 1) * P], tok[:, q, a * P:(a + 1) * P], k.ident[:, :])
                    last.then_inc(s_p, 1)
                    pe.wait_ge(s_v, base + 4)
                    for a in range(KC):
                        last = nc.tensor.matmul(ps[1][:, 0:P], tok_t[:, a, :], w_fx[:, a, pair], start=(a == 0), stop=(a == KC - 1))
                    last.then_inc(s_p, 1)
                    pe.wait_ge(s_v, base + 7)
                    nc.tensor.transpose(ps[0][:, 0:P], st[:, :], k.ident[:, :]).then_inc(s_p, 1)
                    pe.wait_ge(s_v, base + 8)
                    nc.tensor.matmul(ps[1][:, 0:P], pairs[:, 0, :], st_t[:, :], start=True, stop=True)
                    nc.tensor.matmul(ps[1][:, P:2 * P], pairs[:, 1, :], st_t[:, :], start=True, stop=True)
                    nc.tensor.matmul(ps[1][:, 2 * P:3 * P], st_t[:, :], pairs[:, 2, :], start=True, stop=True).then_inc(s_p, 1)
                    pe.wait_ge(s_v, base + 11)
                    nc.tensor.matmul(ps[0][:, 0:P], q_t[:, :], k_t[:, :], start=True, stop=True).then_inc(s_p, 1)
                    pe.wait_ge(s_v, base + 17)
                    nc.tensor.transpose(ps[1][:, 0:P], att[:, :], k.ident[:, :]).then_inc(s_p, 1)
                    pe.wait_ge(s_v, base + 18)
                    nc.tensor.matmul(ps[0][:, 0:P], v[:, :], att_t[:, :], start=True, stop=True).then_inc(s_p, 1)
                    pe.wait_ge(s_v, base + 19)
                    nc.tensor.matmul(ps[1][:, 0:C], o_t[:, :], w_out[:, q, :], start=True, stop=True).then_inc(s_p, 1)


def second_update_stage(nc, k):
    with stage(nc) as (sb, pb, sem):
        bias = sb("su_bias", [P, C])
        soft = [sb(f"su_soft{u}", [P, 2 * C]) for u in range(2)]
        soft_t = [sb(f"su_soft_t{u}", [P, 4, P]) for u in range(2)]
        turned = [pb(f"su_turned{u}") for u in range(2)]
        out = [pb(f"su_out{u}") for u in range(2)]
        s_w, s_zeros = sem("su_bias_loaded"), sem("su_zeros_stored")
        s_soft, s_turned, s_copied, s_out, s_add, s_x, s_stats, s_step, s_rstd = (sem(f"su_{n}") for n in (
            "softmax_copied", "softmax_turned", "turned_copied", "out_ready", "out_added", "x_updated", "stats_ready", "moment_steps", "rstd"))
        with nc.Block() as block:
            @block.sync
            def _(sp):
                sp.dma_start(bias[:, :], k.ins["L0_ffn_b_out"].partition_broadcast(P)).then_inc(s_w, 16)
                sp.dma_start(k.expert_in.rearrange("(s p) c -> p s c", p=P),
                             k.zero_wide[:, :].bitcast(F32).unsqueeze(1).to_broadcast([P, SLOT_TILES, C])).then_inc(s_zeros, 16)
                sp.wait_ge(s_zeros, 16)

            @block.gpsimd
            def _(pool):
                start_at_two(pool, s_soft)

                def head(t, u, i):
                    free(pool, s_turned, t)
                    nc.gpsimd.tensor_copy(soft[u][:, :], at(k.soft, t)).then_inc(s_soft, 1)

                pipelined(pool, head, no_tail)
                row_scale(nc, pool, k, s_step, s_rstd)

            @block.vector
            def _(dve):
                start_at_two(dve, s_add, s_x, s_stats)
                dve.wait_ge(s_w, 16)

                def tail(t, u, rows):
                    ready(dve, s_out, t)
                    nc.vector.tensor_tensor(at(k.x, t), at(k.x, t), out[u][:, 0:C], ALU.add).then_inc(s_add, 1)
                    ready(dve, s_add, t)
                    nc.vector.tensor_tensor(at(k.x, t), at(k.x, t), bias[:, :], ALU.add).then_inc(s_x, 1)
                    ready(dve, s_x, t)
                    carry(dve, k)
                    row_stats(nc, k, t).then_inc(s_stats, 1)

                pipelined(dve, no_head, tail)
                ready(dve, s_stats, TILES - 1)
                row_moments(nc, dve, k, s_step)

            @block.scalar
            def _(act):
                start_at_two(act, s_copied)

                def head(t, u, i):
                    ready(act, s_turned, t)
                    free(act, s_out, t)
                    nc.scalar.activation(soft_t[u][:, :, :].rearrange("p k n -> p (k n)"), turned[u][:, :], ACT.Copy).then_inc(s_copied, 1)

                pipelined(act, head, no_tail)

            @block.tensor
            def _(pe):
                start_at_two(pe, s_turned, s_out)

                def head(t, u, i):
                    ready(pe, s_soft, t)
                    free(pe, s_copied, t)
                    for a in range(4):
                        last = nc.tensor.transpose(turned[u][:, a * P:(a + 1) * P], soft[u][:, a * P:(a + 1) * P], k.ident[:, :])
                    last.then_inc(s_turned, 1)

                def tail(t, u, rows):
                    ready(pe, s_copied, t)
                    free(pe, s_add, t)
                    for q in range(4):
                        last = nc.tensor.matmul(out[u][:, 0:C], soft_t[u][:, q, :], k.slices[:, q, :], start=(q == 0), stop=(q == 3))
                    last.then_inc(s_out, 1)

                pipelined(pe, head, tail)


def layer1_and_attention(nc, k):
    with stage(nc) as (sb, pb, sem):
        hk = [pb(f"la_hk{u}") for u in range(2)]
        product = pb("la_product")
        keysum = pb("la_keysum")
        layer1_stage(nc, k, hk, product, keysum)
        attention_matrix(nc, k, product, keysum, hk)


def layer1_stage(nc, k, hk, product, keysum):
    with stage(nc) as (sb, pb, sem):
        w = sb("la_w", [P, KC, 3 * C])
        b1 = sb("la_b1", [P, C])
        xn = [sb(f"la_xn{u}", [P, C]) for u in range(2)]
        xt = [sb(f"la_xt{u}", [P, KC, P]) for u in range(2)]
        pre = [sb(f"la_pre{u}", [P, C]) for u in range(2)]
        row = [sb(f"la_row{u}", [P, C]) for u in range(2)]
        bn = [sb(f"la_bn{u}", [P, 8, 6]) for u in range(2)]
        mv = [sb(f"la_mv{u}", [P, 8, 2]) for u in range(2)]
        rs = [sb(f"la_rs{u}", [P, 8]) for u in range(2)]
        kv = [sb(f"la_kv{u}", [P, 2 * C]) for u in range(2)]
        turned = [pb(f"la_turned{u}") for u in range(2)]
        vp = [pb(f"la_v{u}") for u in range(2)]
        s_stored = [sem(f"la_table_stored{u}") for u in range(2)]
        s_w = sem("la_weights_loaded")
        s_xn, s_kept, s_turned, s_xt, s_h, s_pre, s_row, s_bn, s_mv, s_eps, s_rs, s_mid, s_kv, s_sum = (sem(f"la_{n}") for n in (
            "rows_ready", "rows_kept", "rows_turned", "turned_copied", "products_ready", "bias_added", "table_row", "bn_ready", "variance_ready",
            "eps_added", "scale_ready", "mean_subtracted", "kv_ready", "product_added"))
        by_head = lambda ap: ap.rearrange("p (h d) -> p h d", d=HD1)
        wide = lambda ap: ap.unsqueeze(2).to_broadcast([P, 4, HD1])
        with nc.Block() as block:
            @block.sync
            def _(sp):
                sp.dma_start(w[:, :, 0:C], k.ins["L1_gnn_c1_w1"].rearrange("(k p) n -> p k n", p=P)).then_inc(s_w, 16)
                sp.dma_start(w[:, :, C:3 * C], k.ins["L1_mix_wkvT"].rearrange("(k p) n -> p k n", p=P)).then_inc(s_w, 16)
                sp.dma_start(b1[:, :], k.ins["L1_gnn_c1_b1"].partition_broadcast(P)).then_inc(s_w, 16)
                for u in range(2):
                    sp.sem_inc(s_stored[u], 16)

                def tail(t, u, rows):
                    ready(sp, s_row, t)
                    sp.dma_start(table_rows(k, t), row[u][:, :]).then_inc(s_stored[u], 16)

                pipelined(sp, no_head, tail)
                sp.wait_ge(s_stored[0], 16 + 16 * (TILES // 2 + 1))
                sp.wait_ge(s_stored[1], 16 + 16 * (TILES // 2))

            @block.gpsimd
            def _(pool):
                start_at_two(pool, s_kept, s_eps, s_rs)

                def head(t, u, i):
                    ready(pool, s_xn, t)
                    nc.gpsimd.tensor_copy(at(k.rows, t), xn[u][:, :]).then_inc(s_kept, 1)

                def tail(t, u, rows):
                    ready(pool, s_mv, t)
                    carry(pool, k)
                    nc.gpsimd.tensor_scalar(rs[u][:, :], mv[u][:, :, 1], EPS, None, ALU.add).then_inc(s_eps, 1)
                    ready(pool, s_eps, t)
                    nc.gpsimd.tensor_tensor(rs[u][:, :], rs[u][:, :], k.half[:, 0:1].to_broadcast([P, 8]), ALU.pow).then_inc(s_rs, 1)

                pipelined(pool, no_head, no_tail, ahead=2, middle=tail, late=head)

            @block.vector
            def _(dve):
                start_at_two(dve, s_xn, s_pre, s_bn, s_mv, s_mid, s_kv)
                dve.wait_ge(s_w, 48)

                def head(t, u, i):
                    free(dve, s_turned, t)
                    free(dve, s_kept, t)
                    normalise(nc, k, xn[u][:, :], t).then_inc(s_xn, 1)

                def statistics(t, u, rows):
                    ready(dve, s_h, t)
                    free(dve, s_row, t)
                    nc.vector.tensor_tensor(pre[u][:, :], hk[u][:, 0:C], b1[:, :], ALU.add).then_inc(s_pre, 1)
                    for h in range(8):
                        src = hk[u][:, C + HD1 * h:C + HD1 * (h + 1)] if h < 4 else vp[u][:, HD1 * (h - 4):HD1 * (h - 3)]
                        last = nc.vector.bn_stats(bn[u][:, h, :], src)
                    last.then_inc(s_bn, 1)
                    ready(dve, s_bn, t)
                    free(dve, s_kv, t)
                    carry(dve, k)
                    for h in range(8):
                        last = nc.vector.bn_aggr(mv[u][:, h, :], bn[u][:, h, :])
                    last.then_inc(s_mv, 1)
                    ready(dve, s_mv, t)
                    free(dve, s_sum, t)
                    nc.vector.tensor_tensor(by_head(kv[u][:, 0:C]), by_head(hk[u][:, C:2 * C]), wide(mv[u][:, 0:4, 0]), ALU.subtract)
                    nc.vector.tensor_tensor(by_head(kv[u][:, C:2 * C]), by_head(vp[u][:, 0:C]), wide(mv[u][:, 4:8, 0]), ALU.subtract).then_inc(s_mid, 1)

                def tail(t, u, rows):
                    ready(dve, s_mid, t)
                    ready(dve, s_rs, t)
                    nc.vector.tensor_tensor(by_head(kv[u][:, :]), by_head(kv[u][:, :]), rs[u][:, :].unsqueeze(2).to_broadcast([P, 8, HD1]),
                                            ALU.mult).then_inc(s_kv, 1)

                pipelined(dve, no_head, tail, ahead=2, middle=statistics, late=head)

            @block.scalar
            def _(act):
                start_at_two(act, s_xt, s_row)

                def head(t, u, i):
                    ready(act, s_turned, t)
                    free(act, s_h, t)
                    nc.scalar.activation(xt[u][:, :, :].rearrange("p k n -> p (k n)"), turned[u][:, 0:C], ACT.Copy).then_inc(s_xt, 1)

                def tail(t, u, rows):
                    ready(act, s_pre, t)
                    act.wait_ge(s_stored[u], 8 * (t - u) + 16)
                    nc.scalar.activation(row[u][:, :], pre[u][:, :], ACT.Relu).then_inc(s_row, 1)

                pipelined(act, no_head, no_tail, ahead=2, middle=tail, late=head)

            @block.tensor
            def _(pe):
                start_at_two(pe, s_turned, s_h, s_sum)
                for bank in (product, keysum):
                    nc.tensor.matmul(bank[:, 0:C + KC], k.zero_b[:, :], k.zero_wide[:, 0:C + KC], start=True, stop=False, skip_group_check=True)
                pe.wait_ge(s_w, 48)

                def head(t, u, i):
                    ready(pe, s_xn, t)
                    free(pe, s_xt, t)
                    for a in range(KC):
                        last = nc.tensor.transpose(turned[u][:, a * P:(a + 1) * P], xn[u][:, a * P:(a + 1) * P], k.ident[:, :])
                    last.then_inc(s_turned, 1)

                def table_keys_values(t, u, i):
                    ready(pe, s_xt, t)
                    free(pe, s_mid, t)
                    for a in range(KC):
                        nc.tensor.matmul(hk[u][:, :], xt[u][:, a, :], w[:, a, 0:2 * C], start=(a == 0), stop=(a == KC - 1))
                    for a in range(KC):
                        last = nc.tensor.matmul(vp[u][:, 0:C], xt[u][:, a, :], w[:, a, 2 * C:3 * C], start=(a == 0), stop=(a == KC - 1))
                    last.then_inc(s_h, 1)

                def products(t, u, rows):
                    ready(pe, s_kv, t)
                    stop = rows == LAST
                    nc.tensor.matmul(keysum[:, 0:C], k.ones[0:rows, :], kv[u][0:rows, 0:C], start=False, stop=stop, skip_group_check=True)
                    for a in range(KC):
                        values = kv[u][0:rows, C + a * P:C + (a + 1) * P]
                        nc.tensor.matmul(product[:, a * P:(a + 1) * P], values, kv[u][0:rows, a * P:(a + 1) * P], start=False, stop=stop,
                                         skip_group_check=True)
                        last = nc.tensor.matmul(product[:, C + a:C + a + 1], values, k.ones[0:rows, 0:1], start=False, stop=stop,
                                                skip_group_check=True)
                    last.then_inc(s_sum, 1)

                pipelined(pe, head, no_tail, ahead=2, middle=products, late=table_keys_values)


def attention_matrix(nc, k, product, keysum, ps):
    with stage(nc) as (sb, pb, sem):
        wq = sb("am_wq", [P, KC, C])
        wo = sb("am_wo", [P, KC, C])
        key_rows = sb("am_key_rows", [P, 2, P])
        val_cols = sb("am_val_cols", [P, 2])
        mask = sb("am_mask", [P, P])
        t0 = sb("am_t0", [P, KC, P])
        t1 = sb("am_t1", [P, KC, P])
        t2 = sb("am_t2", [P, KC, P])
        t3 = sb("am_t3", [P, KC, P])
        kv_t = sb("am_kv_t", [P, KC, P])
        half = sb("am_half", [P, KC, C])
        s_w, s_v, s_p = (sem(f"am_{n}") for n in ("weights_loaded", "vector_steps", "tensor_steps"))
        with nc.Block() as block:
            @block.sync
            def _(sp):
                sp.dma_start(wq[:, :, :], k.ins["L1_mix_wq"].rearrange("(k p) n -> p k n", p=P)).then_inc(s_w, 16)
                sp.dma_start(wo[:, :, :], k.ins["L1_mix_woT"].rearrange("(k p) n -> p k n", p=P)).then_inc(s_w, 16)
                sp.dma_start(key_rows[:, 0, :], k.ins["key_g2"].partition_broadcast(P)).then_inc(s_w, 16)
                sp.dma_start(key_rows[:, 1, :], k.ins["key_b2"].partition_broadcast(P)).then_inc(s_w, 16)
                sp.dma_start(val_cols[:, :], k.ins["val_gb2"]).then_inc(s_w, 16)
                sp.dma_start(mask[:, :], k.ins["blocks64"]).then_inc(s_w, 16)

            @block.vector
            def _(dve):
                dve.wait_ge(s_w, 96)
                for a in range(KC):
                    part = slice(a * P, (a + 1) * P)
                    gk, bk = key_rows[:, 0, :], key_rows[:, 1, :]
                    gv, bv = val_cols[:, 0:1], val_cols[:, 1:2]
                    done = [9 * a]

                    def step(instruction):
                        instruction.then_inc(s_v, 1)
                        done[0] += 1
                        dve.wait_ge(s_v, done[0])

                    step(nc.vector.tensor_scalar(t0[:, a, :], product[:, part], gv, None, ALU.mult))
                    step(nc.vector.tensor_scalar(t1[:, a, :], keysum[:, part], bv, None, ALU.mult))
                    step(nc.vector.tensor_tensor(t0[:, a, :], t0[:, a, :], t1[:, a, :], ALU.add))
                    step(nc.vector.tensor_tensor(t0[:, a, :], t0[:, a, :], gk, ALU.mult))
                    step(nc.vector.tensor_scalar(t2[:, a, 0:1], product[:, C + a:C + a + 1], gv, None, ALU.mult))
                    step(nc.vector.scalar_tensor_tensor(t3[:, a, 0:1], bv, float(NODES), t2[:, a, 0:1], ALU.mult, ALU.add))
                    step(nc.vector.scalar_tensor_tensor(t1[:, a, :], bk, t3[:, a, 0:1], t0[:, a, :], ALU.mult, ALU.add))
                    step(nc.vector.scalar_tensor_tensor(kv_t[:, a, :], t1[:, a, :], 1.0 / NODES, mask[:, :], ALU.mult, ALU.mult))
                    dve.wait_ge(s_p, a + 1)
                    step(nc.vector.tensor_copy(half[:, a, :], ps[0][:, a * C:(a + 1) * C]))
                dve.wait_ge(s_p, KC + 1)
                nc.vector.tensor_copy(k.mix1[:, :, :].rearrange("p k n -> p (k n)"), ps[1][:, :])

            @block.tensor
            def _(pe):
                pe.wait_ge(s_w, 96)
                for a in range(KC):
                    pe.wait_ge(s_v, 9 * a + 8)
                    nc.tensor.matmul(ps[0][:, a * C:(a + 1) * C], kv_t[:, a, :], wo[:, a, :], start=True, stop=True).then_inc(s_p, 1)
                pe.wait_ge(s_v, 9 * KC)
                for b in range(KC):
                    for a in range(KC):
                        last = nc.tensor.matmul(ps[1][:, b * C:(b + 1) * C], wq[:, a, b * P:(b + 1) * P], half[:, a, :], start=(a == 0), stop=(a == KC - 1))
                last.then_inc(s_p, 1)


def node_stats_scale(nc, k, name, stats, gamma, beta, scale, shift):
    with stage(nc) as (sb, pb, sem):
        mv = sb(f"{name}_mv", [P, KC, 2])
        par = sb(f"{name}_par", [P, 2, KC])
        tmp = sb(f"{name}_tmp", [P, 3, KC])
        s_w, s_v, s_p = (sem(f"{name}_{n}") for n in ("parameters", "vector_steps", "pool_steps"))
        with nc.Block() as block:
            @block.sync
            def _(sp):
                sp.dma_start(par[:, 0, :], gamma).then_inc(s_w, 16)
                sp.dma_start(par[:, 1, :], beta).then_inc(s_w, 16)

            @block.gpsimd
            def _(pool):
                pool.wait_ge(s_v, 1)
                nc.gpsimd.tensor_scalar(tmp[:, 0, :], mv[:, :, 1], EPS, None, ALU.add).then_inc(s_p, 1)
                pool.wait_ge(s_p, 1)
                nc.gpsimd.tensor_tensor(tmp[:, 1, :], tmp[:, 0, :], k.half[:, 0:1].to_broadcast([P, KC]), ALU.pow).then_inc(s_p, 1)

            @block.vector
            def _(dve):
                for a in range(KC):
                    last = nc.vector.bn_aggr(mv[:, a, :], stats[:, a, :, :].rearrange("p t s -> p (t s)"))
                last.then_inc(s_v, 1)
                dve.wait_ge(s_w, 32)
                dve.wait_ge(s_p, 2)
                nc.vector.tensor_tensor(scale, tmp[:, 1, :], par[:, 0, :], ALU.mult).then_inc(s_v, 1)
                dve.wait_ge(s_v, 2)
                nc.vector.tensor_tensor(tmp[:, 2, :], scale, mv[:, :, 0], ALU.mult).then_inc(s_v, 1)
                dve.wait_ge(s_v, 3)
                nc.vector.tensor_tensor(shift, par[:, 1, :], tmp[:, 2, :], ALU.subtract)


def convolve_stage(nc, k, name, w2_in, b2_in, gamma1, beta1, gamma2, beta2, scale, shift):
    CHUNK = 448
    CHUNKS = PADDED // CHUNK
    SHORT = NODES - (CHUNKS - 1) * CHUNK
    chunk = lambda c: k.sums_t[:, :, c * CHUNK:(c + 1) * CHUNK] if isinstance(c, int) else k.sums_t[:, :, bass.ds(c * CHUNK, CHUNK)]
    with stage(nc) as (sb, pb, sem):
        w2 = sb(f"{name}_w2", [P, KC, C])
        b2 = sb(f"{name}_b2", [P, KC])
        stats = sb(f"{name}_stats", [P, KC, CHUNKS, 6])
        scale1 = sb(f"{name}_scale1", [P, KC])
        shift1 = sb(f"{name}_shift1", [P, KC])
        out = [[pb(f"{name}_out{u}{a}") for a in range(KC)] for u in range(2)]
        s_w = sem(f"{name}_weights_loaded")
        s_out, s_h, s_stats = (sem(f"{name}_{n}") for n in ("out_ready", "h_ready", "stats_ready"))
        with nc.Block() as block:
            @block.sync
            def _(sp):
                sp.dma_start(w2[:, :, :], w2_in.rearrange("(k p) n -> p k n", p=P)).then_inc(s_w, 16)
                sp.dma_start(b2[:, :], b2_in).then_inc(s_w, 16)

            @block.vector
            def _(dve):
                def tail(c, u, last_chunk):
                    ready(dve, s_h, c)
                    chunk_stats = stats[:, :, c:c + 1, :] if isinstance(c, int) else stats[:, :, bass.ds(c, 1), :]
                    carry(dve, k)
                    for a in range(KC):
                        last = nc.vector.bn_stats(chunk_stats[:, a, 0, :], chunk(c)[:, a, 0:SHORT if last_chunk else CHUNK])
                    last.then_inc(s_stats, 1)

                pipelined_chunks(dve, CHUNKS, no_head, tail)

            @block.scalar
            def _(act):
                start_at_two(act, s_h)
                act.wait_ge(s_w, 32)

                def tail(c, u, last_chunk):
                    ready(act, s_out, c)
                    for a in range(KC):
                        last = nc.scalar.activation(chunk(c)[:, a, :], out[u][a][:, 0:CHUNK], ACT.Identity, bias=b2[:, a:a + 1])
                    last.then_inc(s_h, 1)

                pipelined_chunks(act, CHUNKS, no_head, tail)

            @block.tensor
            def _(pe):
                start_at_two(pe, s_out)
                pe.wait_ge(s_w, 32)

                def head(c, u, i):
                    free(pe, s_h, c)
                    for a in range(KC):
                        for b in range(KC):
                            last = nc.tensor.matmul(out[u][a][:, 0:CHUNK], w2[:, b, a * P:(a + 1) * P], chunk(c)[:, b, :], start=(b == 0), stop=(b == KC - 1))
                    last.then_inc(s_out, 1)

                pipelined_chunks(pe, CHUNKS, head, no_tail)

        node_stats_scale(nc, k, f"{name}_bn1", stats, gamma1, beta1, scale1[:, :], shift1[:, :])
        s_y = sem(f"{name}_relu_ready")
        with nc.Block() as block:
            @block.scalar
            def _(act):
                for c in range(CHUNKS):
                    for a in range(KC):
                        part = chunk(c)[:, a, :]
                        last = nc.scalar.activation(part, part, ACT.Relu, bias=shift1[:, a:a + 1], scale=scale1[:, a:a + 1])
                    last.then_inc(s_y, 1)

            @block.vector
            def _(dve):
                for c in range(CHUNKS):
                    dve.wait_ge(s_y, c + 1)
                    for a in range(KC):
                        nc.vector.bn_stats(stats[:, a, c, :], chunk(c)[:, a, 0:SHORT if c == CHUNKS - 1 else CHUNK])
        node_stats_scale(nc, k, f"{name}_bn2", stats, gamma2, beta2, scale[:, :], shift[:, :])


def table2_stage(nc, k, scale, shift):
    with stage(nc) as (sb, pb, sem):
        w1 = sb("tb_w1", [P, KC, C])
        b1 = sb("tb_b1", [P, C])
        h_t = [sb(f"tb_h_t{u}", [P, KC, P]) for u in range(2)]
        pre = [sb(f"tb_pre{u}", [P, C]) for u in range(2)]
        row = [sb(f"tb_row{u}", [P, C]) for u in range(2)]
        out = [pb(f"tb_out{u}") for u in range(2)]
        s_stored = [sem(f"tb_table_stored{u}") for u in range(2)]
        s_w, s_h, s_out, s_pre, s_row = (sem(f"tb_{n}") for n in ("weights_loaded", "h_ready", "out_ready", "bias_added", "table_row"))
        with nc.Block() as block:
            @block.sync
            def _(sp):
                sp.dma_start(w1[:, :, :], k.ins["L1_gnn_c2_w1"].rearrange("(k p) n -> p k n", p=P)).then_inc(s_w, 16)
                sp.dma_start(b1[:, :], k.ins["L1_gnn_c2_b1"].partition_broadcast(P)).then_inc(s_w, 16)
                for u in range(2):
                    sp.sem_inc(s_stored[u], 16)

                def tail(t, u, rows):
                    ready(sp, s_row, t)
                    sp.dma_start(table_rows(k, t), row[u][:, :]).then_inc(s_stored[u], 16)

                pipelined(sp, no_head, tail)
                sp.wait_ge(s_stored[0], 16 + 16 * (TILES // 2 + 1))
                sp.wait_ge(s_stored[1], 16 + 16 * (TILES // 2))

            @block.vector
            def _(dve):
                start_at_two(dve, s_pre)
                dve.wait_ge(s_w, 32)

                def tail(t, u, rows):
                    ready(dve, s_out, t)
                    free(dve, s_row, t)
                    nc.vector.tensor_tensor(pre[u][:, :], out[u][:, 0:C], b1[:, :], ALU.add).then_inc(s_pre, 1)

                pipelined(dve, no_head, tail)

            @block.scalar
            def _(act):
                start_at_two(act, s_h, s_row)

                def head(t, u, i):
                    free(act, s_out, t)
                    for a in range(KC):
                        last = nc.scalar.activation(h_t[u][:, a, :], nodes(k, t)[:, a, :], ACT.Relu, bias=shift[:, a:a + 1], scale=scale[:, a:a + 1])
                    last.then_inc(s_h, 1)

                def tail(t, u, rows):
                    ready(act, s_pre, t)
                    act.wait_ge(s_stored[u], 8 * (t - u) + 16)
                    nc.scalar.activation(row[u][:, :], pre[u][:, :], ACT.Relu).then_inc(s_row, 1)

                pipelined(act, head, tail, ahead=2)

            @block.tensor
            def _(pe):
                start_at_two(pe, s_out)
                pe.wait_ge(s_w, 32)

                def head(t, u, i):
                    ready(pe, s_h, t)
                    free(pe, s_pre, t)
                    for a in range(KC):
                        last = nc.tensor.matmul(out[u][:, 0:C], h_t[u][:, a, :], w1[:, a, :], start=(a == 0), stop=(a == KC - 1))
                    last.then_inc(s_out, 1)

                pipelined(pe, head, no_tail)


def third_update_stage(nc, k, scale, shift):
    with stage(nc) as (sb, pb, sem):
        bias = sb("tu_bias", [P, C])
        h_t = [sb(f"tu_h_t{u}", [P, KC, P]) for u in range(2)]
        xn = [sb(f"tu_xn{u}", [P, C]) for u in range(2)]
        xt = [sb(f"tu_xt{u}", [P, KC, P]) for u in range(2)]
        res = [sb(f"tu_res{u}", [P, C]) for u in range(2)]
        turned = [pb(f"tu_turned{u}") for u in range(2)]
        x_turned = [pb(f"tu_x_turned{u}") for u in range(2)]
        out = [pb(f"tu_out{u}") for u in range(2)]
        s_w = sem("tu_bias_loaded")
        s_h, s_xn, s_turned, s_xt, s_out, s_res, s_relu, s_add, s_x, s_stats, s_step, s_rstd = (sem(f"tu_{n}") for n in (
            "h_ready", "rows_copied", "turned", "rows_turned_copied", "out_ready", "residual_added", "relu_added", "out_added", "x_updated",
            "stats_ready", "moment_steps", "rstd"))
        with nc.Block() as block:
            @block.sync
            def _(sp):
                sp.dma_start(bias[:, :], k.ins["L1_mix_bo"].partition_broadcast(P)).then_inc(s_w, 16)

            @block.gpsimd
            def _(pool):
                start_at_two(pool, s_xn)

                def head(t, u, i):
                    free(pool, s_turned, t)
                    free(pool, s_res, t)
                    nc.gpsimd.tensor_copy(xn[u][:, :], at(k.rows, t)).then_inc(s_xn, 1)

                pipelined(pool, head, no_tail)
                row_scale(nc, pool, k, s_step, s_rstd)

            @block.vector
            def _(dve):
                start_at_two(dve, s_res, s_relu, s_add, s_x, s_stats)
                dve.wait_ge(s_w, 16)

                def head(t, u, i):
                    ready(dve, s_turned, t)
                    ready(dve, s_xn, t)
                    free(dve, s_relu, t)
                    nc.vector.tensor_tensor(res[u][:, :], turned[u][:, 0:C], xn[u][:, :], ALU.add).then_inc(s_res, 1)

                def add_residual(t, u, rows):
                    ready(dve, s_res, t)
                    nc.vector.scalar_tensor_tensor(at(k.x, t), res[u][:, :], 0.0, at(k.x, t), ALU.max, ALU.add).then_inc(s_relu, 1)

                def tail(t, u, rows):
                    ready(dve, s_relu, t)
                    ready(dve, s_out, t)
                    nc.vector.tensor_tensor(at(k.x, t), at(k.x, t), out[u][:, 0:C], ALU.add).then_inc(s_add, 1)
                    ready(dve, s_add, t)
                    nc.vector.tensor_tensor(at(k.x, t), at(k.x, t), bias[:, :], ALU.add).then_inc(s_x, 1)
                    ready(dve, s_x, t)
                    carry(dve, k)
                    row_stats(nc, k, t).then_inc(s_stats, 1)

                pipelined(dve, no_head, tail, ahead=2, middle=add_residual, late=head)
                ready(dve, s_stats, TILES - 1)
                row_moments(nc, dve, k, s_step)

            @block.scalar
            def _(act):
                start_at_two(act, s_h, s_xt)

                def head(t, u, i):
                    free(act, s_turned, t)
                    for a in range(KC):
                        last = nc.scalar.activation(h_t[u][:, a, :], nodes(k, t)[:, a, :], ACT.Identity, bias=shift[:, a:a + 1], scale=scale[:, a:a + 1])
                    last.then_inc(s_h, 1)
                    ready(act, s_turned, t)
                    free(act, s_out, t)
                    nc.scalar.activation(xt[u][:, :, :].rearrange("p k n -> p (k n)"), x_turned[u][:, 0:C], ACT.Copy).then_inc(s_xt, 1)

                pipelined(act, head, no_tail)

            @block.tensor
            def _(pe):
                start_at_two(pe, s_turned, s_out)

                def head(t, u, i):
                    ready(pe, s_h, t)
                    ready(pe, s_xn, t)
                    free(pe, s_xt, t)
                    free(pe, s_res, t)
                    for a in range(KC):
                        nc.tensor.transpose(turned[u][:, a * P:(a + 1) * P], h_t[u][:, a, :], k.ident[:, :])
                    for a in range(KC):
                        last = nc.tensor.transpose(x_turned[u][:, a * P:(a + 1) * P], xn[u][:, a * P:(a + 1) * P], k.ident[:, :])
                    last.then_inc(s_turned, 1)

                def tail(t, u, rows):
                    ready(pe, s_xt, t)
                    free(pe, s_add, t)
                    for a in range(KC):
                        last = nc.tensor.matmul(out[u][:, 0:C], xt[u][:, a, :], k.mix1[:, a, :], start=(a == 0), stop=(a == KC - 1))
                    last.then_inc(s_out, 1)

                pipelined(pe, head, tail)


def router_stage(nc, k):
    E = EXPERTS
    with stage(nc) as (sb, pb, sem):
        wr = sb("ro_wr", [P, KC, E])
        br = sb("ro_br", [P, E])
        gb = sb("ro_gb", [P, 2, C])
        z = [sb(f"ro_z{u}", [P, C]) for u in range(2)]
        zg = [sb(f"ro_zg{u}", [P, C]) for u in range(2)]
        xn = [sb(f"ro_xn{u}", [P, C]) for u in range(2)]
        xt = [sb(f"ro_xt{u}", [P, KC, P]) for u in range(2)]
        logit = sb("ro_logit", [P, TILES, E])
        turned = [pb(f"ro_turned{u}") for u in range(2)]
        logits = [pb(f"ro_logits{u}") for u in range(2)]
        s_w = sem("ro_weights_loaded")
        s_z, s_zg, s_xn, s_turned, s_xt, s_kept, s_lg, s_logit = (sem(f"ro_{n}") for n in (
            "z_ready", "scaled", "rows_ready", "rows_turned", "turned_copied", "turned_kept", "logits_ready", "bias_added"))
        with nc.Block() as block:
            @block.sync
            def _(sp):
                sp.dma_start(wr[:, :, :], k.ins["L1_ffn_Wr"].rearrange("(k p) n -> p k n", p=P)).then_inc(s_w, 16)
                sp.dma_start(br[:, :], k.ins["L1_ffn_br"].partition_broadcast(P)).then_inc(s_w, 16)
                sp.dma_start(gb[:, 0, :], k.ins["L1_ffn_gamma"].partition_broadcast(P)).then_inc(s_w, 16)
                sp.dma_start(gb[:, 1, :], k.ins["L1_ffn_beta"].partition_broadcast(P)).then_inc(s_w, 16)

            @block.gpsimd
            def _(pool):
                start_at_two(pool, s_kept)

                def head(t, u, i):
                    ready(pool, s_xn, t)
                    nc.gpsimd.tensor_copy(at(k.rows, t), xn[u][:, :]).then_inc(s_kept, 1)

                pipelined(pool, head, no_tail)

            @block.vector
            def _(dve):
                start_at_two(dve, s_z, s_zg, s_xn, s_logit)
                dve.wait_ge(s_w, 64)

                def head(t, u, i):
                    free(dve, s_zg, t)
                    normalise(nc, k, z[u][:, :], t).then_inc(s_z, 1)
                    ready(dve, s_z, t)
                    free(dve, s_xn, t)
                    nc.vector.tensor_tensor(zg[u][:, :], z[u][:, :], gb[:, 0, :], ALU.mult).then_inc(s_zg, 1)
                    ready(dve, s_zg, t)
                    free(dve, s_turned, t)
                    free(dve, s_kept, t)
                    nc.vector.tensor_tensor(xn[u][:, :], zg[u][:, :], gb[:, 1, :], ALU.add).then_inc(s_xn, 1)

                def tail(t, u, rows):
                    ready(dve, s_lg, t)
                    nc.vector.tensor_tensor(at(logit, t), logits[u][:, 0:E], br[:, :], ALU.add).then_inc(s_logit, 1)

                pipelined(dve, head, tail, ahead=2)

            @block.scalar
            def _(act):
                start_at_two(act, s_xt)

                def head(t, u, i):
                    ready(act, s_turned, t)
                    free(act, s_lg, t)
                    nc.scalar.activation(xt[u][:, :, :].rearrange("p k n -> p (k n)"), turned[u][:, 0:C], ACT.Copy).then_inc(s_xt, 1)

                pipelined(act, head, no_tail)

            @block.tensor
            def _(pe):
                start_at_two(pe, s_turned, s_lg)
                pe.wait_ge(s_w, 64)

                def head(t, u, i):
                    ready(pe, s_xn, t)
                    free(pe, s_xt, t)
                    for a in range(KC):
                        last = nc.tensor.transpose(turned[u][:, a * P:(a + 1) * P], xn[u][:, a * P:(a + 1) * P], k.ident[:, :])
                    last.then_inc(s_turned, 1)

                def tail(t, u, rows):
                    ready(pe, s_xt, t)
                    free(pe, s_logit, t)
                    for a in range(KC):
                        last = nc.tensor.matmul(logits[u][:, 0:E], xt[u][:, a, :], wr[:, a, :], start=(a == 0), stop=(a == KC - 1))
                    last.then_inc(s_lg, 1)

                pipelined(pe, head, tail)

        place_rows(nc, k, logit)


def place_rows(nc, k, logit):
    E = EXPERTS
    wide3 = [P, TILES, E]
    with stage(nc) as (sb, pb, sem):
        rank, cmp, exp, gates, mask, pos = (sb(f"pl_{n}", wide3) for n in ("rank", "cmp", "exp", "gates", "mask", "pos"))
        sums = [sb(f"pl_sums{u}", wide3) for u in range(2)]
        top = sb("pl_top", [P, TILES])
        den = sb("pl_den", [P, 2, TILES])
        picked = sb("pl_picked", [P, 2, TILES])
        before = sb("pl_before", [P, P])
        full = sb("pl_full", [P, E])
        full_i = sb("pl_full_i", [P, 2, E], I32)
        base = sb("pl_base", [P, 2, E])
        number = sb("pl_number", [P, SLOT_TILES])
        of = sb("pl_of", [P, SLOT_TILES])
        earlier = pb("pl_earlier")
        in_tile = pb("pl_in_tile")
        s_v, s_e, s_c, s_m, s_p = (sem(f"pl_{n}") for n in ("vector_steps", "exp_ready", "constants", "mask_ready", "prefix_ready"))
        with nc.Block() as block:
            @block.vector
            def _(dve):
                done = [0]

                def step(instruction):
                    instruction.then_inc(s_v, 1)
                    done[0] += 1
                    dve.wait_ge(s_v, done[0])

                step(nc.vector.tensor_reduce(top[:, :], logit[:, :, :], AX.X, ALU.max))
                step(nc.vector.tensor_tensor(exp[:, :, :], logit[:, :, :], top[:, :].unsqueeze(2).to_broadcast(wide3), ALU.subtract))
                step(nc.vector.memset(rank[:, :, :], 0.0))
                for other in range(E):
                    them = logit[:, :, other:other + 1]
                    if other:
                        step(nc.vector.tensor_tensor(cmp[:, :, 0:other], them.to_broadcast([P, TILES, other]), logit[:, :, 0:other], ALU.is_gt))
                        step(nc.vector.tensor_tensor(rank[:, :, 0:other], rank[:, :, 0:other], cmp[:, :, 0:other], ALU.add))
                    if other < E - 1:
                        n = E - 1 - other
                        step(nc.vector.tensor_tensor(cmp[:, :, 0:n], them.to_broadcast([P, TILES, n]), logit[:, :, other + 1:E], ALU.is_ge))
                        step(nc.vector.tensor_tensor(rank[:, :, other + 1:E], rank[:, :, other + 1:E], cmp[:, :, 0:n], ALU.add))
                nc.vector.tensor_scalar(mask[:, :, :], rank[:, :, :], 2.0, None, ALU.is_lt).then_inc(s_m, 1)
                dve.wait_ge(s_m, 1)
                dve.wait_ge(s_e, 1)
                step(nc.vector.tensor_tensor(gates[:, :, :], mask[:, :, :], exp[:, :, :], ALU.mult))
                step(nc.vector.tensor_reduce(den[:, 0, :], gates[:, :, :], AX.X, ALU.add))
                step(nc.vector.reciprocal(den[:, 1, :], den[:, 0, :]))
                step(nc.vector.tensor_tensor(gates[:, :, :], gates[:, :, :], den[:, 1, :].unsqueeze(2).to_broadcast(wide3), ALU.mult))
                tile_sums = in_tile[:, 0:TILES * E].rearrange("p (t e) -> p t e", e=E)
                dve.wait_ge(s_p, 2)
                step(nc.vector.tensor_copy(sums[0][:, :, :], tile_sums))
                u, reach = 0, 1
                while reach < TILES:
                    a, b = sums[u], sums[1 - u]
                    step(nc.vector.tensor_tensor(b[:, reach:, :], a[:, reach:, :], a[:, 0:TILES - reach, :], ALU.add))
                    step(nc.vector.tensor_copy(b[:, 0:reach, :], a[:, 0:reach, :]))
                    u, reach = 1 - u, 2 * reach
                total = sums[u]
                step(nc.vector.tensor_scalar(full_i[:, 0, :], total[:, TILES - 1, :], float(P - 1), None, ALU.add))
                step(nc.vector.tensor_scalar(full_i[:, 1, :], full_i[:, 0, :], 7, None, ALU.arith_shift_right))
                step(nc.vector.tensor_copy(full[:, :], full_i[:, 1, :]))
                step(nc.vector.memset(base[:, 0, :], 0.0))
                for e in range(1, E):
                    step(nc.vector.tensor_tensor(base[:, 0, e:e + 1], base[:, 0, e - 1:e], full[:, e - 1:e], ALU.add))
                step(nc.vector.tensor_scalar(base[:, 1, :], base[:, 0, :], float(P), None, ALU.mult))
                step(nc.vector.tensor_tensor(pos[:, :, :], total[:, :, :], tile_sums, ALU.subtract))
                step(nc.vector.tensor_tensor(pos[:, :, :], pos[:, :, :], earlier[:, 0:TILES * E].rearrange("p (t e) -> p t e", e=E), ALU.add))
                step(nc.vector.tensor_tensor(pos[:, :, :], pos[:, :, :], base[:, 1, :].unsqueeze(1).to_broadcast(wide3), ALU.add))
                for r in range(2):
                    step(nc.vector.tensor_scalar(mask[:, :, :], rank[:, :, :], float(r), None, ALU.is_equal))
                    step(nc.vector.tensor_tensor(cmp[:, :, :], mask[:, :, :], pos[:, :, :], ALU.mult))
                    step(nc.vector.tensor_reduce(picked[:, r, :], cmp[:, :, :], AX.X, ALU.add))
                    step(nc.vector.tensor_copy(k.slot[:, :, r], picked[:, r, :]))
                    step(nc.vector.tensor_tensor(cmp[:, :, :], mask[:, :, :], gates[:, :, :], ALU.mult))
                    step(nc.vector.tensor_reduce(picked[:, r, :], cmp[:, :, :], AX.X, ALU.add))
                    step(nc.vector.tensor_copy(k.gate[:, :, r], picked[:, r, :]))
                dve.wait_ge(s_c, 3)
                step(nc.vector.memset(of[:, :], 0.0))
                for e in range(1, E):
                    step(nc.vector.scalar_tensor_tensor(of[:, :], number[:, :], base[:, 0, e:e + 1], of[:, :], ALU.is_ge, ALU.add))
                step(nc.vector.tensor_copy(k.expert_of[:, :], of[:, :]))

            @block.scalar
            def _(act):
                act.wait_ge(s_v, 2)
                nc.scalar.activation(exp[:, :, :], exp[:, :, :], ACT.Exp).then_inc(s_e, 1)

            @block.gpsimd
            def _(pool):
                nc.gpsimd.memset(before[:, :], 0.0).then_inc(s_c, 1)
                nc.gpsimd.iota(number[:, :], pattern=[[1, SLOT_TILES]], base=0, channel_multiplier=0,
                               allow_small_or_imprecise_dtypes=True).then_inc(s_c, 1)
                pool.wait_ge(s_c, 1)
                nc.gpsimd.affine_select(out=before[:, :], in_=before[:, :], compare_op=ALU.is_ge, fill=1.0, base=0,
                                        pattern=[[-1, P]], channel_multiplier=1).then_inc(s_c, 1)

            @block.tensor
            def _(pe):
                pe.wait_ge(s_m, 1)
                pe.wait_ge(s_c, 3)
                for bank, weights in ((earlier, before), (in_tile, k.ones)):
                    nc.tensor.matmul(bank[:, 0:TILES * E], weights[:, :], mask[:, :, :].rearrange("p t e -> p (t e)"),
                                     start=True, stop=True).then_inc(s_p, 1)


def experts_stage(nc, k):
    with stage(nc) as (sb, pb, sem):
        place = [0]

        def cut(n):
            place[0] += n
            return k.wide[:, place[0] - n:place[0]]

        w1 = cut(EXPERTS * KC * HID).rearrange("p (e k n) -> p e k n", e=EXPERTS, k=KC)
        b1 = cut(EXPERTS * HID).rearrange("p (e n) -> p e n", e=EXPERTS)
        w2 = sb("ex_w2", [P, EXPERTS, FT, C])
        s_w = sem("ex_weights_loaded")
        scatter_stage(nc, k, w1, w2, b1, s_w)
        place[0] = KC * (PADDED + WINDOW)
        b2 = cut(EXPERTS * C).rearrange("p (e n) -> p e n", e=EXPERTS)
        multiply_stage(nc, k, cut, w1, w2, b1, b2, s_w)
        return_stage(nc, k, cut)


def scatter_stage(nc, k, w1, w2, b1, s_w):
    with stage(nc) as (sb, pb, sem):
        row = [sb(f"sc_row{u}", [P, C]) for u in range(2)]
        slot = [sb(f"sc_slot{u}", [P, 2], I32) for u in range(2)]
        s_row, s_slot, s_done = (sem(f"sc_{n}") for n in ("row_copied", "slots_copied", "scattered"))
        with nc.Block() as block:
            @block.sync
            def _(sp):
                for e in range(EXPERTS):
                    sp.dma_start(w1[:, e], k.ins["L1_ffn_W1"][e].rearrange("(k p) n -> p k n", p=P)).then_inc(s_w, 16)
                    sp.dma_start(b1[:, e], k.ins["L1_ffn_b1"][e].partition_broadcast(P)).then_inc(s_w, 16)
                    sp.dma_start(w2[:, e], k.ins["L1_ffn_W2"][e].rearrange("(k p) n -> p k n", p=P)).then_inc(s_w, 16)

            @block.vector
            def _(dve):
                start_at_two(dve, s_slot)

                def head(t, u, i):
                    free(dve, s_done, t)
                    ready(dve, s_row, t)
                    nc.vector.tensor_copy(slot[u][:, :], at(k.slot, t)).then_inc(s_slot, 1)

                pipelined(dve, head, no_tail)

            @block.scalar
            def _(act):
                start_at_two(act, s_row)

                def head(t, u, i):
                    free(act, s_done, t)
                    nc.scalar.activation(row[u][:, :], at(k.rows, t), ACT.Copy).then_inc(s_row, 1)

                pipelined(act, head, no_tail)

            @block.gpsimd
            def _(pool):
                start_at_two(pool, s_done)

                def head(t, u, i):
                    ready(pool, s_slot, t)
                    carry(pool, k)
                    for r in range(2):
                        nc.gpsimd.indirect_dma_start(out=k.expert_in, out_offset=bass.IndirectOffsetOnAxis(ap=slot[u][:, r:r + 1], axis=0),
                                                     in_=row[u][:, :], in_offset=None).then_inc(k.s_scattered[u], 16)

                def tail(t, u, rows):
                    pool.wait_ge(k.s_scattered[u], 16 * (t - u) + 32)
                    pool.sem_inc(s_done, 1)

                pipelined(pool, head, tail)


def multiply_stage(nc, k, cut, w1, w2, b1, b2, s_w):
    with stage(nc) as (sb, pb, sem):
        rows = [cut(C) for u in range(2)]
        rows_t = [cut(C).rearrange("p (a n) -> p a n", a=KC) for u in range(2)]
        pre = [cut(HID) for u in range(2)]
        hid = [cut(HID) for u in range(2)]
        hid_t = [cut(HID).rearrange("p (f n) -> p f n", f=FT) for u in range(2)]
        y = [cut(C) for u in range(2)]
        turned = [pb(f"ex_turned{u}") for u in range(2)]
        up = [pb(f"ex_up{u}") for u in range(2)]
        hid_turned = [pb(f"ex_hid_turned{u}") for u in range(2)]
        down = [pb(f"ex_down{u}") for u in range(2)]
        s_rows = [sem(f"ex_rows_loaded{u}") for u in range(2)]
        s_b2 = sem("ex_b2_loaded")
        s_turned, s_rows_t, s_up, s_pre, s_hid, s_ht, s_hid_t, s_down, s_y, s_done = (sem(f"ex_{n}") for n in (
            "rows_turned", "turned_copied", "up_ready", "bias_added", "hidden_ready", "hidden_turned", "hidden_copied", "down_ready", "y_ready", "y_stored"))
        slots = lambda dram, t: dram[t * P:(t + 1) * P, :] if isinstance(t, int) else dram[bass.ds(t * P, P), :]

        def expert(engine, t):
            at_t = slice(t, t + 1) if isinstance(t, int) else bass.ds(t, 1)
            return engine.value_load(k.expert_of[0:1, at_t], min_val=0, max_val=EXPERTS - 1)

        with nc.Block() as block:
            @block.sync
            def _(sp):
                sp.dma_start(b2.rearrange("p e n -> p (e n)"), k.ins["L1_ffn_b2"].rearrange("e n -> (e n)").partition_broadcast(P)).then_inc(s_b2, 16)
                with sp.Fori(0, SLOT_TILES // 2) as i:
                    for u in range(2):
                        t = 2 * i + u
                        free(sp, s_turned, t)
                        sp.dma_start(rows[u], slots(k.expert_in, t)).then_inc(s_rows[u], 16)

            @block.gpsimd
            def _(pool):
                start_at_two(pool, s_done)
                with pool.Fori(0, SLOT_TILES // 2) as i:
                    for u in range(2):
                        ready(pool, s_y, 2 * i + u)
                        carry(pool, k)
                        nc.gpsimd.dma_start(slots(k.expert_out, 2 * i + u), y[u]).then_inc(k.s_stored[u], 16)
                        pool.wait_ge(k.s_stored[u], 16 * i + 16)
                        pool.sem_inc(s_done, 1)

            @block.scalar
            def _(act):
                start_at_two(act, s_rows_t, s_hid)

                def copy_turned(t, u):
                    ready(act, s_turned, t)
                    free(act, s_up, t)
                    nc.scalar.activation(rows_t[u].rearrange("p a n -> p (a n)"), turned[u][:, 0:C], ACT.Copy).then_inc(s_rows_t, 1)

                def gelu(t, u):
                    ready(act, s_pre, t)
                    free(act, s_ht, t)
                    nc.scalar.activation(hid[u], pre[u], ACT.Gelu).then_inc(s_hid, 1)

                interleaved(act, SLOT_TILES, copy_turned, gelu, nothing, nothing)

            @block.vector
            def _(dve):
                start_at_two(dve, s_pre, s_hid_t, s_y)
                dve.wait_ge(s_w, 48 * EXPERTS)
                dve.wait_ge(s_b2, 16)
                which = [dve.alloc_register(f"ex_dve_expert{u}") for u in range(2)]

                def add_bias(t, u):
                    dve.reg_mov(which[u], expert(dve, t))
                    e = dve.snap(which[u], min_val=0, max_val=EXPERTS - 1)
                    ready(dve, s_up, t)
                    free(dve, s_hid, t)
                    nc.vector.tensor_tensor(pre[u], up[u][:, :], b1[:, bass.ds(e, 1), :].rearrange("p a n -> p (a n)"), ALU.add).then_inc(s_pre, 1)

                def copy_hidden(t, u):
                    ready(dve, s_ht, t)
                    free(dve, s_down, t)
                    nc.vector.tensor_copy(hid_t[u].rearrange("p f n -> p (f n)"), hid_turned[u][:, :]).then_inc(s_hid_t, 1)

                def finish(t, u):
                    e = dve.snap(which[u], min_val=0, max_val=EXPERTS - 1)
                    ready(dve, s_down, t)
                    free(dve, s_done, t)
                    nc.vector.tensor_tensor(y[u], down[u][:, 0:C], b2[:, bass.ds(e, 1), :].rearrange("p a n -> p (a n)"), ALU.add).then_inc(s_y, 1)

                interleaved(dve, SLOT_TILES, nothing, add_bias, copy_hidden, finish)

            @block.tensor
            def _(pe):
                start_at_two(pe, s_turned, s_up, s_ht, s_down)
                pe.wait_ge(s_w, 48 * EXPERTS)
                which = [pe.alloc_register(f"ex_pe_expert{u}") for u in range(2)]

                def turn_rows(t, u):
                    pe.reg_mov(which[u], expert(pe, t))
                    pe.wait_ge(s_rows[u], 8 * (t - u) + 16)
                    free(pe, s_rows_t, t)
                    for a in range(KC):
                        last = nc.tensor.transpose(turned[u][:, a * P:(a + 1) * P], rows[u][:, a * P:(a + 1) * P], k.ident[:, :])
                    last.then_inc(s_turned, 1)

                def multiply_up(t, u):
                    e = pe.snap(which[u], min_val=0, max_val=EXPERTS - 1)
                    ready(pe, s_rows_t, t)
                    free(pe, s_pre, t)
                    for a in range(KC):
                        last = nc.tensor.matmul(up[u][:, :], rows_t[u][:, a, :], w1[:, bass.ds(e, 1), a, :].rearrange("p a n -> p (a n)"),
                                                start=(a == 0), stop=(a == KC - 1))
                    last.then_inc(s_up, 1)

                def turn_hidden(t, u):
                    ready(pe, s_hid, t)
                    free(pe, s_hid_t, t)
                    for f in range(FT):
                        last = nc.tensor.transpose(hid_turned[u][:, f * P:(f + 1) * P], hid[u][:, f * P:(f + 1) * P], k.ident[:, :])
                    last.then_inc(s_ht, 1)

                def multiply_down(t, u):
                    e = pe.snap(which[u], min_val=0, max_val=EXPERTS - 1)
                    ready(pe, s_hid_t, t)
                    free(pe, s_y, t)
                    for f in range(FT):
                        last = nc.tensor.matmul(down[u][:, 0:C], hid_t[u][:, f, :], w2[:, bass.ds(e, 1), f, :].rearrange("p a n -> p (a n)"),
                                                start=(f == 0), stop=(f == FT - 1))
                    last.then_inc(s_down, 1)

                interleaved(pe, SLOT_TILES, turn_rows, multiply_up, turn_hidden, multiply_down)


def return_stage(nc, k, cut):
    with stage(nc) as (sb, pb, sem):
        slot = [sb(f"rt_slot{u}", [P, 2], I32) for u in range(2)]
        y = [[cut(C) for r in range(2)] for u in range(2)]
        one = [cut(C) for u in range(2)]
        both = [cut(C) for u in range(2)]
        s_out = [sem(f"rt_stored{u}") for u in range(2)]
        s_slot, s_one, s_both, s_turn = (sem(f"rt_{n}") for n in ("slots_copied", "one_added", "both_added", "gather_turn"))
        with nc.Block() as block:
            @block.gpsimd
            def _(pool):
                def head(t, u, i):
                    ready(pool, s_slot, t)
                    carry(pool, k)
                    for r in range(2):
                        nc.gpsimd.indirect_dma_start(out=y[u][r], out_offset=None, in_=k.expert_out,
                                                     in_offset=bass.IndirectOffsetOnAxis(ap=slot[u][:, r:r + 1], axis=0)).then_inc(k.s_returned[u], 16)

                pipelined(pool, head, no_tail)

            @block.vector
            def _(dve):
                start_at_two(dve, s_slot, s_one, s_both)

                def head(t, u, i):
                    free(dve, s_both, t)
                    nc.vector.tensor_copy(slot[u][:, :], at(k.slot, t)).then_inc(s_slot, 1)

                def tail(t, u, rows):
                    dve.wait_ge(k.s_returned[u], 16 * (t - u) + 32)
                    dve.wait_ge(s_out[u], 8 * (t - u) + 16)
                    gate = at(k.gate, t)
                    carry(dve, k)
                    nc.vector.scalar_tensor_tensor(one[u], y[u][0], gate[:, 0:1], at(k.x, t), ALU.mult, ALU.add).then_inc(s_one, 1)
                    ready(dve, s_one, t)
                    carry(dve, k)
                    nc.vector.scalar_tensor_tensor(both[u], y[u][1], gate[:, 1:2], one[u], ALU.mult, ALU.add).then_inc(s_both, 1)

                pipelined(dve, head, tail)

            @block.sync
            def _(sp):
                for u in range(2):
                    sp.sem_inc(s_out[u], 16)

                def tail(t, u, rows):
                    ready(sp, s_both, t)
                    out = k.out[t * P:t * P + rows, :] if isinstance(t, int) else k.out[bass.ds(t * P, P), :]
                    sp.dma_start(out, both[u][0:rows, :]).then_inc(s_out[u], 16)

                pipelined(sp, no_head, tail)
                sp.wait_ge(s_out[0], 16 + 16 * (TILES // 2 + 1))
                sp.wait_ge(s_out[1], 16 + 16 * (TILES // 2))


_INS = ["x_in", "edges", "dst_cols", "blocks32", "blocks64",
        "L0_gnn_W", "L0_mix_WqT", "L0_mix_WkvT", "L0_mix_WprojT", "L0_mix_bproj",
        "L0_ffn_W_fx", "L0_ffn_b_fx", "L0_ffn_W_xT", "L0_ffn_b_x4", "pair_slice", "b_slice8", "pair_qkv", "L0_ffn_W_out", "L0_ffn_b_out",
        "temperature",
        "L1_gnn_c1_w1", "L1_gnn_c1_b1", "L1_gnn_c1_w2", "L1_gnn_c2_w1", "L1_gnn_c2_b1", "L1_gnn_c2_w2", "bn_rows",
        "L1_mix_wq", "L1_mix_wkvT", "L1_mix_woT", "L1_mix_bo", "key_g2", "key_b2", "val_gb2",
        "L1_ffn_gamma", "L1_ffn_beta", "L1_ffn_Wr", "L1_ffn_br", "L1_ffn_W1", "L1_ffn_b1", "L1_ffn_W2", "L1_ffn_b2"]


def gps_two_layers(nc, ins, out):
    k = Core()
    k.ins = ins
    k.out = out
    k.table = nc.dram_tensor("table", [PADDED, C], F32).ap()
    k.expert_in = nc.dram_tensor("expert_in", [SLOT_TILES * P, C], F32).ap()
    k.expert_out = nc.dram_tensor("expert_out", [SLOT_TILES * P, C], F32).ap()
    k.win_dram = nc.dram_tensor("window_bounds", [GROUPS // 2, 4], I32).ap()
    bn = [k.ins["bn_rows"][i] for i in range(10)]
    with ExitStack() as ctx:
        residents(nc, k, ctx)
        setup_stage(nc, k)
        wide_residents(nc, k, ctx)
        with ExitStack() as graph:
            graph_residents(nc, k, graph)
            first_stats_stage(nc, k)
            keys_stage(nc, k)
            edge_stage(nc, k, "e0", False, 0)
            first_update_stage(nc, k)
            with ExitStack() as ffn:
                k.w_slice = ffn.enter_context(nc.sbuf_tensor("w_slice", [P, KC, 2 * C], F32))
                k.b_slice = ffn.enter_context(nc.sbuf_tensor("b_slice", [P, 2 * C], F32))
                slice_weights_stage(nc, k)
                slices_and_attention(nc, k)
            second_update_stage(nc, k)
            layer1_and_attention(nc, k)
            edge_stage(nc, k, "e1", True, 1)
            convolve_stage(nc, k, "c1", k.ins["L1_gnn_c1_w2"], bn[0], bn[1], bn[2], bn[3], bn[4], k.bn_scale, k.bn_shift)
            table2_stage(nc, k, k.bn_scale, k.bn_shift)
            edge_stage(nc, k, "e2", True, 2)
            convolve_stage(nc, k, "c2", k.ins["L1_gnn_c2_w2"], bn[5], bn[6], bn[7], bn[8], bn[9], k.bn_scale, k.bn_shift)
            third_update_stage(nc, k, k.bn_scale, k.bn_shift)
            router_stage(nc, k)
        experts_stage(nc, k)


def kernel(**inputs):
    import numpy as np
    import concourse.bacc as bacc
    from concourse.bass_utils import run_bass_kernel_spmd as run

    i = {n: np.asarray(a) for n, a in inputs.items()}

    def by_column(a, fill):
        flat = np.full(GROUPS * SUB * P, fill, a.dtype)
        flat[:EDGES] = a
        return flat.reshape(GROUPS * SUB, P)

    def twice(w):
        m = np.zeros((P, P), w.dtype)
        m[:64, :64] = w
        m[64:, 64:] = w
        return m

    def blocks(n):
        return np.kron(np.eye(P // n, dtype=np.float32), np.ones((n, n), np.float32))

    src, dst, weight = (by_column(a, f) for a, f in ((i["src"], 0), (i["dst"], PADDED - 1), (i["edge_weight"], 0)))
    edges = np.stack([a.view(np.int32).reshape(2 * TRIPS, 16, P) for a in (src, dst, weight)], 1)
    x = np.zeros((PADDED, C), i["x"].dtype)
    x[:NODES] = i["x"]
    channels = lambda a: a.reshape(KC, P).T
    arrays = {
        "x_in": x, "edges": edges.transpose(0, 3, 1, 2), "dst_cols": dst.T, "blocks32": blocks(32), "blocks64": blocks(64),
        "L0_mix_WqT": i["L0_mix_Wq"].T, "L0_mix_WkvT": i["L0_mix_Wkv"].T, "L0_mix_WprojT": i["L0_mix_Wproj"].T,
        "L0_ffn_W_xT": i["L0_ffn_W_x"].T, "L0_ffn_b_x4": i["L0_ffn_b_x"].reshape(4, P).T, "pair_slice": twice(i["L0_ffn_W_slice"]),
        "b_slice8": np.tile(i["L0_ffn_b_slice"], SH), "pair_qkv": np.stack([twice(i["L0_ffn_W_" + n]) for n in "qkv"]),
        "temperature": i["L0_ffn_temperature"].reshape(-1),
        "bn_rows": np.stack([channels(i["L1_gnn_" + n]) for n in ("c1_b2", "c1_g", "c1_b", "bn1_g", "bn1_b", "c2_b2", "c2_g", "c2_b", "bn2_g", "bn2_b")]),
        "L1_mix_wkvT": np.concatenate([i["L1_mix_wk"].T, i["L1_mix_wv"].T], 1), "L1_mix_woT": i["L1_mix_wo"].T,
        "key_g2": np.tile(i["L1_mix_ln_k_g"], 2), "key_b2": np.tile(i["L1_mix_ln_k_b"], 2),
        "val_gb2": np.stack([np.tile(i["L1_mix_ln_v_g"], 2), np.tile(i["L1_mix_ln_v_b"], 2)], 1),
    }
    arrays = {n: np.ascontiguousarray(arrays.get(n, i.get(n))) for n in _INS}
    nc = bacc.Bacc("TRN2", target_bir_lowering=False, num_devices=1)
    ins = {n: nc.dram_tensor(f"in_{n}", a.shape, mybir.dt.from_np(a.dtype), kind="ExternalInput").ap() for n, a in arrays.items()}
    out = nc.dram_tensor("out", (NODES, C), F32, kind="ExternalOutput").ap()
    gps_two_layers(nc, ins, out)
    got = run(nc, [{f"in_{n}": a for n, a in arrays.items()}], core_ids=[0])
    return got.results[0]["out"]
```

```python
import concourse.bass as bass
from concourse import mybir
from contextlib import ExitStack, contextmanager

F32 = mybir.dt.float32
I32 = mybir.dt.int32
I16 = mybir.dt.int16
BF16 = mybir.dt.bfloat16
ALU = mybir.AluOpType
ACT = mybir.ActivationFunctionType
AX = mybir.AxisListType

P = 128
NODES = 6250
EDGES = 200000
C = 256
KC = C // P
TILES = -(-NODES // P)
LAST = NODES - (TILES - 1) * P
PADDED = TILES * P
SUB = 8
TRIPS = -(-EDGES // (P * SUB * 4))
GROUPS = 4 * TRIPS
WINDOW = 64
EPS = 1e-5
HEADS0, HD0 = 8, 32
SLICES, SH = 64, 8
HEADS1, HD1 = 4, 64
EXPERTS, HID = 8, 512
FT = HID // P
SLOT_TILES = (2 * PADDED + EXPERTS * (P - 1)) // P
SLOT_TILES += SLOT_TILES % 2


class Core:
    pass


class Work:

    def __init__(self, scalar, vector, tensor):
        self.scalar, self.vector, self.tensor = scalar, vector, tensor


def start_at_two(engine, *sems):
    for s in sems:
        engine.sem_inc(s, 2)


def ready(engine, sem, t):
    engine.wait_ge(sem, t + 3)


def free(engine, sem, t):
    engine.wait_ge(sem, t + 1)


def carry(engine, k):
    engine.sem_inc(k.carried, 1)


def pipelined(engine, head, tail, ahead=1, middle=None, late=None):
    def heads(t, u, i):
        head(t, u, i)
        if late:
            late(t, u, i)

    def step(t, u, i, then):
        head(t + ahead, then, i)
        if middle:
            middle(t, u, P)
        if late:
            late(t + ahead, then, i)
        tail(t, u, P)

    def end(t, u, rows):
        if middle:
            middle(t, u, rows)
        tail(t, u, rows)

    for t in range(ahead):
        heads(t, t, 0)
    if ahead == 1:
        with engine.Fori(0, TILES // 2) as i:
            step(2 * i, 0, i, 1)
            step(2 * i + 1, 1, i + 1, 0)
    else:
        with engine.Fori(0, TILES // 2 - 1) as i:
            step(2 * i, 0, i + 1, 0)
            step(2 * i + 1, 1, i + 1, 1)
        step(TILES - 3, 0, TILES // 2, 0)
        end(TILES - 2, 1, P)
    end(TILES - 1, 0, LAST)


def three_deep(engine, far, near, last):
    far(0, 0)
    far(1, 1)
    near(0, 0)
    with engine.Fori(0, TILES // 2 - 1) as i:
        far(2 * i + 2, 0)
        near(2 * i + 1, 1)
        last(2 * i, 0, P)
        far(2 * i + 3, 1)
        near(2 * i + 2, 0)
        last(2 * i + 1, 1, P)
    far(TILES - 1, 0)
    near(TILES - 2, 1)
    last(TILES - 3, 0, P)
    near(TILES - 1, 0)
    last(TILES - 2, 1, P)
    last(TILES - 1, 0, LAST)


def pipelined_chunks(engine, count, head, tail):
    head(0, 0, 0)
    with engine.Fori(0, count // 2 - 1) as i:
        head(2 * i + 1, 1, i)
        tail(2 * i, 0, False)
        head(2 * i + 2, 0, i + 1)
        tail(2 * i + 1, 1, False)
    head(count - 1, 1, count // 2 - 1)
    tail(count - 2, 0, False)
    tail(count - 1, 1, True)


def interleaved(engine, count, head_a, head_b, tail_a, tail_b):
    def step(t, u):
        head_a(t + 1, 1 - u)
        tail_a(t, u)
        head_b(t + 1, 1 - u)
        tail_b(t, u)

    head_a(0, 0)
    head_b(0, 0)
    with engine.Fori(0, count // 2 - 1) as i:
        step(2 * i, 0)
        step(2 * i + 1, 1)
    step(count - 2, 0)
    tail_a(count - 1, 1)
    tail_b(count - 1, 1)


def nothing(t, u):
    pass


def no_head(t, u, i):
    pass


def no_tail(t, u, rows):
    pass


def table_rows(k, t):
    return k.table[t * P:(t + 1) * P, :] if isinstance(t, int) else k.table[bass.ds(t * P, P), :]


def col(buf, t):
    return buf[:, t:t + 1] if isinstance(t, int) else buf[:, bass.ds(t, 1)]


@contextmanager
def stage(nc):
    sems = []
    with ExitStack() as ctx:
        def sem(name):
            sems.append(ctx.enter_context(nc.semaphore(name)))
            return sems[-1]

        sb = lambda name, shape, dt=F32: ctx.enter_context(nc.sbuf_tensor(name, shape, dt))
        pb = lambda name, shape=(P, 512), dt=F32: ctx.enter_context(nc.psum_tensor(name, list(shape), dt))
        yield sb, pb, sem
        with nc.Block() as block:
            @block.gpsimd
            def _(pool):
                for s in sems:
                    pool.sem_clear(s)


def at(buf, t):
    if isinstance(t, int):
        return buf[:, t, :]
    return buf[:, bass.ds(t, 1), :].rearrange("p a n -> p (a n)")


def nodes(k, t, tiles=1):
    return k.sums_t[:, :, t * P:(t + tiles) * P] if isinstance(t, int) else k.sums_t[:, :, bass.ds(t * P, tiles * P)]


def setup_stage(nc, k):
    with stage(nc) as (sb, pb, sem):
        dst = sb("dst", [P, GROUPS * SUB], I32)
        dst_f = sb("dst_f", [P, GROUPS * SUB])
        part = sb("part", [P, 2, GROUPS * SUB], I32)
        low = sb("low", [P, GROUPS * SUB], BF16)
        high = sb("high", [P, GROUPS * SUB], BF16)
        count_b = sb("count_b", [P, P, 16], BF16)
        low_hot = [sb(f"low_hot{u}", [P, P, 16], BF16) for u in range(2)]
        high_hot = [sb(f"high_hot{u}", [P, TILES, 16], BF16) for u in range(2)]
        ends = sb("ends", [P, 2, GROUPS])
        ends_t = sb("ends_t", [GROUPS // 2, 2, 2])
        ends_i = sb("ends_i", [GROUPS // 2, 2, 2], I32)
        deg = sb("deg", [P, TILES])
        root = sb("root", [P, TILES])
        linked = sb("linked", [P, TILES])
        turned = pb("turned")
        deg_ps = pb("deg_ps")
        s_load, s_x, s_zero, s_const, s_iota = (sem(n) for n in ("dst_loaded", "x_loaded", "zeroed", "const_ready", "iota_ready"))
        s_f, s_part, s_lh, s_ends, s_turned, s_red, s_int, s_win = (sem(n) for n in (
            "dst_float", "parts_int", "parts_ready", "ends_ready", "ends_turned", "ends_reduced", "bounds_ready", "bounds_moved"))
        s_hot, s_free, s_deg, s_degs, s_r, s_half = (sem(n) for n in ("hot_ready", "hot_free", "deg_ready", "deg_copied", "root_ready", "half_ready"))
        with nc.Block() as block:
            @block.sync
            def _(sp):
                sp.dma_start(dst[:, :], k.ins["dst_cols"]).then_inc(s_load, 16)
                sp.dma_start(k.x[:, :, :], k.ins["x_in"].rearrange("(t p) c -> p t c", p=P)).then_inc(s_x, 16)
                sp.wait_ge(s_int, 2)
                sp.dma_start(k.win_dram, ends_i[:, :, :].rearrange("i j e -> i (j e)")).then_inc(s_win, 16)
                sp.wait_ge(s_win, 16)
                sp.dma_start(k.windows[0:1, :], k.win_dram.rearrange("(a i) e -> a (i e)", a=1)).then_inc(s_win, 16)
                sp.wait_ge(s_win, 32)
                sp.wait_ge(s_x, 16)

            @block.gpsimd
            def _(pool):
                nc.gpsimd.memset(k.ident[:, :], 0.0).then_inc(s_zero, 1)
                nc.gpsimd.memset(k.ones[:, :], 1.0).then_inc(s_const, 1)
                pool.wait_ge(s_zero, 1)
                nc.gpsimd.affine_select(out=k.ident[:, :], in_=k.ident[:, :], compare_op=ALU.not_equal, fill=1.0, base=0,
                                        pattern=[[-1, P]], channel_multiplier=1).then_inc(s_const, 1)
                nc.gpsimd.iota(count_b[:, :, :], pattern=[[1, P], [0, 16]], base=0, channel_multiplier=0,
                               allow_small_or_imprecise_dtypes=True).then_inc(s_iota, 1)
                nc.gpsimd.memset(k.zero_wide[:, :], 0.0)
                nc.gpsimd.memset(k.zero_b[:, :], 0.0).then_inc(s_const, 1)
                nc.gpsimd.memset(k.half[:, :], -0.5).then_inc(s_half, 1)
                pool.wait_ge(s_degs, 1)
                pool.wait_ge(s_half, 1)
                nc.gpsimd.tensor_tensor(root[:, :], deg[:, :], k.half[:,0:1].to_broadcast([P,TILES]), ALU.pow).then_inc(s_r, 1)

            @block.vector
            def _(dve):
                dve.wait_ge(s_load, 16)
                nc.vector.tensor_copy(dst_f[:, :], dst[:, :]).then_inc(s_f, 1)
                nc.vector.tensor_scalar(part[:, 0, :], dst[:, :], P - 1, None, ALU.bitwise_and).then_inc(s_part, 1)
                nc.vector.tensor_scalar(part[:, 1, :], dst[:, :], 7, None, ALU.arith_shift_right).then_inc(s_part, 1)
                dve.wait_ge(s_f, 1)
                by_group = dst_f[:, :].rearrange("p (g k) -> p g k", k=SUB)
                nc.vector.tensor_reduce(ends[:, 0, :], by_group, AX.X, ALU.min).then_inc(s_ends, 1)
                nc.vector.tensor_reduce(ends[:, 1, :], by_group, AX.X, ALU.max).then_inc(s_ends, 1)
                dve.wait_ge(s_part, 2)
                nc.vector.tensor_copy(low[:, :], part[:, 0, :]).then_inc(s_lh, 1)
                nc.vector.tensor_copy(high[:, :], part[:, 1, :]).then_inc(s_lh, 1)
                dve.wait_ge(s_turned, 1)
                ends_ps = turned[0:GROUPS // 2, :].rearrange("i (e j p) -> i e j p", e=2, j=2)
                nc.vector.tensor_reduce(ends_t[:, :, 0], ends_ps[:, 0], AX.X, ALU.min).then_inc(s_red, 1)
                nc.vector.tensor_reduce(ends_t[:, :, 1], ends_ps[:, 1], AX.X, ALU.max).then_inc(s_red, 1)
                dve.wait_ge(s_red, 2)
                nc.vector.tensor_copy(ends_i[:, :, 0], ends_t[:, :, 0]).then_inc(s_int, 1)
                nc.vector.tensor_scalar(ends_i[:, :, 1], ends_t[:, :, 1], 1.0, None, ALU.add).then_inc(s_int, 1)
                dve.wait_ge(s_lh, 2)
                dve.wait_ge(s_iota, 1)
                with dve.Fori(0, TRIPS) as i:
                    for u in range(2):
                        cols = bass.ds(32 * i + 16 * u, 16)
                        dve.wait_ge(s_free, 2 * i + u + 1)
                        nc.vector.tensor_tensor(low_hot[u][:, :, :], count_b[:, :, :],
                                                low[:, cols].unsqueeze(1).to_broadcast([P, P, 16]), ALU.is_equal)
                        nc.vector.tensor_tensor(high_hot[u][:, :, :], count_b[:, 0:TILES, :],
                                                high[:, cols].unsqueeze(1).to_broadcast([P, TILES, 16]),
                                                ALU.is_equal).then_inc(s_hot, 1)
                dve.wait_ge(s_deg, 1)
                nc.vector.tensor_scalar(deg[:, :], deg_ps[:, 0:TILES], 1.0, None, ALU.max).then_inc(s_degs, 1)
                nc.vector.tensor_scalar(linked[:, :], deg_ps[:, 0:TILES], 0.0, None, ALU.is_gt).then_inc(s_r, 1)
                dve.wait_ge(s_r, 2)
                nc.vector.tensor_tensor(k.norm[:, :], root[:, :], linked[:, :], ALU.mult).then_inc(s_r, 1)

            @block.tensor
            def _(pe):
                pe.sem_inc(s_free, 2)
                pe.wait_ge(s_const, 3)
                pe.wait_ge(s_ends, 2)
                for e in range(2):
                    for j in range(2):
                        last = nc.tensor.transpose(turned[0:GROUPS // 2, P * (2 * e + j):P * (2 * e + j + 1)],
                                                   ends[:, e, j::2], k.ident[:, :])
                last.then_inc(s_turned, 1)
                nc.tensor.matmul(deg_ps[:, 0:TILES], k.zero_b[:, :], k.zero_b[:, 0:TILES], start=True, stop=False, skip_group_check=True)
                with pe.Fori(0, TRIPS) as i:
                    for u in range(2):
                        pe.wait_ge(s_hot, 2 * i + u + 1)
                        for m in range(16):
                            last = nc.tensor.matmul(deg_ps[:, 0:TILES], low_hot[u][:, :, m], high_hot[u][:, :, m],
                                                    start=False, stop=False, skip_group_check=True)
                        last.then_inc(s_free, 1)
                nc.tensor.matmul(deg_ps[:, 0:TILES], k.zero_b[:, :], k.zero_b[:, 0:TILES], start=False, stop=True,
                                 skip_group_check=True).then_inc(s_deg, 1)


def edge_stage(nc, k, name, weighted, turn, work=None):
    gathered = turn * 256 * TRIPS
    def trips(engine, trip):
        with engine.Fori(0, TRIPS - 1) as i:
            trip(i, P)
        trip(TRIPS - 1, LAST)

    with stage(nc) as (sb, pb, sem):
        edge = [sb(f"{name}_edge{b}", [P, 3, 16], I32) for b in range(2)]
        dest = [sb(f"{name}_dest{b}", [P, 16]) for b in range(2)]
        rows = sb(f"{name}_rows", [P, 2, SUB, C])
        hot = sb(f"{name}_hot", [P, 2, SUB, WINDOW])
        total = [pb(f"{name}_total{j}") for j in range(2)]
        s_edge = [sem(f"{name}_edges_loaded{b}") for b in range(2)]
        s_free = [sem(f"{name}_slots_free{j}") for j in range(2)]
        s_turn, s_dest, s_hot, s_total, s_added = (sem(f"{name}_{n}") for n in ("gather_turn", "dest_float", "hot_ready", "total_ready", "total_added"))
        with nc.Block() as block:
            @block.sync
            def _(sp):
                with sp.Fori(0, TRIPS) as i:
                    for b in range(2):
                        for j in range(2):
                            sp.wait_ge(s_free[j], 2 * i + b + 1)
                        sp.dma_start(edge[b][:, :, :],
                                     k.ins["edges"][bass.ds(2 * i + b, 1), :, :, :].rearrange("a p f m -> (a p) f m")).then_inc(s_edge[b], 16)

            @block.gpsimd
            def _(pool):
                with pool.Fori(0, TRIPS) as i:
                    for b in range(2):
                        pool.wait_ge(s_edge[b], 16 * i + 16)
                        for j in range(2):
                            pool.wait_ge(s_free[j], 2 * i + b + 2)
                            pool.sem_inc(s_turn, 1)
                            for m in range(SUB):
                                nc.gpsimd.indirect_dma_start(
                                    out=rows[:, j, m, :], out_offset=None, in_=k.table,
                                    in_offset=bass.IndirectOffsetOnAxis(ap=edge[b][:, 0, SUB * j + m:SUB * j + m + 1], axis=0),
                                ).then_inc(k.s_rows[j], 16)

            @block.vector
            def _(dve):
                dve.sem_inc(s_total, 1)
                nc.vector.memset(total[1][:, 0:KC * WINDOW], 0.0)
                nc.vector.memset(k.sums_t[:, :, :], 0.0).then_inc(s_added, 1)
                visit = dve.alloc_register(f"{name}_dve_visit")
                before = dve.alloc_register(f"{name}_dve_before")
                dve.reg_mov(visit, 1)
                dve.reg_mov(before, 0)

                def build(b, j, w):
                    for m in range(SUB):
                        at_m = slice(SUB * j + m, SUB * j + m + 1)
                        weight = edge[b][:, 2, at_m].bitcast(F32) if weighted else 1.0
                        last = nc.vector.tensor_scalar(hot[:, j, m, :], k.node_id[:, bass.ds(w, WINDOW)], dest[b][:, at_m], weight,
                                                       ALU.is_equal, ALU.mult)
                    last.then_inc(s_hot, 1)

                def add(j, v):
                    window = dve.snap(before, min_val=0, max_val=PADDED - 1)
                    dve.wait_ge(s_total, v)
                    dve.wait_ge(s_added, v)
                    out = k.sums_t[:, :, bass.ds(window, WINDOW)]
                    nc.vector.tensor_tensor(out, out, total[j][:, 0:KC * WINDOW].rearrange("p (a n) -> p a n", a=KC), ALU.add).then_inc(s_added, 1)

                def trip(i, rows):
                    for b in range(2):
                        dve.wait_ge(s_edge[b], 16 * i + 16)
                        nc.vector.tensor_copy(dest[b][:, :], edge[b][:, 1, :]).then_inc(s_dest, 1)
                        for j in range(2):
                            first = dve.value_load(k.windows[0:1, bass.ds(8 * i + 4 * b + 2 * j, 1)], min_val=0, max_val=PADDED - 1)
                            end = dve.value_load(k.windows[0:1, bass.ds(8 * i + 4 * b + 2 * j + 1, 1)], min_val=1, max_val=PADDED)
                            v = dve.snap(visit, min_val=1, max_val=1 << 20)
                            if j == 0:
                                dve.wait_ge(s_dest, 2 * i + b + 1)
                            build(b, j, first)
                            add(1 - j, v)
                            dve.reg_mov(before, first)
                            dve.reg_add(visit, visit, 1)
                            with dve.If(end > first + WINDOW):
                                with dve.Fori(first + WINDOW, end, WINDOW) as w:
                                    v = dve.snap(visit, min_val=1, max_val=1 << 20)
                                    add(j, v)
                                    build(b, j, w)
                                    dve.reg_mov(before, w)
                                    dve.reg_add(visit, visit, 1)
                            if work:
                                work.vector(i, 2 * b + j, rows)

                trips(dve, trip)
                add(1, dve.snap(visit, min_val=1, max_val=1 << 20))

            @block.tensor
            def _(pe):
                pe.sem_inc(s_free[0], 2)
                pe.sem_inc(s_free[1], 1)
                visit = pe.alloc_register(f"{name}_pe_visit")
                pe.reg_mov(visit, 1)

                def multiply(j):
                    for a in range(KC):
                        for m in range(SUB):
                            last = nc.tensor.matmul(total[j][:, a * WINDOW:(a + 1) * WINDOW], rows[:, j, m, a * P:(a + 1) * P], hot[:, j, m, :],
                                                    start=(m == 0), stop=(m == SUB - 1))
                    last.then_inc(s_total, 1)

                def trip(i, rows_of_tile):
                    for b in range(2):
                        for j in range(2):
                            first = pe.value_load(k.windows[0:1, bass.ds(8 * i + 4 * b + 2 * j, 1)], min_val=0, max_val=PADDED - 1)
                            end = pe.value_load(k.windows[0:1, bass.ds(8 * i + 4 * b + 2 * j + 1, 1)], min_val=1, max_val=PADDED)
                            v = pe.snap(visit, min_val=1, max_val=1 << 20)
                            pe.wait_ge(s_total, v)
                            pe.sem_inc(s_free[1 - j], 1)
                            if work:
                                work.tensor(i, 2 * b + j, rows_of_tile)
                            pe.wait_ge(s_hot, v)
                            pe.wait_ge(k.s_rows[j], gathered + 256 * i + 128 * b + 128)
                            multiply(j)
                            pe.reg_add(visit, visit, 1)
                            with pe.If(end > first + WINDOW):
                                with pe.Fori(first + WINDOW, end, WINDOW) as w:
                                    v = pe.snap(visit, min_val=1, max_val=1 << 20)
                                    pe.wait_ge(s_hot, v)
                                    multiply(j)
                                    pe.reg_add(visit, visit, 1)

                trips(pe, trip)

            if work:
                @block.scalar
                def _(act):
                    trips(act, work.scalar)


def residents(nc, k, ctx):
    sb = lambda name, shape, dt=F32: ctx.enter_context(nc.sbuf_tensor(name, shape, dt))
    k.carried = ctx.enter_context(nc.semaphore("carried_waits"))
    k.s_rows = [ctx.enter_context(nc.semaphore(f"rows_gathered{j}")) for j in range(2)]
    k.x = sb("x", [P, TILES, C])
    k.windows = sb("windows", [1, 2 * GROUPS], I32)
    k.norm = sb("norm", [P, TILES])
    k.ident = sb("ident", [P, P])
    k.ones = sb("ones", [P, P])
    k.half = sb("half", [P, 1])
    k.zero_b = sb("zero_b", [P, P], BF16)
    k.zero_wide = sb("zero_wide", [P, 512], BF16)
    k.raw = sb("raw", [P, TILES, 6])
    k.mean = sb("mean", [P, TILES])
    k.moment = sb("moment", [P, 2, TILES])
    k.rstd = sb("rstd", [P, TILES])
    k.key_sum = sb("key_sum", [P, C])
    k.mix0 = sb("mix0", [P, KC, C])
    k.slices = sb("slices", [P, 4, C])
    k.bn_scale = sb("bn_scale", [P, KC])
    k.bn_shift = sb("bn_shift", [P, KC])
    k.gate = sb("gate", [P, TILES, 2])
    k.slot = sb("slot", [P, TILES, 2], I32)
    k.expert_of = sb("expert_of", [P, SLOT_TILES], I32)
    k.s_scattered = ctx.enter_context(nc.semaphore("rows_scattered"))
    k.s_returned = [ctx.enter_context(nc.semaphore(f"rows_returned{u}")) for u in range(2)]
    k.s_stored = [ctx.enter_context(nc.semaphore(f"expert_rows_stored{u}")) for u in range(2)]
    k.mix1 = sb("mix1", [P, KC, C])


def wide_residents(nc, k, ctx):
    k.wide = wide = ctx.enter_context(nc.sbuf_tensor("wide", [P, TILES * 2 * C + KC * WINDOW], F32))
    n = KC * (PADDED + WINDOW)
    k.sums_t = wide[:, 0:n].rearrange("p (a n) -> p a n", a=KC)
    k.rows = wide[:, n:n + TILES * C].rearrange("p (t c) -> p t c", c=C)
    k.soft = wide[:, 0:TILES * 2 * C].rearrange("p (t c) -> p t c", c=2 * C)


def graph_residents(nc, k, ctx):
    k.node_id = ctx.enter_context(nc.sbuf_tensor("node_id", [P, PADDED + WINDOW], I16))


def row_stats(nc, k, t):
    return nc.vector.bn_stats(at(k.raw, t), at(k.x, t))


def row_moments(nc, dve, k, s_step):
    done = [0]

    def step(instruction):
        instruction.then_inc(s_step, 1)
        done[0] += 1
        dve.wait_ge(s_step, done[0])

    step(nc.vector.tensor_tensor(k.moment[:, 0, :], k.raw[:, :, 1], k.raw[:, :, 4], ALU.add))
    step(nc.vector.tensor_scalar(k.mean[:, :], k.moment[:, 0, :], 0.5, None, ALU.mult))
    step(nc.vector.tensor_tensor(k.moment[:, 0, :], k.raw[:, :, 1], k.mean[:, :], ALU.subtract))
    step(nc.vector.tensor_tensor(k.moment[:, 0, :], k.moment[:, 0, :], k.moment[:, 0, :], ALU.mult))
    step(nc.vector.tensor_tensor(k.moment[:, 1, :], k.raw[:, :, 2], k.raw[:, :, 5], ALU.add))
    step(nc.vector.scalar_tensor_tensor(k.moment[:, 1, :], k.moment[:, 1, :], 1.0 / C, k.moment[:, 0, :], ALU.mult, ALU.add))
    step(nc.vector.tensor_scalar(k.moment[:, 0, :], k.moment[:, 1, :], EPS, None, ALU.add))


MOMENTS = 7


def row_scale(nc, pool, k, s_step, s_rstd):
    pool.wait_ge(s_step, MOMENTS)
    nc.gpsimd.tensor_tensor(k.rstd[:, :], k.moment[:, 0, :], k.half[:, 0:1].to_broadcast([P, TILES]), ALU.pow).then_inc(s_rstd, 1)


def normalise(nc, k, out, t):
    return nc.vector.tensor_scalar(out, at(k.x, t), col(k.mean, t), col(k.rstd, t), ALU.subtract, ALU.mult)


def first_stats_stage(nc, k):
    with stage(nc) as (sb, pb, sem):
        s_stats, s_step, s_rstd = (sem(f"in_{n}") for n in ("stats", "moment_steps", "rstd"))
        with nc.Block() as block:
            @block.vector
            def _(dve):
                with dve.Fori(0, TILES) as t:
                    row_stats(nc, k, t).then_inc(s_stats, 1)
                dve.wait_ge(s_stats, TILES)
                row_moments(nc, dve, k, s_step)

            @block.gpsimd
            def _(pool):
                nc.gpsimd.iota(k.node_id[:, :], pattern=[[1, PADDED + WINDOW]], base=0, channel_multiplier=0,
                               allow_small_or_imprecise_dtypes=True)
                row_scale(nc, pool, k, s_step, s_rstd)


def keys_stage(nc, k):
    with stage(nc) as (sb, pb, sem):
        w = sb("ky_w", [P, KC, 2 * C])
        w_proj = sb("ky_wproj", [P, KC, C])
        xn = [sb(f"ky_xn{u}", [P, C]) for u in range(2)]
        xt = [sb(f"ky_xt{u}", [P, KC, P]) for u in range(2)]
        row = [sb(f"ky_row{u}", [P, C]) for u in range(2)]
        neg = [sb(f"ky_neg{u}", [P, C]) for u in range(2)]
        exp = [sb(f"ky_exp{u}", [P, C]) for u in range(2)]
        key = [sb(f"ky_key{u}", [P, C]) for u in range(2)]
        val = [sb(f"ky_val{u}", [P, C]) for u in range(2)]
        blocks = sb("ky_blocks", [P, P])
        ctx_t = sb("ky_ctx_t", [P, KC, P])
        turned = [pb(f"ky_turned{u}") for u in range(2)]
        kv = [pb(f"ky_kv{u}") for u in range(2)]
        context = pb("ky_context")
        keysum = pb("ky_keysum")
        proj = pb("ky_proj")
        s_stored = [sem(f"ky_table_stored{u}") for u in range(2)]
        s_w, s_done, s_ctx, s_m = (sem(f"ky_{n}") for n in ("weights_loaded", "context_ready", "context_masked", "mix_ready"))
        s_xn, s_kept, s_turned, s_xt, s_row, s_kv, s_neg, s_exp, s_val, s_key, s_sum = (sem(f"ky_{n}") for n in (
            "rows_ready", "rows_kept", "rows_turned", "turned_copied", "table_row", "kv_ready", "negative_ready",
            "exp_ready", "value_copied", "key_ready", "context_added"))
        with nc.Block() as block:
            @block.sync
            def _(sp):
                sp.dma_start(w[:, :, :], k.ins["L0_mix_WkvT"].rearrange("(k p) n -> p k n", p=P)).then_inc(s_w, 16)
                sp.dma_start(w_proj[:, :, :], k.ins["L0_mix_WprojT"].rearrange("(k p) n -> p k n", p=P)).then_inc(s_w, 16)
                sp.dma_start(blocks[:, :], k.ins["blocks32"]).then_inc(s_w, 16)
                for u in range(2):
                    sp.sem_inc(s_stored[u], 16)

                def head(t, u, i):
                    ready(sp, s_row, t)
                    sp.dma_start(table_rows(k, t), row[u][:, :]).then_inc(s_stored[u], 16)

                pipelined(sp, head, no_tail)
                sp.wait_ge(s_stored[0], 16 + 16 * (TILES // 2 + 1))
                sp.wait_ge(s_stored[1], 16 + 16 * (TILES // 2))

            @block.gpsimd
            def _(pool):
                start_at_two(pool, s_kept)

                def head(t, u, i):
                    ready(pool, s_xn, t)
                    nc.gpsimd.tensor_copy(at(k.rows, t), xn[u][:, :]).then_inc(s_kept, 1)

                pipelined(pool, head, no_tail)

            @block.vector
            def _(dve):
                start_at_two(dve, s_xn, s_neg, s_key)

                def head(t, u, i):
                    free(dve, s_turned, t)
                    free(dve, s_row, t)
                    free(dve, s_kept, t)
                    normalise(nc, k, xn[u][:, :], t).then_inc(s_xn, 1)

                def negative(t, u, rows):
                    ready(dve, s_kv, t)
                    free(dve, s_exp, t)
                    nc.vector.tensor_scalar(neg[u][:, :], kv[u][:, 0:C], 0.0, None, ALU.min).then_inc(s_neg, 1)

                def tail(t, u, rows):
                    ready(dve, s_exp, t)
                    ready(dve, s_val, t)
                    free(dve, s_sum, t)
                    nc.vector.scalar_tensor_tensor(key[u][:, :], kv[u][:, 0:C], 0.0, exp[u][:, :], ALU.max, ALU.add).then_inc(s_key, 1)

                pipelined(dve, no_head, tail, ahead=2, middle=negative, late=head)
                dve.wait_ge(s_done, 1)
                dve.wait_ge(s_w, 48)
                for a in range(KC):
                    nc.vector.tensor_tensor(ctx_t[:, a, :], context[:, a * P:(a + 1) * P], blocks[:, :], ALU.mult).then_inc(s_ctx, 1)
                nc.vector.tensor_copy(k.key_sum[:, :], keysum[:, 0:C])
                dve.wait_ge(s_m, 1)
                nc.vector.tensor_copy(k.mix0[:, :, :].rearrange("p k n -> p (k n)"), proj[:, :])

            @block.scalar
            def _(act):
                start_at_two(act, s_xt, s_row, s_exp, s_val)

                def head(t, u, i):
                    ready(act, s_turned, t)
                    free(act, s_kv, t)
                    nc.scalar.activation(xt[u][:, :, :].rearrange("p k n -> p (k n)"), turned[u][:, 0:C], ACT.Copy).then_inc(s_xt, 1)
                    ready(act, s_xn, t)
                    act.wait_ge(s_stored[u], 16 * i + 16)
                    nc.scalar.activation(row[u][:, :], xn[u][:, :], ACT.Copy, scale=col(k.norm, t)).then_inc(s_row, 1)

                def tail(t, u, rows):
                    ready(act, s_neg, t)
                    free(act, s_sum, t)
                    nc.scalar.activation(val[u][:, :], kv[u][:, C:2 * C], ACT.Copy).then_inc(s_val, 1)
                    free(act, s_key, t)
                    nc.scalar.activation(exp[u][:, :], neg[u][:, :], ACT.Exp).then_inc(s_exp, 1)

                pipelined(act, no_head, no_tail, ahead=2, middle=tail, late=head)

            @block.tensor
            def _(pe):
                start_at_two(pe, s_turned, s_kv, s_sum)
                for bank in (context, keysum):
                    nc.tensor.matmul(bank[:, 0:C], k.zero_b[:, :], k.zero_wide[:, 0:C], start=True, stop=False, skip_group_check=True)
                pe.wait_ge(s_w, 48)

                def head(t, u, i):
                    ready(pe, s_xn, t)
                    free(pe, s_xt, t)
                    for a in range(KC):
                        last = nc.tensor.transpose(turned[u][:, a * P:(a + 1) * P], xn[u][:, a * P:(a + 1) * P], k.ident[:, :])
                    last.then_inc(s_turned, 1)

                def keys_values(t, u, i):
                    ready(pe, s_xt, t)
                    free(pe, s_key, t)
                    free(pe, s_val, t)
                    for a in range(KC):
                        last = nc.tensor.matmul(kv[u][:, :], xt[u][:, a, :], w[:, a, :], start=(a == 0), stop=(a == KC - 1))
                    last.then_inc(s_kv, 1)

                def products(t, u, rows):
                    ready(pe, s_key, t)
                    ready(pe, s_val, t)
                    stop = rows == LAST
                    nc.tensor.matmul(keysum[:, 0:C], k.ones[0:rows, :], key[u][0:rows, :], start=False, stop=stop, skip_group_check=True)
                    for a in range(KC):
                        half = slice(a * P, (a + 1) * P)
                        last = nc.tensor.matmul(context[:, half], val[u][0:rows, half], key[u][0:rows, half], start=False, stop=stop,
                                                skip_group_check=True)
                    last.then_inc(s_sum, 1)

                pipelined(pe, head, no_tail, ahead=2, middle=products, late=keys_values)
                ready(pe, s_sum, TILES - 1)
                pe.sem_inc(s_done, 1)
                pe.wait_ge(s_ctx, KC)
                for a in range(KC):
                    last = nc.tensor.matmul(proj[:, a * C:(a + 1) * C], ctx_t[:, a, :], w_proj[:, a, :], start=True, stop=True)
                last.then_inc(s_m, 1)


def layer0_sums_and_attention(nc, k):
    with stage(nc) as (sb, pb, sem):
        spare = k.slices[:, :, :].rearrange("p q c -> p (q c)")
        wq = spare[:, 0:KC * C].rearrange("p (k n) -> p k n", k=KC)
        bias = spare[:, KC * C:(KC + 1) * C]
        rows_in = spare[:, (KC + 1) * C:(KC + 2) * C]
        rows_t = sb("at_rows_t", [P, KC, P])
        neg = sb("at_neg", [P, C])
        exp = sb("at_exp", [P, C])
        phi = sb("at_phi", [P, C])
        prod = sb("at_prod", [P, C])
        qn = sb("at_qn", [P, C])
        qn_t = sb("at_qn_t", [P, KC, P])
        den = sb("at_den", [P, 3, HEADS0])
        turned = pb("at_turned")
        query = pb("at_query")
        q_turned = pb("at_q_turned")
        out = pb("at_out")
        s_w = sem("at_weights_loaded")
        s_in, s_turned, s_t, s_q, s_neg, s_exp, s_phi, s_prod, s_den_sum, s_max, s_den, s_qn, s_qt, s_qnt, s_out, s_x, s_bias = (sem(f"at_{n}") for n in (
            "row_copied", "row_turned", "turned_copied", "query_ready", "negative_ready", "exp_ready", "phi_ready", "product_ready",
            "denominator_summed", "denominator_guarded", "denominator_inverted", "query_scaled", "query_turned", "query_copied", "out_ready",
            "out_added", "bias_added"))
        by_head = lambda ap: ap.rearrange("p (h d) -> p h d", h=HEADS0)
        with nc.Block() as block:
            @block.sync
            def _(sp):
                sp.dma_start(wq, k.ins["L0_mix_WqT"].rearrange("(k p) n -> p k n", p=P)).then_inc(s_w, 16)
                sp.dma_start(bias, k.ins["L0_mix_bproj"].partition_broadcast(P)).then_inc(s_w, 16)
                sp.wait_ge(s_w, 32)

            @block.tensor
            def _(pe):
                for s in (s_turned, s_t, s_q, s_phi, s_qt, s_qnt, s_out, s_x):
                    pe.sem_inc(s, 1)

        def scalar(t, rows):
            act = nc.scalar
            act.wait_ge(s_turned, t + 1)
            act.activation(rows_in, at(k.rows, t), ACT.Copy).then_inc(s_in, 1)
            act.wait_ge(s_turned, t + 2)
            act.wait_ge(s_q, t + 1)
            act.activation(rows_t[:, :, :].rearrange("p k n -> p (k n)"), turned[:, 0:C], ACT.Copy).then_inc(s_t, 1)
            act.wait_ge(s_neg, t + 1)
            act.activation(exp[:, :], neg[:, :], ACT.Exp).then_inc(s_exp, 1)
            act.wait_ge(s_qt, t + 2)
            act.wait_ge(s_out, t + 1)
            act.activation(qn_t[:, :, :].rearrange("p k n -> p (k n)"), q_turned[:, 0:C], ACT.Copy).then_inc(s_qnt, 1)

        def vector(t, group, rows):
            dve = nc.vector
            if group == 1:
                dve.wait_ge(s_q, t + 2)
                dve.tensor_scalar(neg[:, :], query[:, 0:C], 0.0, None, ALU.min).then_inc(s_neg, 1)
                dve.wait_ge(s_exp, t + 1)
                dve.scalar_tensor_tensor(phi[:, :], query[:, 0:C], 0.0, exp[:, :], ALU.max, ALU.add).then_inc(s_phi, 1)
                dve.wait_ge(s_phi, t + 2)
                dve.tensor_tensor(prod[:, :], phi[:, :], k.key_sum[:, :], ALU.mult).then_inc(s_prod, 1)
                dve.wait_ge(s_prod, t + 1)
                dve.tensor_reduce(den[:, 0, :], by_head(prod[:, :]), AX.X, ALU.add).then_inc(s_den_sum, 1)
                dve.wait_ge(s_den_sum, t + 1)
                dve.tensor_scalar(den[:, 1, :], den[:, 0, :], 1e-6, None, ALU.max).then_inc(s_max, 1)
                dve.wait_ge(s_max, t + 1)
                dve.reciprocal(den[:, 2, :], den[:, 1, :]).then_inc(s_den, 1)
                dve.wait_ge(s_den, t + 1)
                dve.wait_ge(s_qt, t + 1)
                dve.tensor_tensor(by_head(qn[:, :]), by_head(phi[:, :]), den[:, 2, :].unsqueeze(2).to_broadcast([P, HEADS0, HD0]), ALU.mult).then_inc(s_qn, 1)
            if group == 3:
                dve.wait_ge(s_out, t + 2)
                dve.tensor_tensor(at(k.x, t), at(k.x, t), out[:, 0:C], ALU.add).then_inc(s_x, 1)
                dve.wait_ge(s_x, t + 2)
                dve.tensor_tensor(at(k.x, t), at(k.x, t), bias, ALU.add).then_inc(s_bias, 1)

        def tensor(t, group, rows):
            pe = nc.tensor
            if group == 0:
                pe.wait_ge(s_in, t + 1)
                pe.wait_ge(s_t, t + 1)
                for a in range(KC):
                    last = pe.transpose(turned[:, a * P:(a + 1) * P], rows_in[:, a * P:(a + 1) * P], k.ident[:, :])
                last.then_inc(s_turned, 1)
            if group == 1:
                pe.wait_ge(s_t, t + 2)
                pe.wait_ge(s_phi, t + 1)
                for a in range(KC):
                    last = pe.matmul(query[:, 0:C], rows_t[:, a, :], wq[:, a, :], start=(a == 0), stop=(a == KC - 1))
                last.then_inc(s_q, 1)
            if group == 2:
                pe.wait_ge(s_qn, t + 1)
                pe.wait_ge(s_qnt, t + 1)
                for a in range(KC):
                    last = pe.transpose(q_turned[:, a * P:(a + 1) * P], qn[:, a * P:(a + 1) * P], k.ident[:, :])
                last.then_inc(s_qt, 1)
            if group == 3:
                pe.wait_ge(s_qnt, t + 2)
                pe.wait_ge(s_x, t + 1)
                for a in range(KC):
                    last = pe.matmul(out[:, 0:C], qn_t[:, a, :], k.mix0[:, a, :], start=(a == 0), stop=(a == KC - 1))
                last.then_inc(s_out, 1)

        edge_stage(nc, k, "e0", False, 0, Work(scalar, vector, tensor))


def first_update_stage(nc, k):
    with stage(nc) as (sb, pb, sem):
        wg = sb("fu_wg", [P, KC, C])
        agg_t = [sb(f"fu_sums_t{u}", [P, KC, P]) for u in range(2)]
        out = [pb(f"fu_out{u}") for u in range(2)]
        s_w = sem("fu_weights_loaded")
        s_agg, s_out, s_x, s_stats, s_step, s_rstd = (
            sem(f"fu_{n}") for n in ("sums_copied", "out_ready", "x_updated", "stats_ready", "moment_steps", "rstd"))
        with nc.Block() as block:
            @block.sync
            def _(sp):
                sp.dma_start(wg[:, :, :], k.ins["L0_gnn_W"].rearrange("(k p) n -> p k n", p=P)).then_inc(s_w, 16)

            @block.gpsimd
            def _(pool):
                row_scale(nc, pool, k, s_step, s_rstd)

            @block.vector
            def _(dve):
                start_at_two(dve, s_x, s_stats)

                def update(t, u, i):
                    ready(dve, s_out, t)
                    carry(dve, k)
                    nc.vector.scalar_tensor_tensor(at(k.x, t), out[u][:, 0:C], col(k.norm, t), at(k.x, t), ALU.mult, ALU.add).then_inc(s_x, 1)

                def statistics(t, u, rows):
                    ready(dve, s_x, t)
                    carry(dve, k)
                    row_stats(nc, k, t).then_inc(s_stats, 1)

                pipelined(dve, update, statistics)
                ready(dve, s_stats, TILES - 1)
                row_moments(nc, dve, k, s_step)

            @block.scalar
            def _(act):
                start_at_two(act, s_agg)

                def head(t, u, i):
                    free(act, s_out, t)
                    nc.scalar.activation(agg_t[u][:, :, :], nodes(k, t), ACT.Copy).then_inc(s_agg, 1)

                pipelined(act, head, no_tail)

            @block.tensor
            def _(pe):
                start_at_two(pe, s_out)
                pe.wait_ge(s_w, 16)

                def head(t, u, i):
                    ready(pe, s_agg, t)
                    free(pe, s_x, t)
                    for a in range(KC):
                        last = nc.tensor.matmul(out[u][:, 0:C], agg_t[u][:, a, :], wg[:, a, :], start=(a == 0), stop=(a == KC - 1))
                    last.then_inc(s_out, 1)

                pipelined(pe, head, no_tail)


def slice_weights_stage(nc, k):
    with stage(nc) as (sb, pb, sem):
        wx_t = sb("sl_wx_t", [P, 4, C])
        pair = sb("sl_pair", [P, P])
        bx = sb("sl_bx", [P, 4])
        bx_wide = sb("sl_bx_wide", [P, 4, P])
        b_slice = sb("sl_b", [P, 2 * C])
        temp = sb("sl_temp", [P, SH])
        clipped = sb("sl_clipped", [P, SH])
        inv = sb("sl_inv", [P, SH])
        summed = sb("sl_summed", [P, 2 * C])
        mats = [pb(f"sl_mat{a}") for a in range(KC)]
        row = pb("sl_row")
        s_w, s_clip, s_inv, s_wide, s_mat, s_b = (sem(f"sl_{n}") for n in ("loaded", "clipped", "inverted", "bias_wide", "products", "bias_summed"))
        with nc.Block() as block:
            @block.sync
            def _(sp):
                sp.dma_start(wx_t[:, :, :], k.ins["L0_ffn_W_xT"].rearrange("(q p) c -> p q c", p=P)).then_inc(s_w, 16)
                sp.dma_start(pair[:, :], k.ins["pair_slice"]).then_inc(s_w, 16)
                sp.dma_start(bx[:, :], k.ins["L0_ffn_b_x4"]).then_inc(s_w, 16)
                sp.dma_start(b_slice[:, :], k.ins["b_slice8"].partition_broadcast(P)).then_inc(s_w, 16)
                sp.dma_start(temp[:, :], k.ins["temperature"].partition_broadcast(P)).then_inc(s_w, 16)

            @block.vector
            def _(dve):
                dve.wait_ge(s_w, 80)
                nc.vector.tensor_scalar(clipped[:, :], temp[:, :], 0.1, 5.0, ALU.max, ALU.min).then_inc(s_clip, 1)
                for q in range(4):
                    last = nc.vector.tensor_scalar(bx_wide[:, q, :], k.ones[:, :], bx[:, q:q + 1], None, ALU.mult)
                last.then_inc(s_wide, 1)
                dve.wait_ge(s_clip, 1)
                nc.vector.reciprocal(inv[:, :], clipped[:, :]).then_inc(s_inv, 1)
                dve.wait_ge(s_mat, 1)
                dve.wait_ge(s_inv, 1)
                inv_wide = inv[:, :].unsqueeze(2).to_broadcast([P, SH, SLICES])
                for a in range(KC):
                    nc.vector.tensor_tensor(k.w_slice[:, a, :].rearrange("p (h g) -> p h g", h=SH),
                                            mats[a][:, :].rearrange("p (h g) -> p h g", h=SH), inv_wide, ALU.mult)
                nc.vector.tensor_tensor(summed[:, :], row[:, :], b_slice[:, :], ALU.add).then_inc(s_b, 1)
                dve.wait_ge(s_b, 1)
                nc.vector.tensor_tensor(k.b_slice[:, :].rearrange("p (h g) -> p h g", h=SH),
                                        summed[:, :].rearrange("p (h g) -> p h g", h=SH), inv_wide, ALU.mult)

            @block.tensor
            def _(pe):
                pe.wait_ge(s_w, 80)
                pe.wait_ge(s_wide, 1)
                for q in range(4):
                    cols = slice(q * P, (q + 1) * P)
                    for a in range(KC):
                        nc.tensor.matmul(mats[a][:, cols], wx_t[:, q, a * P:(a + 1) * P], pair[:, :], start=True, stop=True)
                    last = nc.tensor.matmul(row[:, cols], bx_wide[:, q, :], pair[:, :], start=True, stop=True)
                last.then_inc(s_mat, 1)


def slices_stage(nc, k, token, logits):
    with stage(nc) as (sb, pb, sem):
        xn = [sb(f"sw_xn{u}", [P, C]) for u in range(2)]
        xk = [sb(f"sw_xk{u}", [P, C + 1]) for u in range(2)]
        xt = [sb(f"sw_xt{u}", [P, KC, P]) for u in range(2)]
        logit = [sb(f"sw_logit{u}", [P, 2 * C]) for u in range(2)]
        top = [sb(f"sw_top{u}", [P, SH]) for u in range(2)]
        exp = [sb(f"sw_exp{u}", [P, 2 * C]) for u in range(2)]
        den = [sb(f"sw_den{u}", [P, 2, SH]) for u in range(2)]
        soft = [sb(f"sw_soft{u}", [P, 2 * C]) for u in range(2)]
        turned = [pb(f"sw_turned{u}") for u in range(2)]
        s_one, s_xn, s_turned, s_xt, s_lg, s_biased, s_top, s_off, s_exp, s_sum, s_inv, s_soft, s_kept, s_tok, s_xk = (sem(f"sw_{n}") for n in (
            "ones_set", "rows_ready", "rows_turned", "turned_copied", "logits_ready", "bias_added", "maximum_ready", "maximum_subtracted",
            "exp_ready", "exp_summed", "sum_inverted", "softmax_ready", "softmax_kept", "tokens_added", "rows_copied"))
        by_head = lambda ap: ap.rearrange("p (h g) -> p h g", h=SH)
        wide = lambda ap: ap.unsqueeze(2).to_broadcast([P, SH, SLICES])
        with nc.Block() as block:
            @block.gpsimd
            def _(pool):
                start_at_two(pool, s_kept)

                def head(t, u, i):
                    pass

                def tail(t, u, rows):
                    ready(pool, s_soft, t)
                    nc.gpsimd.tensor_copy(at(k.soft, t), soft[u][:, :]).then_inc(s_kept, 1)

                pipelined(pool, head, tail)

            @block.vector
            def _(dve):
                start_at_two(dve, s_xn, s_biased, s_top, s_off, s_sum, s_inv, s_soft)
                for u in range(2):
                    nc.vector.memset(xk[u][:, C:C + 1], 1.0).then_inc(s_one, 1)

                def rows(t, u):
                    free(dve, s_turned, t)
                    free(dve, s_xk, t)
                    normalise(nc, k, xn[u][:, :], t).then_inc(s_xn, 1)

                def logits_less_maximum(t, u):
                    ready(dve, s_lg, t)
                    free(dve, s_off, t)
                    nc.vector.tensor_tensor(logit[u][:, :], logits[u][:, :], k.b_slice[:, :], ALU.add).then_inc(s_biased, 1)
                    ready(dve, s_biased, t)
                    nc.vector.tensor_reduce(top[u][:, :], by_head(logit[u][:, :]), AX.X, ALU.max).then_inc(s_top, 1)
                    ready(dve, s_top, t)
                    free(dve, s_soft, t)
                    nc.vector.tensor_tensor(by_head(logit[u][:, :]), by_head(logit[u][:, :]), wide(top[u][:, :]), ALU.subtract).then_inc(s_off, 1)

                def tail(t, u, rows):
                    ready(dve, s_exp, t)
                    nc.vector.tensor_reduce(den[u][:, 0, :], by_head(exp[u][:, :]), AX.X, ALU.add).then_inc(s_sum, 1)
                    ready(dve, s_sum, t)
                    nc.vector.reciprocal(den[u][:, 1, :], den[u][:, 0, :]).then_inc(s_inv, 1)
                    ready(dve, s_inv, t)
                    free(dve, s_tok, t)
                    free(dve, s_kept, t)
                    nc.vector.tensor_tensor(by_head(soft[u][:, :]), by_head(exp[u][:, :]), wide(den[u][:, 1, :]), ALU.mult).then_inc(s_soft, 1)

                three_deep(dve, rows, logits_less_maximum, tail)

            @block.scalar
            def _(act):
                start_at_two(act, s_xt, s_exp, s_xk)

                def copy_turned(t, u):
                    ready(act, s_turned, t)
                    free(act, s_lg, t)
                    nc.scalar.activation(xt[u][:, :, :].rearrange("p k n -> p (k n)"), turned[u][:, 0:C], ACT.Copy).then_inc(s_xt, 1)

                def exponentials(t, u):
                    ready(act, s_off, t)
                    free(act, s_soft, t)
                    nc.scalar.activation(exp[u][:, :], logit[u][:, :], ACT.Exp).then_inc(s_exp, 1)
                    ready(act, s_xn, t)
                    free(act, s_tok, t)
                    nc.scalar.activation(xk[u][:, 0:C], xn[u][:, :], ACT.Copy).then_inc(s_xk, 1)

                three_deep(act, copy_turned, exponentials, no_tail)

            @block.tensor
            def _(pe):
                start_at_two(pe, s_turned, s_lg, s_tok)
                for q in range(4):
                    nc.tensor.matmul(token[q][:, 0:C + 1], k.zero_b[:, :], k.zero_wide[:, 0:C + 1], start=True, stop=False, skip_group_check=True)

                def turn_and_multiply(t, u):
                    ready(pe, s_xn, t)
                    free(pe, s_xt, t)
                    for a in range(KC):
                        last = nc.tensor.transpose(turned[u][:, a * P:(a + 1) * P], xn[u][:, a * P:(a + 1) * P], k.ident[:, :])
                    last.then_inc(s_turned, 1)
                    ready(pe, s_xt, t)
                    free(pe, s_biased, t)
                    for a in range(KC):
                        last = nc.tensor.matmul(logits[u][:, :], xt[u][:, a, :], k.w_slice[:, a, :], start=(a == 0), stop=(a == KC - 1))
                    last.then_inc(s_lg, 1)

                def add_tokens(t, u, rows):
                    ready(pe, s_xk, t)
                    ready(pe, s_soft, t)
                    pe.wait_ge(s_one, 2)
                    for q in range(4):
                        last = nc.tensor.matmul(token[q][:, 0:C + 1], soft[u][0:rows, q * P:(q + 1) * P], xk[u][0:rows, :], start=False,
                                                stop=(rows == LAST), skip_group_check=True)
                    last.then_inc(s_tok, 1)

                three_deep(pe, turn_and_multiply, lambda t, u: None, add_tokens)


def slices_and_attention(nc, k):
    with stage(nc) as (sb, pb, sem):
        token = [pb(f"sw_token{q}") for q in range(4)]
        logits = [pb(f"sw_logits{u}") for u in range(2)]
        slices_stage(nc, k, token, logits)
        slice_attention(nc, k, token, logits)


def slice_attention(nc, k, token, ps):
    with stage(nc) as (sb, pb, sem):
        w_fx = sb("sa_wfx", [P, KC, 2 * C])
        b_fx = sb("sa_bfx", [P, 4, P])
        pairs = sb("sa_pairs", [P, 3, P])
        w_out = sb("sa_wout", [P, 4, C])
        mask = sb("sa_mask", [P, P])
        tok = sb("sa_tok", [P, 4, C + 1])
        tok_t = sb("sa_tok_t", [P, 2, P])
        den = sb("sa_den", [P, 2])
        bterm = sb("sa_bterm", [P, P])
        fx = sb("sa_fx", [P, P])
        fx2 = sb("sa_fx2", [P, P])
        st = sb("sa_st", [P, P])
        st_t = sb("sa_st_t", [P, P])
        q_t = sb("sa_q_t", [P, P])
        k_t = sb("sa_k_t", [P, P])
        v = sb("sa_v", [P, P])
        sc = sb("sa_sc", [P, HD1])
        stat = sb("sa_stat", [P, 3])
        ex = sb("sa_ex", [P, HD1])
        att = sb("sa_att", [P, P])
        att_t = sb("sa_att_t", [P, P])
        o_t = sb("sa_o_t", [P, P])
        s_w, s_v, s_p, s_a = (sem(f"sa_{n}") for n in ("weights_loaded", "vector_steps", "tensor_steps", "exp_steps"))
        V, T = 20, 8
        with nc.Block() as block:
            @block.sync
            def _(sp):
                sp.dma_start(w_fx[:, :, :], k.ins["L0_ffn_W_fx"].rearrange("(k p) n -> p k n", p=P)).then_inc(s_w, 16)
                sp.dma_start(b_fx[:, :, :].rearrange("p q d -> p (q d)"), k.ins["L0_ffn_b_fx"].partition_broadcast(P)).then_inc(s_w, 16)
                sp.dma_start(pairs[:, :, :], k.ins["pair_qkv"].rearrange("i p d -> p i d")).then_inc(s_w, 16)
                sp.dma_start(w_out[:, :, :], k.ins["L0_ffn_W_out"].rearrange("(q p) c -> p q c", p=P)).then_inc(s_w, 16)
                sp.dma_start(mask[:, :], k.ins["blocks64"]).then_inc(s_w, 16)

            @block.vector
            def _(dve):
                nc.vector.memset(att[:, :], 0.0).then_inc(s_v, 1)
                for q in range(4):
                    last = nc.vector.tensor_copy(tok[:, q, :], token[q][:, 0:C + 1])
                last.then_inc(s_v, 1)
                dve.wait_ge(s_w, 80)
                for q in range(4):
                    done = [2 + V * q]

                    def step(instruction):
                        instruction.then_inc(s_v, 1)
                        done[0] += 1
                        dve.wait_ge(s_v, done[0])

                    dve.wait_ge(s_v, 2 + V * q)
                    step(nc.vector.tensor_scalar(den[:, 0:1], tok[:, q, C:C + 1], 1e-5, None, ALU.add))
                    step(nc.vector.reciprocal(den[:, 1:2], den[:, 0:1]))
                    step(nc.vector.tensor_scalar(bterm[:, :], b_fx[:, q, :], tok[:, q, C:C + 1], None, ALU.mult))
                    dve.wait_ge(s_p, T * q + 1)
                    step(nc.vector.tensor_copy(tok_t[:, :, :].rearrange("p a g -> p (a g)"), ps[0][:, 0:C]))
                    dve.wait_ge(s_p, T * q + 2)
                    step(nc.vector.tensor_tensor(fx[:, :], ps[1][:, 0:P], bterm[:, :], ALU.add))
                    step(nc.vector.tensor_scalar(fx2[:, :], fx[:, :], den[:, 1:2], None, ALU.mult))
                    step(nc.vector.tensor_tensor(st[:, :], fx2[:, :], mask[:, :], ALU.mult))
                    dve.wait_ge(s_p, T * q + 3)
                    step(nc.vector.tensor_copy(st_t[:, :], ps[0][:, 0:P]))
                    dve.wait_ge(s_p, T * q + 4)
                    step(nc.vector.tensor_copy(q_t[:, :], ps[1][:, 0:P]))
                    step(nc.vector.tensor_copy(k_t[:, :], ps[1][:, P:2 * P]))
                    step(nc.vector.tensor_copy(v[:, :], ps[1][:, 2 * P:3 * P]))
                    dve.wait_ge(s_p, T * q + 5)
                    nc.vector.tensor_scalar(sc[0:64, :], ps[0][0:64, 0:64], 64 ** -0.5, None, ALU.mult)
                    step(nc.vector.tensor_scalar(sc[64:P, :], ps[0][64:P, 64:P], 64 ** -0.5, None, ALU.mult))
                    step(nc.vector.tensor_reduce(stat[:, 0:1], sc[:, :], AX.X, ALU.max))
                    step(nc.vector.tensor_scalar(sc[:, :], sc[:, :], stat[:, 0:1], None, ALU.subtract))
                    dve.wait_ge(s_a, q + 1)
                    step(nc.vector.tensor_reduce(stat[:, 1:2], ex[:, :], AX.X, ALU.add))
                    step(nc.vector.reciprocal(stat[:, 2:3], stat[:, 1:2]))
                    nc.vector.tensor_scalar(att[0:64, 0:64], ex[0:64, :], stat[0:64, 2:3], None, ALU.mult)
                    step(nc.vector.tensor_scalar(att[64:P, 64:P], ex[64:P, :], stat[64:P, 2:3], None, ALU.mult))
                    dve.wait_ge(s_p, T * q + 6)
                    step(nc.vector.tensor_copy(att_t[:, :], ps[1][:, 0:P]))
                    dve.wait_ge(s_p, T * q + 7)
                    step(nc.vector.tensor_copy(o_t[:, :], ps[0][:, 0:P]))
                    dve.wait_ge(s_p, T * q + 8)
                    step(nc.vector.tensor_copy(k.slices[:, q, :], ps[1][:, 0:C]))
                    assert done[0] == 2 + V * (q + 1)

            @block.scalar
            def _(act):
                for q in range(4):
                    act.wait_ge(s_v, 2 + V * q + 14)
                    nc.scalar.activation(ex[:, :], sc[:, :], ACT.Exp).then_inc(s_a, 1)

            @block.tensor
            def _(pe):
                pe.wait_ge(s_w, 80)
                for q in range(4):
                    base = 2 + V * q
                    pair = slice(q * P, (q + 1) * P)
                    pe.wait_ge(s_v, base)
                    for a in range(KC):
                        last = nc.tensor.transpose(ps[0][:, a * P:(a + 1) * P], tok[:, q, a * P:(a + 1) * P], k.ident[:, :])
                    last.then_inc(s_p, 1)
                    pe.wait_ge(s_v, base + 4)
                    for a in range(KC):
                        last = nc.tensor.matmul(ps[1][:, 0:P], tok_t[:, a, :], w_fx[:, a, pair], start=(a == 0), stop=(a == KC - 1))
                    last.then_inc(s_p, 1)
                    pe.wait_ge(s_v, base + 7)
                    nc.tensor.transpose(ps[0][:, 0:P], st[:, :], k.ident[:, :]).then_inc(s_p, 1)
                    pe.wait_ge(s_v, base + 8)
                    nc.tensor.matmul(ps[1][:, 0:P], pairs[:, 0, :], st_t[:, :], start=True, stop=True)
                    nc.tensor.matmul(ps[1][:, P:2 * P], pairs[:, 1, :], st_t[:, :], start=True, stop=True)
                    nc.tensor.matmul(ps[1][:, 2 * P:3 * P], st_t[:, :], pairs[:, 2, :], start=True, stop=True).then_inc(s_p, 1)
                    pe.wait_ge(s_v, base + 11)
                    nc.tensor.matmul(ps[0][:, 0:P], q_t[:, :], k_t[:, :], start=True, stop=True).then_inc(s_p, 1)
                    pe.wait_ge(s_v, base + 17)
                    nc.tensor.transpose(ps[1][:, 0:P], att[:, :], k.ident[:, :]).then_inc(s_p, 1)
                    pe.wait_ge(s_v, base + 18)
                    nc.tensor.matmul(ps[0][:, 0:P], v[:, :], att_t[:, :], start=True, stop=True).then_inc(s_p, 1)
                    pe.wait_ge(s_v, base + 19)
                    nc.tensor.matmul(ps[1][:, 0:C], o_t[:, :], w_out[:, q, :], start=True, stop=True).then_inc(s_p, 1)


def second_update_stage(nc, k):
    with stage(nc) as (sb, pb, sem):
        bias = sb("su_bias", [P, C])
        soft = [sb(f"su_soft{u}", [P, 2 * C]) for u in range(2)]
        soft_t = [sb(f"su_soft_t{u}", [P, 4, P]) for u in range(2)]
        turned = [pb(f"su_turned{u}") for u in range(2)]
        out = [pb(f"su_out{u}") for u in range(2)]
        s_w, s_zeros = sem("su_bias_loaded"), sem("su_zeros_stored")
        s_soft, s_turned, s_copied, s_out, s_add, s_x, s_stats, s_step, s_rstd = (sem(f"su_{n}") for n in (
            "softmax_copied", "softmax_turned", "turned_copied", "out_ready", "out_added", "x_updated", "stats_ready", "moment_steps", "rstd"))
        with nc.Block() as block:
            @block.sync
            def _(sp):
                sp.dma_start(bias[:, :], k.ins["L0_ffn_b_out"].partition_broadcast(P)).then_inc(s_w, 16)
                sp.dma_start(k.expert_in.rearrange("(s p) c -> p s c", p=P),
                             k.zero_wide[:, :].bitcast(F32).unsqueeze(1).to_broadcast([P, SLOT_TILES, C])).then_inc(s_zeros, 16)
                sp.wait_ge(s_zeros, 16)

            @block.gpsimd
            def _(pool):
                start_at_two(pool, s_soft)

                def head(t, u, i):
                    free(pool, s_turned, t)
                    nc.gpsimd.tensor_copy(soft[u][:, :], at(k.soft, t)).then_inc(s_soft, 1)

                pipelined(pool, head, no_tail)
                row_scale(nc, pool, k, s_step, s_rstd)

            @block.vector
            def _(dve):
                start_at_two(dve, s_add, s_x, s_stats)
                dve.wait_ge(s_w, 16)

                def tail(t, u, rows):
                    ready(dve, s_out, t)
                    nc.vector.tensor_tensor(at(k.x, t), at(k.x, t), out[u][:, 0:C], ALU.add).then_inc(s_add, 1)
                    ready(dve, s_add, t)
                    nc.vector.tensor_tensor(at(k.x, t), at(k.x, t), bias[:, :], ALU.add).then_inc(s_x, 1)
                    ready(dve, s_x, t)
                    carry(dve, k)
                    row_stats(nc, k, t).then_inc(s_stats, 1)

                pipelined(dve, no_head, tail)
                ready(dve, s_stats, TILES - 1)
                row_moments(nc, dve, k, s_step)

            @block.scalar
            def _(act):
                start_at_two(act, s_copied)

                def head(t, u, i):
                    ready(act, s_turned, t)
                    free(act, s_out, t)
                    nc.scalar.activation(soft_t[u][:, :, :].rearrange("p k n -> p (k n)"), turned[u][:, :], ACT.Copy).then_inc(s_copied, 1)

                pipelined(act, head, no_tail)

            @block.tensor
            def _(pe):
                start_at_two(pe, s_turned, s_out)

                def head(t, u, i):
                    ready(pe, s_soft, t)
                    free(pe, s_copied, t)
                    for a in range(4):
                        last = nc.tensor.transpose(turned[u][:, a * P:(a + 1) * P], soft[u][:, a * P:(a + 1) * P], k.ident[:, :])
                    last.then_inc(s_turned, 1)

                def tail(t, u, rows):
                    ready(pe, s_copied, t)
                    free(pe, s_add, t)
                    for q in range(4):
                        last = nc.tensor.matmul(out[u][:, 0:C], soft_t[u][:, q, :], k.slices[:, q, :], start=(q == 0), stop=(q == 3))
                    last.then_inc(s_out, 1)

                pipelined(pe, head, tail)


def layer1_sums_and_attention(nc, k):
    with stage(nc) as (sb, pb, sem):
        product = pb("la_product")
        keysum = pb("la_keysum")
        turned = pb("la_turned")
        kv_ps = pb("la_kv_ps")
        w = k.slices[:, :, :].rearrange("p q c -> p (q c)").rearrange("p (a n) -> p a n", a=KC)
        rows_in = sb("la_rows", [P, C])
        rows_t = sb("la_rows_t", [P, KC, P])
        bn = sb("la_bn", [P, 8, 6])
        mv = sb("la_mv", [P, 8, 2])
        rs = sb("la_rs", [P, 3, 8])
        kv = sb("la_kv", [P, 2 * C])
        s_w = sem("la_kv_weights_loaded")
        s_in, s_turned, s_t, s_ps, s_bn, s_mv, s_eps, s_mid, s_root, s_rs, s_kv, s_sum = (sem(f"la_{n}") for n in (
            "row_copied", "row_turned", "turned_copied", "kv_products", "bn_ready", "variance_ready", "eps_added", "mean_subtracted", "root_ready",
            "scale_ready", "kv_ready", "product_added"))
        by_head = lambda ap: ap.rearrange("p (h d) -> p h d", d=HD1)
        with nc.Block() as block:
            @block.sync
            def _(sp):
                sp.dma_start(w, k.ins["L1_mix_wkvT"].rearrange("(k p) n -> p k n", p=P)).then_inc(s_w, 16)
                sp.wait_ge(s_w, 16)

            @block.tensor
            def _(pe):
                for bank in (product, keysum):
                    nc.tensor.matmul(bank[:, 0:C + KC], k.zero_b[:, :], k.zero_wide[:, 0:C + KC], start=True, stop=False, skip_group_check=True)
                for s in (s_turned, s_t, s_ps, s_mid, s_sum):
                    pe.sem_inc(s, 1)

        def scalar(t, rows):
            act = nc.scalar
            act.wait_ge(s_turned, t + 1)
            act.activation(rows_in[:, :], at(k.rows, t), ACT.Copy).then_inc(s_in, 1)
            act.wait_ge(s_turned, t + 2)
            act.wait_ge(s_ps, t + 1)
            act.activation(rows_t[:, :, :].rearrange("p k n -> p (k n)"), turned[:, 0:C], ACT.Copy).then_inc(s_t, 1)
            act.wait_ge(s_eps, t + 1)
            act.activation(rs[:, 1, :], rs[:, 0, :], ACT.Sqrt).then_inc(s_root, 1)

        def vector(t, group, rows):
            dve = nc.vector
            if group == 2:
                dve.wait_ge(s_ps, t + 2)
                for h in range(8):
                    last = dve.bn_stats(bn[:, h, :], kv_ps[:, HD1 * h:HD1 * (h + 1)])
                last.then_inc(s_bn, 1)
                dve.wait_ge(s_bn, t + 1)
                carry(dve, k)
                for h in range(8):
                    last = dve.bn_aggr(mv[:, h, :], bn[:, h, :])
                last.then_inc(s_mv, 1)
                dve.wait_ge(s_mv, t + 1)
                dve.tensor_scalar(rs[:, 0, :], mv[:, :, 1], EPS, None, ALU.add).then_inc(s_eps, 1)
                dve.wait_ge(s_sum, t + 1)
                dve.tensor_tensor(by_head(kv[:, :]), by_head(kv_ps[:, :]), mv[:, :, 0].unsqueeze(2).to_broadcast([P, 8, HD1]),
                                  ALU.subtract).then_inc(s_mid, 1)
                dve.wait_ge(s_root, t + 1)
                dve.reciprocal(rs[:, 2, :], rs[:, 1, :]).then_inc(s_rs, 1)
                dve.wait_ge(s_rs, t + 1)
                dve.wait_ge(s_mid, t + 2)
                dve.tensor_tensor(by_head(kv[:, :]), by_head(kv[:, :]), rs[:, 2, :].unsqueeze(2).to_broadcast([P, 8, HD1]), ALU.mult).then_inc(s_kv, 1)

        def tensor(t, group, rows):
            pe = nc.tensor
            if group == 0:
                pe.wait_ge(s_in, t + 1)
                pe.wait_ge(s_t, t + 1)
                for a in range(KC):
                    last = pe.transpose(turned[:, a * P:(a + 1) * P], rows_in[:, a * P:(a + 1) * P], k.ident[:, :])
                last.then_inc(s_turned, 1)
            if group == 1:
                pe.wait_ge(s_t, t + 2)
                pe.wait_ge(s_mid, t + 1)
                for a in range(KC):
                    last = pe.matmul(kv_ps[:, :], rows_t[:, a, :], w[:, a, :], start=(a == 0), stop=(a == KC - 1))
                last.then_inc(s_ps, 1)
            if group == 3:
                pe.wait_ge(s_kv, t + 1)
                stop = rows == LAST
                pe.matmul(keysum[:, 0:C], k.ones[0:rows, :], kv[0:rows, 0:C], start=False, stop=stop, skip_group_check=True)
                for a in range(KC):
                    values = kv[0:rows, C + a * P:C + (a + 1) * P]
                    pe.matmul(product[:, a * P:(a + 1) * P], values, kv[0:rows, a * P:(a + 1) * P], start=False, stop=stop, skip_group_check=True)
                    last = pe.matmul(product[:, C + a:C + a + 1], values, k.ones[0:rows, 0:1], start=False, stop=stop, skip_group_check=True)
                last.then_inc(s_sum, 1)

        edge_stage(nc, k, "e1", True, 1, Work(scalar, vector, tensor))
        attention_matrix(nc, k, product, keysum, [turned, kv_ps])


def table1_stage(nc, k):
    with stage(nc) as (sb, pb, sem):
        w = sb("ta_w", [P, KC, C])
        b1 = sb("ta_b1", [P, C])
        xn = [sb(f"ta_xn{u}", [P, C]) for u in range(2)]
        xt = [sb(f"ta_xt{u}", [P, KC, P]) for u in range(2)]
        pre = [sb(f"ta_pre{u}", [P, C]) for u in range(2)]
        row = [sb(f"ta_row{u}", [P, C]) for u in range(2)]
        turned = [pb(f"ta_turned{u}") for u in range(2)]
        out = [pb(f"ta_out{u}") for u in range(2)]
        s_stored = [sem(f"ta_table_stored{u}") for u in range(2)]
        s_w = sem("ta_weights_loaded")
        s_xn, s_kept, s_turned, s_xt, s_h, s_pre, s_row = (sem(f"ta_{n}") for n in (
            "rows_ready", "rows_kept", "rows_turned", "turned_copied", "products_ready", "bias_added", "table_row"))
        with nc.Block() as block:
            @block.sync
            def _(sp):
                sp.dma_start(w[:, :, :], k.ins["L1_gnn_c1_w1"].rearrange("(k p) n -> p k n", p=P)).then_inc(s_w, 16)
                sp.dma_start(b1[:, :], k.ins["L1_gnn_c1_b1"].partition_broadcast(P)).then_inc(s_w, 16)
                for u in range(2):
                    sp.sem_inc(s_stored[u], 16)

                def tail(t, u, rows):
                    ready(sp, s_row, t)
                    sp.dma_start(table_rows(k, t), row[u][:, :]).then_inc(s_stored[u], 16)

                pipelined(sp, no_head, tail)
                sp.wait_ge(s_stored[0], 16 + 16 * (TILES // 2 + 1))
                sp.wait_ge(s_stored[1], 16 + 16 * (TILES // 2))

            @block.gpsimd
            def _(pool):
                start_at_two(pool, s_kept)

                def head(t, u, i):
                    ready(pool, s_xn, t)
                    nc.gpsimd.tensor_copy(at(k.rows, t), xn[u][:, :]).then_inc(s_kept, 1)

                pipelined(pool, head, no_tail)

            @block.vector
            def _(dve):
                start_at_two(dve, s_xn, s_pre)
                dve.wait_ge(s_w, 32)

                def head(t, u, i):
                    free(dve, s_turned, t)
                    free(dve, s_kept, t)
                    normalise(nc, k, xn[u][:, :], t).then_inc(s_xn, 1)

                def tail(t, u, rows):
                    ready(dve, s_h, t)
                    free(dve, s_row, t)
                    nc.vector.tensor_tensor(pre[u][:, :], out[u][:, 0:C], b1[:, :], ALU.add).then_inc(s_pre, 1)

                pipelined(dve, head, tail, ahead=2)

            @block.scalar
            def _(act):
                start_at_two(act, s_xt, s_row)

                def head(t, u, i):
                    ready(act, s_turned, t)
                    free(act, s_h, t)
                    nc.scalar.activation(xt[u][:, :, :].rearrange("p k n -> p (k n)"), turned[u][:, 0:C], ACT.Copy).then_inc(s_xt, 1)

                def tail(t, u, rows):
                    ready(act, s_pre, t)
                    act.wait_ge(s_stored[u], 8 * (t - u) + 16)
                    nc.scalar.activation(row[u][:, :], pre[u][:, :], ACT.Relu).then_inc(s_row, 1)

                pipelined(act, head, tail, ahead=2)

            @block.tensor
            def _(pe):
                start_at_two(pe, s_turned, s_h)
                pe.wait_ge(s_w, 32)

                def head(t, u, i):
                    ready(pe, s_xn, t)
                    free(pe, s_xt, t)
                    for a in range(KC):
                        last = nc.tensor.transpose(turned[u][:, a * P:(a + 1) * P], xn[u][:, a * P:(a + 1) * P], k.ident[:, :])
                    last.then_inc(s_turned, 1)

                def tail(t, u, rows):
                    ready(pe, s_xt, t)
                    free(pe, s_pre, t)
                    for a in range(KC):
                        last = nc.tensor.matmul(out[u][:, 0:C], xt[u][:, a, :], w[:, a, :], start=(a == 0), stop=(a == KC - 1))
                    last.then_inc(s_h, 1)

                pipelined(pe, head, tail)


def attention_matrix(nc, k, product, keysum, ps):
    with stage(nc) as (sb, pb, sem):
        wq = sb("am_wq", [P, KC, C])
        wo = sb("am_wo", [P, KC, C])
        key_rows = sb("am_key_rows", [P, 2, P])
        val_cols = sb("am_val_cols", [P, 2])
        mask = sb("am_mask", [P, P])
        t0 = sb("am_t0", [P, KC, P])
        t1 = sb("am_t1", [P, KC, P])
        t2 = sb("am_t2", [P, KC, P])
        t3 = sb("am_t3", [P, KC, P])
        kv_t = sb("am_kv_t", [P, KC, P])
        half = sb("am_half", [P, KC, C])
        s_w, s_v, s_p = (sem(f"am_{n}") for n in ("weights_loaded", "vector_steps", "tensor_steps"))
        with nc.Block() as block:
            @block.sync
            def _(sp):
                sp.dma_start(wq[:, :, :], k.ins["L1_mix_wq"].rearrange("(k p) n -> p k n", p=P)).then_inc(s_w, 16)
                sp.dma_start(wo[:, :, :], k.ins["L1_mix_woT"].rearrange("(k p) n -> p k n", p=P)).then_inc(s_w, 16)
                sp.dma_start(key_rows[:, 0, :], k.ins["key_g2"].partition_broadcast(P)).then_inc(s_w, 16)
                sp.dma_start(key_rows[:, 1, :], k.ins["key_b2"].partition_broadcast(P)).then_inc(s_w, 16)
                sp.dma_start(val_cols[:, :], k.ins["val_gb2"]).then_inc(s_w, 16)
                sp.dma_start(mask[:, :], k.ins["blocks64"]).then_inc(s_w, 16)

            @block.vector
            def _(dve):
                dve.wait_ge(s_w, 96)
                for a in range(KC):
                    part = slice(a * P, (a + 1) * P)
                    gk, bk = key_rows[:, 0, :], key_rows[:, 1, :]
                    gv, bv = val_cols[:, 0:1], val_cols[:, 1:2]
                    done = [9 * a]

                    def step(instruction):
                        instruction.then_inc(s_v, 1)
                        done[0] += 1
                        dve.wait_ge(s_v, done[0])

                    step(nc.vector.tensor_scalar(t0[:, a, :], product[:, part], gv, None, ALU.mult))
                    step(nc.vector.tensor_scalar(t1[:, a, :], keysum[:, part], bv, None, ALU.mult))
                    step(nc.vector.tensor_tensor(t0[:, a, :], t0[:, a, :], t1[:, a, :], ALU.add))
                    step(nc.vector.tensor_tensor(t0[:, a, :], t0[:, a, :], gk, ALU.mult))
                    step(nc.vector.tensor_scalar(t2[:, a, 0:1], product[:, C + a:C + a + 1], gv, None, ALU.mult))
                    step(nc.vector.scalar_tensor_tensor(t3[:, a, 0:1], bv, float(NODES), t2[:, a, 0:1], ALU.mult, ALU.add))
                    step(nc.vector.scalar_tensor_tensor(t1[:, a, :], bk, t3[:, a, 0:1], t0[:, a, :], ALU.mult, ALU.add))
                    step(nc.vector.scalar_tensor_tensor(kv_t[:, a, :], t1[:, a, :], 1.0 / NODES, mask[:, :], ALU.mult, ALU.mult))
                    dve.wait_ge(s_p, a + 1)
                    step(nc.vector.tensor_copy(half[:, a, :], ps[0][:, a * C:(a + 1) * C]))
                dve.wait_ge(s_p, KC + 1)
                nc.vector.tensor_copy(k.mix1[:, :, :].rearrange("p k n -> p (k n)"), ps[1][:, :])

            @block.tensor
            def _(pe):
                pe.wait_ge(s_w, 96)
                for a in range(KC):
                    pe.wait_ge(s_v, 9 * a + 8)
                    nc.tensor.matmul(ps[0][:, a * C:(a + 1) * C], kv_t[:, a, :], wo[:, a, :], start=True, stop=True).then_inc(s_p, 1)
                pe.wait_ge(s_v, 9 * KC)
                for b in range(KC):
                    for a in range(KC):
                        last = nc.tensor.matmul(ps[1][:, b * C:(b + 1) * C], wq[:, a, b * P:(b + 1) * P], half[:, a, :], start=(a == 0), stop=(a == KC - 1))
                last.then_inc(s_p, 1)


def node_stats_scale(nc, k, name, stats, gamma, beta, scale, shift):
    with stage(nc) as (sb, pb, sem):
        mv = sb(f"{name}_mv", [P, KC, 2])
        par = sb(f"{name}_par", [P, 2, KC])
        tmp = sb(f"{name}_tmp", [P, 3, KC])
        s_w, s_v, s_p = (sem(f"{name}_{n}") for n in ("parameters", "vector_steps", "pool_steps"))
        with nc.Block() as block:
            @block.sync
            def _(sp):
                sp.dma_start(par[:, 0, :], gamma).then_inc(s_w, 16)
                sp.dma_start(par[:, 1, :], beta).then_inc(s_w, 16)

            @block.gpsimd
            def _(pool):
                pool.wait_ge(s_v, 1)
                nc.gpsimd.tensor_scalar(tmp[:, 0, :], mv[:, :, 1], EPS, None, ALU.add).then_inc(s_p, 1)
                pool.wait_ge(s_p, 1)
                nc.gpsimd.tensor_tensor(tmp[:, 1, :], tmp[:, 0, :], k.half[:, 0:1].to_broadcast([P, KC]), ALU.pow).then_inc(s_p, 1)

            @block.vector
            def _(dve):
                for a in range(KC):
                    last = nc.vector.bn_aggr(mv[:, a, :], stats[:, a, :, :].rearrange("p t s -> p (t s)"))
                last.then_inc(s_v, 1)
                dve.wait_ge(s_w, 32)
                dve.wait_ge(s_p, 2)
                nc.vector.tensor_tensor(scale, tmp[:, 1, :], par[:, 0, :], ALU.mult).then_inc(s_v, 1)
                dve.wait_ge(s_v, 2)
                nc.vector.tensor_tensor(tmp[:, 2, :], scale, mv[:, :, 0], ALU.mult).then_inc(s_v, 1)
                dve.wait_ge(s_v, 3)
                nc.vector.tensor_tensor(shift, par[:, 1, :], tmp[:, 2, :], ALU.subtract)


def convolve_stage(nc, k, name, w2_in, b2_in, gamma1, beta1, gamma2, beta2, scale, shift):
    CHUNK = 448
    CHUNKS = PADDED // CHUNK
    SHORT = NODES - (CHUNKS - 1) * CHUNK
    chunk = lambda c: k.sums_t[:, :, c * CHUNK:(c + 1) * CHUNK] if isinstance(c, int) else k.sums_t[:, :, bass.ds(c * CHUNK, CHUNK)]
    with stage(nc) as (sb, pb, sem):
        w2 = sb(f"{name}_w2", [P, KC, C])
        b2 = sb(f"{name}_b2", [P, KC])
        stats = sb(f"{name}_stats", [P, KC, CHUNKS, 6])
        scale1 = sb(f"{name}_scale1", [P, KC])
        shift1 = sb(f"{name}_shift1", [P, KC])
        out = [[pb(f"{name}_out{u}{a}") for a in range(KC)] for u in range(2)]
        s_w = sem(f"{name}_weights_loaded")
        s_out, s_h, s_stats = (sem(f"{name}_{n}") for n in ("out_ready", "h_ready", "stats_ready"))
        with nc.Block() as block:
            @block.sync
            def _(sp):
                sp.dma_start(w2[:, :, :], w2_in.rearrange("(k p) n -> p k n", p=P)).then_inc(s_w, 16)
                sp.dma_start(b2[:, :], b2_in).then_inc(s_w, 16)

            @block.vector
            def _(dve):
                def tail(c, u, last_chunk):
                    ready(dve, s_h, c)
                    chunk_stats = stats[:, :, c:c + 1, :] if isinstance(c, int) else stats[:, :, bass.ds(c, 1), :]
                    carry(dve, k)
                    for a in range(KC):
                        last = nc.vector.bn_stats(chunk_stats[:, a, 0, :], chunk(c)[:, a, 0:SHORT if last_chunk else CHUNK])
                    last.then_inc(s_stats, 1)

                pipelined_chunks(dve, CHUNKS, no_head, tail)

            @block.scalar
            def _(act):
                start_at_two(act, s_h)
                act.wait_ge(s_w, 32)

                def tail(c, u, last_chunk):
                    ready(act, s_out, c)
                    for a in range(KC):
                        last = nc.scalar.activation(chunk(c)[:, a, :], out[u][a][:, 0:CHUNK], ACT.Identity, bias=b2[:, a:a + 1])
                    last.then_inc(s_h, 1)

                pipelined_chunks(act, CHUNKS, no_head, tail)

            @block.tensor
            def _(pe):
                start_at_two(pe, s_out)
                pe.wait_ge(s_w, 32)

                def head(c, u, i):
                    free(pe, s_h, c)
                    for a in range(KC):
                        for b in range(KC):
                            last = nc.tensor.matmul(out[u][a][:, 0:CHUNK], w2[:, b, a * P:(a + 1) * P], chunk(c)[:, b, :], start=(b == 0), stop=(b == KC - 1))
                    last.then_inc(s_out, 1)

                pipelined_chunks(pe, CHUNKS, head, no_tail)

        node_stats_scale(nc, k, f"{name}_bn1", stats, gamma1, beta1, scale1[:, :], shift1[:, :])
        s_y = sem(f"{name}_relu_ready")
        with nc.Block() as block:
            @block.scalar
            def _(act):
                for c in range(CHUNKS):
                    for a in range(KC):
                        part = chunk(c)[:, a, :]
                        last = nc.scalar.activation(part, part, ACT.Relu, bias=shift1[:, a:a + 1], scale=scale1[:, a:a + 1])
                    last.then_inc(s_y, 1)

            @block.vector
            def _(dve):
                for c in range(CHUNKS):
                    dve.wait_ge(s_y, c + 1)
                    for a in range(KC):
                        nc.vector.bn_stats(stats[:, a, c, :], chunk(c)[:, a, 0:SHORT if c == CHUNKS - 1 else CHUNK])
        node_stats_scale(nc, k, f"{name}_bn2", stats, gamma2, beta2, scale[:, :], shift[:, :])


def table2_stage(nc, k, scale, shift):
    with stage(nc) as (sb, pb, sem):
        w1 = sb("tb_w1", [P, KC, C])
        b1 = sb("tb_b1", [P, C])
        h_t = [sb(f"tb_h_t{u}", [P, KC, P]) for u in range(2)]
        pre = [sb(f"tb_pre{u}", [P, C]) for u in range(2)]
        row = [sb(f"tb_row{u}", [P, C]) for u in range(2)]
        out = [pb(f"tb_out{u}") for u in range(2)]
        s_stored = [sem(f"tb_table_stored{u}") for u in range(2)]
        s_w, s_h, s_out, s_pre, s_row = (sem(f"tb_{n}") for n in ("weights_loaded", "h_ready", "out_ready", "bias_added", "table_row"))
        with nc.Block() as block:
            @block.sync
            def _(sp):
                sp.dma_start(w1[:, :, :], k.ins["L1_gnn_c2_w1"].rearrange("(k p) n -> p k n", p=P)).then_inc(s_w, 16)
                sp.dma_start(b1[:, :], k.ins["L1_gnn_c2_b1"].partition_broadcast(P)).then_inc(s_w, 16)
                for u in range(2):
                    sp.sem_inc(s_stored[u], 16)

                def tail(t, u, rows):
                    ready(sp, s_row, t)
                    sp.dma_start(table_rows(k, t), row[u][:, :]).then_inc(s_stored[u], 16)

                pipelined(sp, no_head, tail)
                sp.wait_ge(s_stored[0], 16 + 16 * (TILES // 2 + 1))
                sp.wait_ge(s_stored[1], 16 + 16 * (TILES // 2))

            @block.vector
            def _(dve):
                start_at_two(dve, s_pre, s_row)
                dve.wait_ge(s_w, 32)

                def tail(t, u, rows):
                    ready(dve, s_out, t)
                    nc.vector.tensor_tensor(pre[u][:, :], out[u][:, 0:C], b1[:, :], ALU.add).then_inc(s_pre, 1)
                    ready(dve, s_pre, t)
                    dve.wait_ge(s_stored[u], 8 * (t - u) + 16)
                    nc.vector.tensor_scalar(row[u][:, :], pre[u][:, :], 0.0, None, ALU.max).then_inc(s_row, 1)

                pipelined(dve, no_head, tail)

            @block.scalar
            def _(act):
                start_at_two(act, s_h)

                def head(t, u, i):
                    free(act, s_out, t)
                    for a in range(KC):
                        last = nc.scalar.activation(h_t[u][:, a, :], nodes(k, t)[:, a, :], ACT.Relu, bias=shift[:, a:a + 1], scale=scale[:, a:a + 1])
                    last.then_inc(s_h, 1)

                pipelined(act, head, no_tail)

            @block.tensor
            def _(pe):
                start_at_two(pe, s_out)
                pe.wait_ge(s_w, 32)

                def head(t, u, i):
                    ready(pe, s_h, t)
                    free(pe, s_pre, t)
                    for a in range(KC):
                        last = nc.tensor.matmul(out[u][:, 0:C], h_t[u][:, a, :], w1[:, a, :], start=(a == 0), stop=(a == KC - 1))
                    last.then_inc(s_out, 1)

                pipelined(pe, head, no_tail)


def layer1_second_sums(nc, k):
    with stage(nc) as (sb, pb, sem):
        bias = sb("as_bias", [P, C])
        rows_in = sb("as_rows", [P, C])
        rows_t = sb("as_rows_t", [P, KC, P])
        turned = pb("as_turned")
        out = pb("as_out")
        s_w = sem("as_bias_loaded")
        s_in, s_turned, s_t, s_out, s_x, s_bias = (sem(f"as_{n}") for n in (
            "row_copied", "row_turned", "turned_copied", "out_ready", "out_added", "bias_added"))
        with nc.Block() as block:
            @block.sync
            def _(sp):
                sp.dma_start(bias[:, :], k.ins["L1_mix_bo"].partition_broadcast(P)).then_inc(s_w, 16)
                sp.wait_ge(s_w, 16)

            @block.tensor
            def _(pe):
                for s in (s_turned, s_t, s_out, s_x):
                    pe.sem_inc(s, 1)

        def scalar(t, rows):
            act = nc.scalar
            act.wait_ge(s_turned, t + 1)
            act.activation(rows_in[:, :], at(k.rows, t), ACT.Copy).then_inc(s_in, 1)
            act.wait_ge(s_turned, t + 2)
            act.wait_ge(s_out, t + 1)
            act.activation(rows_t[:, :, :].rearrange("p k n -> p (k n)"), turned[:, 0:C], ACT.Copy).then_inc(s_t, 1)

        def vector(t, group, rows):
            dve = nc.vector
            if group == 3:
                dve.wait_ge(s_out, t + 2)
                dve.tensor_tensor(at(k.x, t), at(k.x, t), out[:, 0:C], ALU.add).then_inc(s_x, 1)
                dve.wait_ge(s_x, t + 2)
                dve.tensor_tensor(at(k.x, t), at(k.x, t), bias[:, :], ALU.add).then_inc(s_bias, 1)

        def tensor(t, group, rows):
            pe = nc.tensor
            if group == 0:
                pe.wait_ge(s_in, t + 1)
                pe.wait_ge(s_t, t + 1)
                for a in range(KC):
                    last = pe.transpose(turned[:, a * P:(a + 1) * P], rows_in[:, a * P:(a + 1) * P], k.ident[:, :])
                last.then_inc(s_turned, 1)
            if group == 1:
                pe.wait_ge(s_t, t + 2)
                pe.wait_ge(s_x, t + 1)
                for a in range(KC):
                    last = pe.matmul(out[:, 0:C], rows_t[:, a, :], k.mix1[:, a, :], start=(a == 0), stop=(a == KC - 1))
                last.then_inc(s_out, 1)

        edge_stage(nc, k, "e2", True, 2, Work(scalar, vector, tensor))


def third_update_stage(nc, k, scale, shift):
    with stage(nc) as (sb, pb, sem):
        h_t = [sb(f"tu_h_t{u}", [P, KC, P]) for u in range(2)]
        res = [sb(f"tu_res{u}", [P, C]) for u in range(2)]
        turned = [pb(f"tu_turned{u}") for u in range(2)]
        s_h, s_turned, s_res, s_relu, s_stats, s_step, s_rstd = (sem(f"tu_{n}") for n in (
            "h_ready", "turned", "residual_added", "relu_added", "stats_ready", "moment_steps", "rstd"))
        with nc.Block() as block:
            @block.gpsimd
            def _(pool):
                row_scale(nc, pool, k, s_step, s_rstd)

            @block.vector
            def _(dve):
                start_at_two(dve, s_res, s_relu, s_stats)

                def head(t, u, i):
                    ready(dve, s_turned, t)
                    free(dve, s_relu, t)
                    nc.vector.tensor_tensor(res[u][:, :], turned[u][:, 0:C], at(k.rows, t), ALU.add).then_inc(s_res, 1)

                def add_residual(t, u, rows):
                    ready(dve, s_res, t)
                    nc.vector.scalar_tensor_tensor(at(k.x, t), res[u][:, :], 0.0, at(k.x, t), ALU.max, ALU.add).then_inc(s_relu, 1)

                def tail(t, u, rows):
                    ready(dve, s_relu, t)
                    carry(dve, k)
                    row_stats(nc, k, t).then_inc(s_stats, 1)

                pipelined(dve, no_head, tail, ahead=2, middle=add_residual, late=head)
                ready(dve, s_stats, TILES - 1)
                row_moments(nc, dve, k, s_step)

            @block.scalar
            def _(act):
                start_at_two(act, s_h)

                def head(t, u, i):
                    free(act, s_turned, t)
                    for a in range(KC):
                        last = nc.scalar.activation(h_t[u][:, a, :], nodes(k, t)[:, a, :], ACT.Identity, bias=shift[:, a:a + 1], scale=scale[:, a:a + 1])
                    last.then_inc(s_h, 1)

                pipelined(act, head, no_tail)

            @block.tensor
            def _(pe):
                start_at_two(pe, s_turned)

                def head(t, u, i):
                    ready(pe, s_h, t)
                    free(pe, s_res, t)
                    for a in range(KC):
                        last = nc.tensor.transpose(turned[u][:, a * P:(a + 1) * P], h_t[u][:, a, :], k.ident[:, :])
                    last.then_inc(s_turned, 1)

                pipelined(pe, head, no_tail)


def router_stage(nc, k):
    E = EXPERTS
    with stage(nc) as (sb, pb, sem):
        wr = sb("ro_wr", [P, KC, E])
        br = sb("ro_br", [P, E])
        gb = sb("ro_gb", [P, 2, C])
        z = [sb(f"ro_z{u}", [P, C]) for u in range(2)]
        zg = [sb(f"ro_zg{u}", [P, C]) for u in range(2)]
        xn = [sb(f"ro_xn{u}", [P, C]) for u in range(2)]
        xt = [sb(f"ro_xt{u}", [P, KC, P]) for u in range(2)]
        logit = sb("ro_logit", [P, TILES, E])
        turned = [pb(f"ro_turned{u}") for u in range(2)]
        logits = [pb(f"ro_logits{u}") for u in range(2)]
        s_w = sem("ro_weights_loaded")
        s_z, s_zg, s_xn, s_turned, s_xt, s_kept, s_lg, s_logit = (sem(f"ro_{n}") for n in (
            "z_ready", "scaled", "rows_ready", "rows_turned", "turned_copied", "turned_kept", "logits_ready", "bias_added"))
        with nc.Block() as block:
            @block.sync
            def _(sp):
                sp.dma_start(wr[:, :, :], k.ins["L1_ffn_Wr"].rearrange("(k p) n -> p k n", p=P)).then_inc(s_w, 16)
                sp.dma_start(br[:, :], k.ins["L1_ffn_br"].partition_broadcast(P)).then_inc(s_w, 16)
                sp.dma_start(gb[:, 0, :], k.ins["L1_ffn_gamma"].partition_broadcast(P)).then_inc(s_w, 16)
                sp.dma_start(gb[:, 1, :], k.ins["L1_ffn_beta"].partition_broadcast(P)).then_inc(s_w, 16)

            @block.gpsimd
            def _(pool):
                start_at_two(pool, s_kept)

                def head(t, u, i):
                    ready(pool, s_xn, t)
                    nc.gpsimd.tensor_copy(at(k.rows, t), xn[u][:, :]).then_inc(s_kept, 1)

                pipelined(pool, head, no_tail)

            @block.vector
            def _(dve):
                start_at_two(dve, s_z, s_zg, s_xn, s_logit)
                dve.wait_ge(s_w, 64)

                def head(t, u, i):
                    free(dve, s_zg, t)
                    normalise(nc, k, z[u][:, :], t).then_inc(s_z, 1)
                    ready(dve, s_z, t)
                    free(dve, s_xn, t)
                    nc.vector.tensor_tensor(zg[u][:, :], z[u][:, :], gb[:, 0, :], ALU.mult).then_inc(s_zg, 1)
                    ready(dve, s_zg, t)
                    free(dve, s_turned, t)
                    free(dve, s_kept, t)
                    nc.vector.tensor_tensor(xn[u][:, :], zg[u][:, :], gb[:, 1, :], ALU.add).then_inc(s_xn, 1)

                def tail(t, u, rows):
                    ready(dve, s_lg, t)
                    nc.vector.tensor_tensor(at(logit, t), logits[u][:, 0:E], br[:, :], ALU.add).then_inc(s_logit, 1)

                pipelined(dve, head, tail, ahead=2)

            @block.scalar
            def _(act):
                start_at_two(act, s_xt)

                def head(t, u, i):
                    ready(act, s_turned, t)
                    free(act, s_lg, t)
                    nc.scalar.activation(xt[u][:, :, :].rearrange("p k n -> p (k n)"), turned[u][:, 0:C], ACT.Copy).then_inc(s_xt, 1)

                pipelined(act, head, no_tail)

            @block.tensor
            def _(pe):
                start_at_two(pe, s_turned, s_lg)
                pe.wait_ge(s_w, 64)

                def head(t, u, i):
                    ready(pe, s_xn, t)
                    free(pe, s_xt, t)
                    for a in range(KC):
                        last = nc.tensor.transpose(turned[u][:, a * P:(a + 1) * P], xn[u][:, a * P:(a + 1) * P], k.ident[:, :])
                    last.then_inc(s_turned, 1)

                def tail(t, u, rows):
                    ready(pe, s_xt, t)
                    free(pe, s_logit, t)
                    for a in range(KC):
                        last = nc.tensor.matmul(logits[u][:, 0:E], xt[u][:, a, :], wr[:, a, :], start=(a == 0), stop=(a == KC - 1))
                    last.then_inc(s_lg, 1)

                pipelined(pe, head, tail)

        place_rows(nc, k, logit)


def place_rows(nc, k, logit):
    E = EXPERTS
    wide3 = [P, TILES, E]
    with stage(nc) as (sb, pb, sem):
        rank, cmp, exp, gates, mask, pos = (sb(f"pl_{n}", wide3) for n in ("rank", "cmp", "exp", "gates", "mask", "pos"))
        sums = [sb(f"pl_sums{u}", wide3) for u in range(2)]
        top = sb("pl_top", [P, TILES])
        den = sb("pl_den", [P, 2, TILES])
        picked = sb("pl_picked", [P, 2, TILES])
        before = sb("pl_before", [P, P])
        full = sb("pl_full", [P, E])
        full_i = sb("pl_full_i", [P, 2, E], I32)
        base = sb("pl_base", [P, 2, E])
        number = sb("pl_number", [P, SLOT_TILES])
        of = sb("pl_of", [P, SLOT_TILES])
        earlier = pb("pl_earlier")
        in_tile = pb("pl_in_tile")
        s_v, s_e, s_c, s_m, s_p = (sem(f"pl_{n}") for n in ("vector_steps", "exp_ready", "constants", "mask_ready", "prefix_ready"))
        with nc.Block() as block:
            @block.vector
            def _(dve):
                done = [0]

                def step(instruction):
                    instruction.then_inc(s_v, 1)
                    done[0] += 1
                    dve.wait_ge(s_v, done[0])

                step(nc.vector.tensor_reduce(top[:, :], logit[:, :, :], AX.X, ALU.max))
                step(nc.vector.tensor_tensor(exp[:, :, :], logit[:, :, :], top[:, :].unsqueeze(2).to_broadcast(wide3), ALU.subtract))
                step(nc.vector.memset(rank[:, :, :], 0.0))
                for other in range(E):
                    them = logit[:, :, other:other + 1]
                    if other:
                        step(nc.vector.tensor_tensor(cmp[:, :, 0:other], them.to_broadcast([P, TILES, other]), logit[:, :, 0:other], ALU.is_gt))
                        step(nc.vector.tensor_tensor(rank[:, :, 0:other], rank[:, :, 0:other], cmp[:, :, 0:other], ALU.add))
                    if other < E - 1:
                        n = E - 1 - other
                        step(nc.vector.tensor_tensor(cmp[:, :, 0:n], them.to_broadcast([P, TILES, n]), logit[:, :, other + 1:E], ALU.is_ge))
                        step(nc.vector.tensor_tensor(rank[:, :, other + 1:E], rank[:, :, other + 1:E], cmp[:, :, 0:n], ALU.add))
                nc.vector.tensor_scalar(mask[:, :, :], rank[:, :, :], 2.0, None, ALU.is_lt).then_inc(s_m, 1)
                dve.wait_ge(s_m, 1)
                dve.wait_ge(s_e, 1)
                step(nc.vector.tensor_tensor(gates[:, :, :], mask[:, :, :], exp[:, :, :], ALU.mult))
                step(nc.vector.tensor_reduce(den[:, 0, :], gates[:, :, :], AX.X, ALU.add))
                step(nc.vector.reciprocal(den[:, 1, :], den[:, 0, :]))
                step(nc.vector.tensor_tensor(gates[:, :, :], gates[:, :, :], den[:, 1, :].unsqueeze(2).to_broadcast(wide3), ALU.mult))
                tile_sums = in_tile[:, 0:TILES * E].rearrange("p (t e) -> p t e", e=E)
                dve.wait_ge(s_p, 2)
                step(nc.vector.tensor_copy(sums[0][:, :, :], tile_sums))
                u, reach = 0, 1
                while reach < TILES:
                    a, b = sums[u], sums[1 - u]
                    step(nc.vector.tensor_tensor(b[:, reach:, :], a[:, reach:, :], a[:, 0:TILES - reach, :], ALU.add))
                    step(nc.vector.tensor_copy(b[:, 0:reach, :], a[:, 0:reach, :]))
                    u, reach = 1 - u, 2 * reach
                total = sums[u]
                step(nc.vector.tensor_scalar(full_i[:, 0, :], total[:, TILES - 1, :], float(P - 1), None, ALU.add))
                step(nc.vector.tensor_scalar(full_i[:, 1, :], full_i[:, 0, :], 7, None, ALU.arith_shift_right))
                step(nc.vector.tensor_copy(full[:, :], full_i[:, 1, :]))
                step(nc.vector.memset(base[:, 0, :], 0.0))
                for e in range(1, E):
                    step(nc.vector.tensor_tensor(base[:, 0, e:e + 1], base[:, 0, e - 1:e], full[:, e - 1:e], ALU.add))
                step(nc.vector.tensor_scalar(base[:, 1, :], base[:, 0, :], float(P), None, ALU.mult))
                step(nc.vector.tensor_tensor(pos[:, :, :], total[:, :, :], tile_sums, ALU.subtract))
                step(nc.vector.tensor_tensor(pos[:, :, :], pos[:, :, :], earlier[:, 0:TILES * E].rearrange("p (t e) -> p t e", e=E), ALU.add))
                step(nc.vector.tensor_tensor(pos[:, :, :], pos[:, :, :], base[:, 1, :].unsqueeze(1).to_broadcast(wide3), ALU.add))
                for r in range(2):
                    step(nc.vector.tensor_scalar(mask[:, :, :], rank[:, :, :], float(r), None, ALU.is_equal))
                    step(nc.vector.tensor_tensor(cmp[:, :, :], mask[:, :, :], pos[:, :, :], ALU.mult))
                    step(nc.vector.tensor_reduce(picked[:, r, :], cmp[:, :, :], AX.X, ALU.add))
                    step(nc.vector.tensor_copy(k.slot[:, :, r], picked[:, r, :]))
                    step(nc.vector.tensor_tensor(cmp[:, :, :], mask[:, :, :], gates[:, :, :], ALU.mult))
                    step(nc.vector.tensor_reduce(picked[:, r, :], cmp[:, :, :], AX.X, ALU.add))
                    step(nc.vector.tensor_copy(k.gate[:, :, r], picked[:, r, :]))
                dve.wait_ge(s_c, 3)
                step(nc.vector.memset(of[:, :], 0.0))
                for e in range(1, E):
                    step(nc.vector.scalar_tensor_tensor(of[:, :], number[:, :], base[:, 0, e:e + 1], of[:, :], ALU.is_ge, ALU.add))
                step(nc.vector.tensor_copy(k.expert_of[:, :], of[:, :]))

            @block.scalar
            def _(act):
                act.wait_ge(s_v, 2)
                nc.scalar.activation(exp[:, :, :], exp[:, :, :], ACT.Exp).then_inc(s_e, 1)

            @block.gpsimd
            def _(pool):
                nc.gpsimd.memset(before[:, :], 0.0).then_inc(s_c, 1)
                nc.gpsimd.iota(number[:, :], pattern=[[1, SLOT_TILES]], base=0, channel_multiplier=0,
                               allow_small_or_imprecise_dtypes=True).then_inc(s_c, 1)
                pool.wait_ge(s_c, 1)
                nc.gpsimd.affine_select(out=before[:, :], in_=before[:, :], compare_op=ALU.is_ge, fill=1.0, base=0,
                                        pattern=[[-1, P]], channel_multiplier=1).then_inc(s_c, 1)

            @block.tensor
            def _(pe):
                pe.wait_ge(s_m, 1)
                pe.wait_ge(s_c, 3)
                for bank, weights in ((earlier, before), (in_tile, k.ones)):
                    nc.tensor.matmul(bank[:, 0:TILES * E], weights[:, :], mask[:, :, :].rearrange("p t e -> p (t e)"),
                                     start=True, stop=True).then_inc(s_p, 1)


def experts_stage(nc, k):
    with stage(nc) as (sb, pb, sem):
        place = [0]

        def cut(n):
            place[0] += n
            return k.wide[:, place[0] - n:place[0]]

        w1 = cut(EXPERTS * KC * HID).rearrange("p (e k n) -> p e k n", e=EXPERTS, k=KC)
        b1 = cut(EXPERTS * HID).rearrange("p (e n) -> p e n", e=EXPERTS)
        w2 = sb("ex_w2", [P, EXPERTS, FT, C])
        s_w = sem("ex_weights_loaded")
        scatter_stage(nc, k, w1, w2, b1, s_w)
        place[0] = KC * (PADDED + WINDOW)
        b2 = cut(EXPERTS * C).rearrange("p (e n) -> p e n", e=EXPERTS)
        multiply_stage(nc, k, cut, w1, w2, b1, b2, s_w)
        return_stage(nc, k)


def scatter_stage(nc, k, w1, w2, b1, s_w):
    with nc.Block() as block:
        @block.sync
        def _(sp):
            for e in range(EXPERTS):
                sp.dma_start(w1[:, e], k.ins["L1_ffn_W1"][e].rearrange("(k p) n -> p k n", p=P)).then_inc(s_w, 16)
                sp.dma_start(b1[:, e], k.ins["L1_ffn_b1"][e].partition_broadcast(P)).then_inc(s_w, 16)
                sp.dma_start(w2[:, e], k.ins["L1_ffn_W2"][e].rearrange("(k p) n -> p k n", p=P)).then_inc(s_w, 16)

        @block.gpsimd
        def _(pool):
            for t in range(TILES):
                for r in range(2):
                    nc.gpsimd.indirect_dma_start(out=k.expert_in, out_offset=bass.IndirectOffsetOnAxis(ap=k.slot[:, t, r:r + 1], axis=0),
                                                 in_=k.rows[:, t, :], in_offset=None).then_inc(k.s_scattered, 16)
            pool.wait_ge(k.s_scattered, 2 * TILES * 16)


def multiply_stage(nc, k, cut, w1, w2, b1, b2, s_w):
    with stage(nc) as (sb, pb, sem):
        rows = [cut(C) for u in range(2)]
        rows_t = [cut(C).rearrange("p (a n) -> p a n", a=KC) for u in range(2)]
        pre = [cut(HID) for u in range(2)]
        hid = [cut(HID) for u in range(2)]
        hid_t = [cut(HID).rearrange("p (f n) -> p f n", f=FT) for u in range(2)]
        y = [cut(C) for u in range(2)]
        turned = [pb(f"ex_turned{u}") for u in range(2)]
        up = [pb(f"ex_up{u}") for u in range(2)]
        hid_turned = [pb(f"ex_hid_turned{u}") for u in range(2)]
        down = [pb(f"ex_down{u}") for u in range(2)]
        s_rows = [sem(f"ex_rows_loaded{u}") for u in range(2)]
        s_b2 = sem("ex_b2_loaded")
        s_turned, s_rows_t, s_up, s_pre, s_hid, s_ht, s_hid_t, s_down, s_y, s_done = (sem(f"ex_{n}") for n in (
            "rows_turned", "turned_copied", "up_ready", "bias_added", "hidden_ready", "hidden_turned", "hidden_copied", "down_ready", "y_ready", "y_stored"))
        slots = lambda dram, t: dram[t * P:(t + 1) * P, :] if isinstance(t, int) else dram[bass.ds(t * P, P), :]

        def expert(engine, t):
            at_t = slice(t, t + 1) if isinstance(t, int) else bass.ds(t, 1)
            return engine.value_load(k.expert_of[0:1, at_t], min_val=0, max_val=EXPERTS - 1)

        with nc.Block() as block:
            @block.sync
            def _(sp):
                sp.dma_start(b2.rearrange("p e n -> p (e n)"), k.ins["L1_ffn_b2"].rearrange("e n -> (e n)").partition_broadcast(P)).then_inc(s_b2, 16)
                with sp.Fori(0, SLOT_TILES // 2) as i:
                    for u in range(2):
                        t = 2 * i + u
                        free(sp, s_turned, t)
                        sp.dma_start(rows[u], slots(k.expert_in, t)).then_inc(s_rows[u], 16)

            @block.gpsimd
            def _(pool):
                start_at_two(pool, s_done)
                with pool.Fori(0, SLOT_TILES // 2) as i:
                    for u in range(2):
                        ready(pool, s_y, 2 * i + u)
                        carry(pool, k)
                        nc.gpsimd.dma_start(slots(k.expert_out, 2 * i + u), y[u]).then_inc(k.s_stored[u], 16)
                        pool.wait_ge(k.s_stored[u], 16 * i + 16)
                        pool.sem_inc(s_done, 1)

            @block.scalar
            def _(act):
                start_at_two(act, s_rows_t, s_hid)

                def copy_turned(t, u):
                    ready(act, s_turned, t)
                    free(act, s_up, t)
                    nc.scalar.activation(rows_t[u].rearrange("p a n -> p (a n)"), turned[u][:, 0:C], ACT.Copy).then_inc(s_rows_t, 1)

                def gelu(t, u):
                    ready(act, s_pre, t)
                    free(act, s_ht, t)
                    nc.scalar.activation(hid[u], pre[u], ACT.Gelu).then_inc(s_hid, 1)

                interleaved(act, SLOT_TILES, copy_turned, gelu, nothing, nothing)

            @block.vector
            def _(dve):
                start_at_two(dve, s_pre, s_hid_t, s_y)
                dve.wait_ge(s_w, 48 * EXPERTS)
                dve.wait_ge(s_b2, 16)
                which = [dve.alloc_register(f"ex_dve_expert{u}") for u in range(2)]

                def add_bias(t, u):
                    dve.reg_mov(which[u], expert(dve, t))
                    e = dve.snap(which[u], min_val=0, max_val=EXPERTS - 1)
                    ready(dve, s_up, t)
                    free(dve, s_hid, t)
                    nc.vector.tensor_tensor(pre[u], up[u][:, :], b1[:, bass.ds(e, 1), :].rearrange("p a n -> p (a n)"), ALU.add).then_inc(s_pre, 1)

                def copy_hidden(t, u):
                    ready(dve, s_ht, t)
                    free(dve, s_down, t)
                    nc.vector.tensor_copy(hid_t[u].rearrange("p f n -> p (f n)"), hid_turned[u][:, :]).then_inc(s_hid_t, 1)

                def finish(t, u):
                    e = dve.snap(which[u], min_val=0, max_val=EXPERTS - 1)
                    ready(dve, s_down, t)
                    free(dve, s_done, t)
                    nc.vector.tensor_tensor(y[u], down[u][:, 0:C], b2[:, bass.ds(e, 1), :].rearrange("p a n -> p (a n)"), ALU.add).then_inc(s_y, 1)

                interleaved(dve, SLOT_TILES, nothing, add_bias, copy_hidden, finish)

            @block.tensor
            def _(pe):
                start_at_two(pe, s_turned, s_up, s_ht, s_down)
                pe.wait_ge(s_w, 48 * EXPERTS)
                which = [pe.alloc_register(f"ex_pe_expert{u}") for u in range(2)]

                def turn_rows(t, u):
                    pe.reg_mov(which[u], expert(pe, t))
                    pe.wait_ge(s_rows[u], 8 * (t - u) + 16)
                    free(pe, s_rows_t, t)
                    for a in range(KC):
                        last = nc.tensor.transpose(turned[u][:, a * P:(a + 1) * P], rows[u][:, a * P:(a + 1) * P], k.ident[:, :])
                    last.then_inc(s_turned, 1)

                def multiply_up(t, u):
                    e = pe.snap(which[u], min_val=0, max_val=EXPERTS - 1)
                    ready(pe, s_rows_t, t)
                    free(pe, s_pre, t)
                    for a in range(KC):
                        last = nc.tensor.matmul(up[u][:, :], rows_t[u][:, a, :], w1[:, bass.ds(e, 1), a, :].rearrange("p a n -> p (a n)"),
                                                start=(a == 0), stop=(a == KC - 1))
                    last.then_inc(s_up, 1)

                def turn_hidden(t, u):
                    ready(pe, s_hid, t)
                    free(pe, s_hid_t, t)
                    for f in range(FT):
                        last = nc.tensor.transpose(hid_turned[u][:, f * P:(f + 1) * P], hid[u][:, f * P:(f + 1) * P], k.ident[:, :])
                    last.then_inc(s_ht, 1)

                def multiply_down(t, u):
                    e = pe.snap(which[u], min_val=0, max_val=EXPERTS - 1)
                    ready(pe, s_hid_t, t)
                    free(pe, s_y, t)
                    for f in range(FT):
                        last = nc.tensor.matmul(down[u][:, 0:C], hid_t[u][:, f, :], w2[:, bass.ds(e, 1), f, :].rearrange("p a n -> p (a n)"),
                                                start=(f == 0), stop=(f == FT - 1))
                    last.then_inc(s_down, 1)

                interleaved(pe, SLOT_TILES, turn_rows, multiply_up, turn_hidden, multiply_down)


def return_stage(nc, k):
    ROUND = 7
    ROUNDS = TILES // ROUND
    with stage(nc) as (sb, pb, sem):
        n = ROUND * C
        slot = [sb(f"rt_slot{u}", [P, ROUND, 2], I32) for u in range(2)]
        gate = [sb(f"rt_gate{u}", [P, ROUND, 2]) for u in range(2)]
        y = [k.wide[:, 2 * u * n:2 * (u + 1) * n].rearrange("p (t r c) -> p t r c", t=ROUND, r=2) for u in range(2)]
        one = [k.wide[:, (4 + u) * n:(5 + u) * n].rearrange("p (t c) -> p t c", t=ROUND) for u in range(2)]
        both = [k.wide[:, (6 + u) * n:(7 + u) * n].rearrange("p (t c) -> p t c", t=ROUND) for u in range(2)]
        s_out = [sem(f"rt_stored{u}") for u in range(2)]
        s_slot, s_gate, s_one, s_both = (sem(f"rt_{n}") for n in ("slots_copied", "gates_copied", "one_added", "both_added"))

        def rounds(engine, body):
            with engine.Fori(0, ROUNDS // 2) as i:
                body(2 * i, 0, i)
                body(2 * i + 1, 1, i)
            body(ROUNDS - 1, 0, ROUNDS // 2)

        def of_round(buf, r):
            return buf[:, r * ROUND:(r + 1) * ROUND] if isinstance(r, int) else buf[:, bass.ds(r * ROUND, ROUND)]

        with nc.Block() as block:
            @block.gpsimd
            def _(pool):
                def gather(r, u, i):
                    pool.wait_ge(s_both, ROUND * r + ROUND)
                    carry(pool, k)
                    nc.gpsimd.tensor_copy(slot[u][:, :, :], of_round(k.slot, r)).then_inc(s_slot, 1)
                    pool.wait_ge(s_slot, r + 1)
                    carry(pool, k)
                    for t in range(ROUND):
                        for e in range(2):
                            nc.gpsimd.indirect_dma_start(out=y[u][:, t, e, :], out_offset=None, in_=k.expert_out,
                                                         in_offset=bass.IndirectOffsetOnAxis(ap=slot[u][:, t, e:e + 1], axis=0)).then_inc(k.s_returned[u], 16)

                rounds(pool, gather)

            @block.scalar
            def _(act):
                act.sem_inc(s_both, 2 * ROUND)

                def copy_gates(r, u, i):
                    act.wait_ge(s_both, ROUND * r + ROUND)
                    nc.scalar.activation(gate[u][:, :, :], of_round(k.gate, r), ACT.Copy).then_inc(s_gate, 1)

                rounds(act, copy_gates)

            @block.vector
            def _(dve):
                def add(r, u, i):
                    dve.wait_ge(s_gate, r + 1)
                    carry(dve, k)
                    dve.wait_ge(k.s_returned[u], 32 * ROUND * i + 32 * ROUND)
                    carry(dve, k)
                    dve.wait_ge(s_out[u], 16 * i + 16)
                    carry(dve, k)
                    for t in range(ROUND):
                        x = of_round(k.x, r)[:, t, :]
                        last = nc.vector.scalar_tensor_tensor(one[u][:, t, :], y[u][:, t, 0, :], gate[u][:, t, 0:1], x, ALU.mult, ALU.add)
                    last.then_inc(s_one, 1)
                    dve.wait_ge(s_one, r + 1)
                    carry(dve, k)
                    for t in range(ROUND):
                        nc.vector.scalar_tensor_tensor(both[u][:, t, :], y[u][:, t, 1, :], gate[u][:, t, 1:2], one[u][:, t, :],
                                                       ALU.mult, ALU.add).then_inc(s_both, 1)

                rounds(dve, add)

            @block.sync
            def _(sp):
                for u in range(2):
                    sp.sem_inc(s_out[u], 16)

                def store(r, u, i):
                    sp.wait_ge(s_both, ROUND * r + 3 * ROUND)
                    if isinstance(r, int):
                        first, whole = r * ROUND * P, (TILES - 1) * P
                        sp.dma_start(k.out[first:whole, :].rearrange("(t p) c -> p t c", p=P), both[u][:, 0:ROUND - 1, :]).then_inc(s_out[u], 16)
                        sp.dma_start(k.out[whole:NODES, :], both[u][0:LAST, ROUND - 1, :]).then_inc(s_out[u], 16)
                    else:
                        sp.dma_start(k.out[bass.ds(r * ROUND * P, ROUND * P), :].rearrange("(t p) c -> p t c", p=P), both[u][:, :, :]).then_inc(s_out[u], 16)

                rounds(sp, store)
                sp.wait_ge(s_out[0], 16 + 16 * (ROUNDS // 2 + 2))
                sp.wait_ge(s_out[1], 16 + 16 * (ROUNDS // 2))


_INS = ["x_in", "edges", "dst_cols", "blocks32", "blocks64",
        "L0_gnn_W", "L0_mix_WqT", "L0_mix_WkvT", "L0_mix_WprojT", "L0_mix_bproj",
        "L0_ffn_W_fx", "L0_ffn_b_fx", "L0_ffn_W_xT", "L0_ffn_b_x4", "pair_slice", "b_slice8", "pair_qkv", "L0_ffn_W_out", "L0_ffn_b_out",
        "temperature",
        "L1_gnn_c1_w1", "L1_gnn_c1_b1", "L1_gnn_c1_w2", "L1_gnn_c2_w1", "L1_gnn_c2_b1", "L1_gnn_c2_w2", "bn_rows",
        "L1_mix_wq", "L1_mix_wkvT", "L1_mix_woT", "L1_mix_bo", "key_g2", "key_b2", "val_gb2",
        "L1_ffn_gamma", "L1_ffn_beta", "L1_ffn_Wr", "L1_ffn_br", "L1_ffn_W1", "L1_ffn_b1", "L1_ffn_W2", "L1_ffn_b2"]


def gps_two_layers(nc, ins, out):
    k = Core()
    k.ins = ins
    k.out = out
    k.table = nc.dram_tensor("table", [PADDED, C], F32).ap()
    k.expert_in = nc.dram_tensor("expert_in", [SLOT_TILES * P, C], F32).ap()
    k.expert_out = nc.dram_tensor("expert_out", [SLOT_TILES * P, C], F32).ap()
    k.win_dram = nc.dram_tensor("window_bounds", [GROUPS // 2, 4], I32).ap()
    bn = [k.ins["bn_rows"][i] for i in range(10)]
    with ExitStack() as ctx:
        residents(nc, k, ctx)
        setup_stage(nc, k)
        wide_residents(nc, k, ctx)
        with ExitStack() as graph:
            graph_residents(nc, k, graph)
            first_stats_stage(nc, k)
            keys_stage(nc, k)
            layer0_sums_and_attention(nc, k)
            first_update_stage(nc, k)
            with ExitStack() as ffn:
                k.w_slice = ffn.enter_context(nc.sbuf_tensor("w_slice", [P, KC, 2 * C], F32))
                k.b_slice = ffn.enter_context(nc.sbuf_tensor("b_slice", [P, 2 * C], F32))
                slice_weights_stage(nc, k)
                slices_and_attention(nc, k)
            second_update_stage(nc, k)
            table1_stage(nc, k)
            layer1_sums_and_attention(nc, k)
            convolve_stage(nc, k, "c1", k.ins["L1_gnn_c1_w2"], bn[0], bn[1], bn[2], bn[3], bn[4], k.bn_scale, k.bn_shift)
            table2_stage(nc, k, k.bn_scale, k.bn_shift)
            layer1_second_sums(nc, k)
            convolve_stage(nc, k, "c2", k.ins["L1_gnn_c2_w2"], bn[5], bn[6], bn[7], bn[8], bn[9], k.bn_scale, k.bn_shift)
            third_update_stage(nc, k, k.bn_scale, k.bn_shift)
            router_stage(nc, k)
        experts_stage(nc, k)


def kernel(**inputs):
    import numpy as np
    import concourse.bacc as bacc
    from concourse.bass_utils import run_bass_kernel_spmd as run

    i = {n: np.asarray(a) for n, a in inputs.items()}

    def by_column(a, fill):
        flat = np.full(GROUPS * SUB * P, fill, a.dtype)
        flat[:EDGES] = a
        return flat.reshape(GROUPS * SUB, P)

    def twice(w):
        m = np.zeros((P, P), w.dtype)
        m[:64, :64] = w
        m[64:, 64:] = w
        return m

    def blocks(n):
        return np.kron(np.eye(P // n, dtype=np.float32), np.ones((n, n), np.float32))

    src, dst, weight = (by_column(a, f) for a, f in ((i["src"], 0), (i["dst"], PADDED - 1), (i["edge_weight"], 0)))
    edges = np.stack([a.view(np.int32).reshape(2 * TRIPS, 16, P) for a in (src, dst, weight)], 1)
    x = np.zeros((PADDED, C), i["x"].dtype)
    x[:NODES] = i["x"]
    channels = lambda a: a.reshape(KC, P).T
    arrays = {
        "x_in": x, "edges": edges.transpose(0, 3, 1, 2), "dst_cols": dst.T, "blocks32": blocks(32), "blocks64": blocks(64),
        "L0_mix_WqT": i["L0_mix_Wq"].T, "L0_mix_WkvT": i["L0_mix_Wkv"].T, "L0_mix_WprojT": i["L0_mix_Wproj"].T,
        "L0_ffn_W_xT": i["L0_ffn_W_x"].T, "L0_ffn_b_x4": i["L0_ffn_b_x"].reshape(4, P).T, "pair_slice": twice(i["L0_ffn_W_slice"]),
        "b_slice8": np.tile(i["L0_ffn_b_slice"], SH), "pair_qkv": np.stack([twice(i["L0_ffn_W_" + n]) for n in "qkv"]),
        "temperature": i["L0_ffn_temperature"].reshape(-1),
        "bn_rows": np.stack([channels(i["L1_gnn_" + n]) for n in ("c1_b2", "c1_g", "c1_b", "bn1_g", "bn1_b", "c2_b2", "c2_g", "c2_b", "bn2_g", "bn2_b")]),
        "L1_mix_wkvT": np.concatenate([i["L1_mix_wk"].T, i["L1_mix_wv"].T], 1), "L1_mix_woT": i["L1_mix_wo"].T,
        "key_g2": np.tile(i["L1_mix_ln_k_g"], 2), "key_b2": np.tile(i["L1_mix_ln_k_b"], 2),
        "val_gb2": np.stack([np.tile(i["L1_mix_ln_v_g"], 2), np.tile(i["L1_mix_ln_v_b"], 2)], 1),
    }
    arrays = {n: np.ascontiguousarray(arrays.get(n, i.get(n))) for n in _INS}
    nc = bacc.Bacc("TRN2", target_bir_lowering=False, num_devices=1)
    ins = {n: nc.dram_tensor(f"in_{n}", a.shape, mybir.dt.from_np(a.dtype), kind="ExternalInput").ap() for n, a in arrays.items()}
    out = nc.dram_tensor("out", (NODES, C), F32, kind="ExternalOutput").ap()
    gps_two_layers(nc, ins, out)
    got = run(nc, [{f"in_{n}": a for n, a in arrays.items()}], core_ids=[0])
    return got.results[0]["out"]
```
